# Optimizing a Trainium2 kernel written in Bass

```python
import numpy as np
import jax
import jax.numpy as jnp

def _softmax(x, axis=-1):
    return jax.nn.softmax(x, axis=axis)

def _gelu(x):
    return jax.nn.gelu(x, approximate=True)

def _silu(x):
    return jax.nn.silu(x)

def _sigmoid(x):
    return jax.nn.sigmoid(x)

def _layernorm(x, axis=-1, eps=1e-05):
    m = jnp.mean(x, axis=axis, keepdims=True)
    v = jnp.var(x, axis=axis, keepdims=True)
    return (x - m) / jnp.sqrt(v + eps)

def _scatter_add(tgt, idx, src, axis=0):
    return tgt.at[idx].add(src)

def _segment_sum(src, seg, n):
    return jax.ops.segment_sum(src, seg, n)
kernel_name = 'mk_gnn_resnorm_d2_gnn_r8_f4b518'

def setup_inputs(seed: int=0):
    np.random.seed(seed)
    _w = jnp.asarray

    def _rec_inputs():
        import jax
        import jax.numpy as jnp
        _gk = jax.random.key(seed)
        x = -1.686e-05 + 1 * jax.random.normal(jax.random.fold_in(_gk, 1), (6250, 160), jnp.float32)
        src = jax.random.randint(jax.random.fold_in(_gk, 2), (100000,), 0, 6250, jnp.int32)
        dst = jax.random.randint(jax.random.fold_in(_gk, 3), (100000,), 0, 6250, jnp.int32)
        _o = jnp.argsort(dst, stable=True)
        src = src[_o]
        dst = dst[_o]
        edge_attr_10 = jax.random.uniform(jax.random.fold_in(_gk, 12), (100000, 10), jnp.float32, 0.0, 1)
        edge_attr_32 = 0.000196303 + 1.00016 * jax.random.normal(jax.random.fold_in(_gk, 13), (100000, 32), jnp.float32)
        edge_attr_4 = -0.000107899 + 1.00008 * jax.random.normal(jax.random.fold_in(_gk, 14), (100000, 4), jnp.float32)
        node_vec1 = -0.00915711 + 0.999674 * jax.random.normal(jax.random.fold_in(_gk, 16), (6250, 1), jnp.float32)
        return (x, src, dst, edge_attr_10, edge_attr_32, edge_attr_4, node_vec1)
    x, src, dst, edge_attr_10, edge_attr_32, edge_attr_4, node_vec1 = _rec_inputs()

    def _L0_gnn_setup():
        import jax, jax.numpy as jnp
        import numpy as np
        MUL0_N, MUL1_N = (64, 32)
        MUL0_E, MUL1_E = (8, 8)
        MUL0_H, MUL1_H = (64, 32)
        N_NODES, N_EDGES = (6250, 100000)
        D_NODE = MUL0_N + 3 * MUL1_N
        D_EDGE = MUL0_E + 3 * MUL1_E
        D_HID = MUL0_H + 3 * MUL1_H

        def _split(x, mul0, mul1):
            s = x[..., :mul0]
            v = x[..., mul0:].reshape(x.shape[0], mul1, 3)
            return (s, v)

        def fctp_messages(x, e, W1, W2, W3, W4):
            xs, xv = _split(x, MUL0_N, MUL1_N)
            es, ev = _split(e, MUL0_E, MUL1_E)
            inv_sqrt2 = 1.0 / np.sqrt(2.0)
            s1 = jnp.einsum('ea,eb,abc->ec', xs, es, W1) * (1.0 / np.sqrt(MUL0_N * MUL0_E))
            s2 = jnp.einsum('eai,ebi,abc->ec', xv, ev, W2) * (1.0 / (np.sqrt(3.0) * np.sqrt(MUL1_N * MUL1_E)))
            out_s = (s1 + s2) * inv_sqrt2
            v1 = jnp.einsum('ea,ebi,abc->eci', xs, ev, W3) * (1.0 / np.sqrt(MUL0_N * MUL1_E))
            v2 = jnp.einsum('eai,eb,abc->eci', xv, es, W4) * (1.0 / np.sqrt(MUL1_N * MUL0_E))
            out_v = (v1 + v2) * inv_sqrt2
            return jnp.concatenate([out_s, out_v.reshape(out_v.shape[0], -1)], axis=-1)
        key = jax.random.key(seed)
        ks = jax.random.split(key, 12)
        node_features = jax.random.normal(ks[0], (N_NODES, D_NODE), dtype=jnp.float32)
        edge_index = jax.random.randint(ks[1], (2, N_EDGES), 0, N_NODES, dtype=jnp.int64)
        edge_attr_tensor = jax.random.normal(ks[2], (N_EDGES, D_EDGE), dtype=jnp.float32)
        node_attr_scalar_raw = jax.random.normal(ks[3], (N_NODES, 1), dtype=jnp.float32)
        W1 = jax.random.normal(ks[4], (MUL0_N, MUL0_E, MUL0_H), dtype=jnp.float32)
        W2 = jax.random.normal(ks[5], (MUL1_N, MUL1_E, MUL0_H), dtype=jnp.float32)
        W3 = jax.random.normal(ks[6], (MUL0_N, MUL1_E, MUL1_H), dtype=jnp.float32)
        W4 = jax.random.normal(ks[7], (MUL1_N, MUL0_E, MUL1_H), dtype=jnp.float32)
        Wm = jax.random.normal(ks[8], (D_HID, D_HID), dtype=jnp.float32) / np.sqrt(D_HID)
        bm = jnp.zeros((D_HID,), dtype=jnp.float32)
        Wu = jax.random.normal(ks[9], (D_NODE + D_HID, D_NODE), dtype=jnp.float32) / np.sqrt(D_NODE + D_HID)
        bu = jnp.zeros((D_NODE,), dtype=jnp.float32)
        return {'node_features': node_features, 'edge_index': edge_index, 'edge_attr_tensor': edge_attr_tensor, 'node_attr_scalar_raw': node_attr_scalar_raw, 'W1': W1, 'W2': W2, 'W3': W3, 'W4': W4, 'Wm': Wm, 'bm': bm, 'Wu': Wu, 'bu': bu}
    _L0_gnn_all = _L0_gnn_setup()
    _L0_gnn_in = {k: v for k, v in _L0_gnn_all.items() if k in ('W1', 'W2', 'W3', 'W4', 'Wm', 'bm', 'Wu', 'bu')}
    del _L0_gnn_all

    def _L1_gnn_setup():
        import jax, jax.numpy as jnp
        import numpy as np
        N_NODES = 6250
        N_EDGES = 100000
        MUL0, MUL1 = (64, 32)
        N_BASIS, N_RADIAL = (10, 100)
        W_NUMEL = 192
        NUM_NEIGHBORS = 16.0
        INV_SQRT3 = np.float32(1.0 / np.sqrt(3.0))
        RELU_GAIN = np.float32(np.sqrt(2.0))
        FAN_L2 = np.float32(np.sqrt(MUL0 + MUL1))

        def _fctp_scalar_attr(x0, x1, a, W0, W1):
            o0 = x0 @ W0 * a * (1.0 / np.sqrt(W0.shape[0]))
            o1 = jnp.einsum('nud,uw->nwd', x1, W1) * a[..., None] * (1.0 / np.sqrt(W1.shape[0]))
            return (o0, o1)
        key = jax.random.key(seed)
        ks = jax.random.split(key, 16)
        return {'node_input': jax.random.normal(ks[0], (N_NODES, MUL0 + 3 * MUL1), jnp.float32), 'node_attr': jnp.ones((N_NODES, 1), jnp.float32), 'edge_attr': jax.random.normal(ks[1], (N_EDGES, 4), jnp.float32), 'edge_length_embedded': jax.random.uniform(ks[2], (N_EDGES, N_BASIS), dtype=jnp.float32), 'W_si0': jax.random.normal(ks[3], (MUL0, MUL0), jnp.float32), 'W_si1': jax.random.normal(ks[4], (MUL1, MUL1), jnp.float32), 'W_l1_0': jax.random.normal(ks[5], (MUL0, MUL0), jnp.float32), 'W_l1_1': jax.random.normal(ks[6], (MUL1, MUL1), jnp.float32), 'W_l2_00': jax.random.normal(ks[7], (MUL0, MUL0), jnp.float32), 'W_l2_10': jax.random.normal(ks[8], (MUL1, MUL0), jnp.float32), 'W_l2_01': jax.random.normal(ks[9], (MUL0, MUL1), jnp.float32), 'W_l2_11': jax.random.normal(ks[10], (MUL1, MUL1), jnp.float32), 'W_fc1': jax.random.normal(ks[11], (N_BASIS, N_RADIAL), jnp.float32), 'W_fc2': jax.random.normal(ks[12], (N_RADIAL, W_NUMEL), jnp.float32), 'edge_src': jax.random.randint(ks[13], (N_EDGES,), 0, N_NODES), 'edge_dst': jax.random.randint(ks[14], (N_EDGES,), 0, N_NODES)}
    _L1_gnn_all = _L1_gnn_setup()
    _L1_gnn_in = {k: v for k, v in _L1_gnn_all.items() if k in ('W_si0', 'W_si1', 'W_l1_0', 'W_l1_1', 'W_l2_00', 'W_l2_10', 'W_l2_01', 'W_l2_11', 'W_fc1', 'W_fc2')}
    del _L1_gnn_all
    return {'x': x, 'src': src, 'dst': dst, 'edge_attr_10': edge_attr_10, 'edge_attr_32': edge_attr_32, 'edge_attr_4': edge_attr_4, 'node_vec1': node_vec1, 'L0_gnn_W1': _L0_gnn_in['W1'], 'L0_gnn_W2': _L0_gnn_in['W2'], 'L0_gnn_W3': _L0_gnn_in['W3'], 'L0_gnn_W4': _L0_gnn_in['W4'], 'L0_gnn_Wm': _L0_gnn_in['Wm'], 'L0_gnn_bm': _L0_gnn_in['bm'], 'L0_gnn_Wu': _L0_gnn_in['Wu'], 'L0_gnn_bu': _L0_gnn_in['bu'], 'L1_gnn_W_si0': _L1_gnn_in['W_si0'], 'L1_gnn_W_si1': _L1_gnn_in['W_si1'], 'L1_gnn_W_l1_0': _L1_gnn_in['W_l1_0'], 'L1_gnn_W_l1_1': _L1_gnn_in['W_l1_1'], 'L1_gnn_W_l2_00': _L1_gnn_in['W_l2_00'], 'L1_gnn_W_l2_10': _L1_gnn_in['W_l2_10'], 'L1_gnn_W_l2_01': _L1_gnn_in['W_l2_01'], 'L1_gnn_W_l2_11': _L1_gnn_in['W_l2_11'], 'L1_gnn_W_fc1': _L1_gnn_in['W_fc1'], 'L1_gnn_W_fc2': _L1_gnn_in['W_fc2']}

def reference(x, src, dst, edge_attr_10, edge_attr_32, edge_attr_4, node_vec1, L0_gnn_W1, L0_gnn_W2, L0_gnn_W3, L0_gnn_W4, L0_gnn_Wm, L0_gnn_bm, L0_gnn_Wu, L0_gnn_bu, L1_gnn_W_si0, L1_gnn_W_si1, L1_gnn_W_l1_0, L1_gnn_W_l1_1, L1_gnn_W_l2_00, L1_gnn_W_l2_10, L1_gnn_W_l2_01, L1_gnn_W_l2_11, L1_gnn_W_fc1, L1_gnn_W_fc2):
    import jax
    import jax.numpy as jnp

    def _L0_gnn_ref(node_features, edge_index, edge_attr_tensor, node_attr_scalar_raw, W1, W2, W3, W4, Wm, bm, Wu, bu):
        import jax, jax.numpy as jnp
        import numpy as np
        MUL0_N, MUL1_N = (64, 32)
        MUL0_E, MUL1_E = (8, 8)
        MUL0_H, MUL1_H = (64, 32)
        N_NODES, N_EDGES = (6250, 100000)
        D_NODE = MUL0_N + 3 * MUL1_N
        D_EDGE = MUL0_E + 3 * MUL1_E
        D_HID = MUL0_H + 3 * MUL1_H

        def _split(x, mul0, mul1):
            s = x[..., :mul0]
            v = x[..., mul0:].reshape(x.shape[0], mul1, 3)
            return (s, v)

        def fctp_messages(x, e, W1, W2, W3, W4):
            xs, xv = _split(x, MUL0_N, MUL1_N)
            es, ev = _split(e, MUL0_E, MUL1_E)
            inv_sqrt2 = 1.0 / np.sqrt(2.0)
            s1 = jnp.einsum('ea,eb,abc->ec', xs, es, W1) * (1.0 / np.sqrt(MUL0_N * MUL0_E))
            s2 = jnp.einsum('eai,ebi,abc->ec', xv, ev, W2) * (1.0 / (np.sqrt(3.0) * np.sqrt(MUL1_N * MUL1_E)))
            out_s = (s1 + s2) * inv_sqrt2
            v1 = jnp.einsum('ea,ebi,abc->eci', xs, ev, W3) * (1.0 / np.sqrt(MUL0_N * MUL1_E))
            v2 = jnp.einsum('eai,eb,abc->eci', xv, es, W4) * (1.0 / np.sqrt(MUL1_N * MUL0_E))
            out_v = (v1 + v2) * inv_sqrt2
            return jnp.concatenate([out_s, out_v.reshape(out_v.shape[0], -1)], axis=-1)
        row, col = (edge_index[0], edge_index[1])
        tp = fctp_messages(node_features[col], edge_attr_tensor, W1, W2, W3, W4)
        messages = tp @ Wm + bm
        agg = jax.ops.segment_sum(messages, row, num_segments=N_NODES)
        upd = jnp.concatenate([node_features, agg], axis=-1) @ Wu + bu
        return node_features + upd

    def _L1_gnn_ref(node_input, node_attr, edge_src, edge_dst, edge_attr, edge_length_embedded, W_si0, W_si1, W_l1_0, W_l1_1, W_l2_00, W_l2_10, W_l2_01, W_l2_11, W_fc1, W_fc2):
        import jax, jax.numpy as jnp
        import numpy as np
        N_NODES = 6250
        N_EDGES = 100000
        MUL0, MUL1 = (64, 32)
        N_BASIS, N_RADIAL = (10, 100)
        W_NUMEL = 192
        NUM_NEIGHBORS = 16.0
        INV_SQRT3 = np.float32(1.0 / np.sqrt(3.0))
        RELU_GAIN = np.float32(np.sqrt(2.0))
        FAN_L2 = np.float32(np.sqrt(MUL0 + MUL1))

        def _fctp_scalar_attr(x0, x1, a, W0, W1):
            o0 = x0 @ W0 * a * (1.0 / np.sqrt(W0.shape[0]))
            o1 = jnp.einsum('nud,uw->nwd', x1, W1) * a[..., None] * (1.0 / np.sqrt(W1.shape[0]))
            return (o0, o1)
        N = node_input.shape[0]
        x0 = node_input[:, :MUL0]
        x1 = node_input[:, MUL0:].reshape(N, MUL1, 3)
        a = node_attr
        h = jax.nn.relu(edge_length_embedded @ W_fc1 * (1.0 / np.sqrt(N_BASIS))) * RELU_GAIN
        w = h @ W_fc2 * (1.0 / np.sqrt(N_RADIAL))
        w0, w1, w2, w3 = (w[:, :64], w[:, 64:128], w[:, 128:160], w[:, 160:192])
        si0, si1 = _fctp_scalar_attr(x0, x1, a, W_si0, W_si1)
        l0, l1 = _fctp_scalar_attr(x0, x1, a, W_l1_0, W_l1_1)
        y0 = l0[edge_src]
        y1 = l1[edge_src]
        e0 = edge_attr[:, :1]
        e1 = edge_attr[:, 1:4]
        m0 = w0 * y0 * e0
        m1 = (w1 * y0)[:, :, None] * e1[:, None, :]
        m2 = (w2 * e0)[:, :, None] * y1
        m3 = w3 * jnp.einsum('eud,ed->eu', y1, e1) * INV_SQRT3
        inv = np.float32(1.0 / np.sqrt(NUM_NEIGHBORS))
        s0 = jax.ops.segment_sum(m0, edge_dst, num_segments=N) * inv
        s1 = jax.ops.segment_sum(m1, edge_dst, num_segments=N) * inv
        s2 = jax.ops.segment_sum(m2, edge_dst, num_segments=N) * inv
        s3 = jax.ops.segment_sum(m3, edge_dst, num_segments=N) * inv
        o0 = (s0 @ W_l2_00 + s3 @ W_l2_10) * a / FAN_L2
        o1 = (jnp.einsum('nud,uw->nwd', s1, W_l2_01) + jnp.einsum('nud,uw->nwd', s2, W_l2_11)) * a[..., None] / FAN_L2
        out0 = si0 + 0.5 * o0
        out1 = si1 + 0.5 * o1
        return jnp.concatenate([out0, out1.reshape(N, 3 * MUL1)], axis=1)
    edge_index = jnp.stack([src, dst])
    x = _layernorm(x + _L0_gnn_ref(x, edge_index, edge_attr_32, node_vec1, L0_gnn_W1, L0_gnn_W2, L0_gnn_W3, L0_gnn_W4, L0_gnn_Wm, L0_gnn_bm, L0_gnn_Wu, L0_gnn_bu), axis=-1)
    x = _layernorm(x + _L1_gnn_ref(x, node_vec1, src, dst, edge_attr_4, edge_attr_10, L1_gnn_W_si0, L1_gnn_W_si1, L1_gnn_W_l1_0, L1_gnn_W_l1_1, L1_gnn_W_l2_00, L1_gnn_W_l2_10, L1_gnn_W_l2_01, L1_gnn_W_l2_11, L1_gnn_W_fc1, L1_gnn_W_fc2), axis=-1)
    return x

_drawn_inputs = setup_inputs


def setup_inputs(seed=0):
    import zlib

    import numpy as np

    out = dict(_drawn_inputs(seed))
    spreads = {'L0_gnn_bm': (0.0, 0.1), 'L0_gnn_bu': (0.0, 0.28)}
    factors = {}
    for name, (base, spread) in spreads.items():
        noise = np.random.default_rng([zlib.crc32(name.encode()), seed]).standard_normal(out[name].shape)
        drawn = base * np.exp(spread * noise) if base else spread * noise
        out[name] = jnp.asarray(drawn.astype(out[name].dtype))
    for name, factor in factors.items():
        out[name] = (out[name] * factor).astype(out[name].dtype)
    return out
```

```python
import math
from contextlib import ExitStack

import concourse.bass as bass
from concourse import mybir

F32 = mybir.dt.float32
I32 = mybir.dt.int32
ALU = mybir.AluOpType
ACT = mybir.ActivationFunctionType
AX = mybir.AxisListType

P = 128
NODES, EDGES = 6250, 100000
BLOCKS = 50
NODE_ROWS = BLOCKS * P
TILES = 784
PAD_NODE = NODES
TABLE_ROWS = NODE_ROWS + P
DUMP = NODE_ROWS
S, V, D = 64, 32, 160
NB = 32
GW = NB * D
MW = D + 1
UW = 384
COPIES = 4
EPS = 1e-5

K1 = 1.0 / math.sqrt(S * 8) / math.sqrt(2.0)
K2 = 1.0 / (math.sqrt(3.0) * math.sqrt(V * 8)) / math.sqrt(2.0)
K3 = 1.0 / math.sqrt(S * 8) / math.sqrt(2.0)
K4 = 1.0 / math.sqrt(V * 8) / math.sqrt(2.0)


class Chain:

    def __init__(self, eng, sem, base=0):
        self.eng, self.sem, self.base, self.n = eng, sem, base, 0

    def step(self, ins):
        self.n += 1
        return ins.then_inc(self.sem, 1)

    def settle(self):
        self.eng.wait_ge(self.sem, self.base + self.n)

    def link(self, ins):
        self.step(ins)
        self.settle()


class Shared:
    pass


def build_program(nc, t, out):
    ctx = ExitStack()
    with ctx:
        def sb(name, shape, dt=F32, where=ctx):
            return where.enter_context(nc.sbuf_tensor(name, shape, dt))

        def ps(name, shape, where=ctx):
            return where.enter_context(nc.psum_tensor(name, shape, F32))

        def sem(name, where=ctx):
            return where.enter_context(nc.semaphore(name))

        def dram(name, shape):
            return nc.dram_tensor(name, shape, F32).ap()

        v = Shared()
        v.sb, v.ps, v.sem = sb, ps, sem
        v.products = dram("products", (NODE_ROWS, GW))
        v.sums0 = [dram(f"sums0_{r}", (TABLE_ROWS, MW)) for r in range(COPIES)]
        v.sums1 = [dram(f"sums1_{r}", (TABLE_ROWS, UW)) for r in range(COPIES)]
        v.y_table = dram("y_table", (NODE_ROWS, D))
        v.base_table = dram("base_table", (NODE_ROWS, D))

        v.ident = sb("ident", [P, P])
        v.ones = sb("ones", [P, P])
        v.dump_before = sb("dump_before", [P, P])
        v.w1 = sb("w1", [S, 512])
        v.w2 = sb("w2", [96, 512])
        v.w3 = sb("w3", [S, 256])
        v.w4 = sb("w4", [96, 256])
        v.wm_t = sb("wm_t", [P, 2, MW])
        v.wu_bot = sb("wu_bot", [P, 2, D])
        v.wu_s = sb("wu_s", [S, D])
        v.wu_v = sb("wu_v", [96, D])
        v.bu = sb("bu", [1, D])
        v.wmu_a = sb("wmu_a", [P, D])
        v.wmu_b = sb("wmu_b", [33, D])
        v.w_node0 = sb("w_node0", [S, 128])
        v.w_node1 = sb("w_node1", [V, 64])
        v.w_out0 = sb("w_out0", [96, S])
        v.w_out1 = sb("w_out1", [96, V])
        v.fc1 = sb("fc1", [10, 100])
        v.fc2 = sb("fc2", [100, 192])
        v.src_col = sb("src_col", [P, TILES])
        v.dst_col = sb("dst_col", [P, TILES])
        v.src_int = sb("src_int", [P, TILES], I32)
        v.dst_int = sb("dst_int", [P, TILES], I32)
        v.a_col = sb("a_col", [P, BLOCKS])

        setup_phase(nc, t, v)
        products_phase(nc, t, v)
        layer0_edges_any_order(nc, t, v)
        layer0_nodes(nc, t, v)
        layer1_edges_any_order(nc, t, v)
        layer1_nodes(nc, t, v, out)


def setup_phase(nc, t, v):
    with ExitStack() as local:
        sb = lambda name, shape, dt=F32: v.sb(name, shape, dt, local)
        zeros = sb("zeros", [P, 51 * MW])
        psum = v.ps("setup_psum", [P, 2, 512], local)
        loaded = v.sem("setup_loaded", local)
        cleared = v.sem("setup_cleared", local)
        zeroed = v.sem("setup_zeroed", local)
        filled = v.sem("setup_filled", local)
        scaled = v.sem("setup_scaled", local)
        merged = v.sem("setup_merged", local)
        n_loads = [0]
        with nc.Block() as block:

            @block.sync
            def _(sp):
                def load(dst, src):
                    n_loads[0] += 1
                    sp.dma_start(dst, src).then_inc(loaded, 16)

                load(v.w1[:], t["w1"])
                load(v.w3[:], t["w3"])
                load(v.w_node0[:], t["w_node0"])
                load(v.w_node1[:], t["w_node1"])
                for i in range(3):
                    load(v.w2[32 * i:32 * i + 32, :], t["w2"])
                    load(v.w4[32 * i:32 * i + 32, :], t["w4"])
                load(v.wm_t[:, 0, :], t["wm_t"][0:P, :])
                load(v.wm_t[0:32, 1, :], t["wm_t"][P:D, :])
                load(v.wu_bot[:, 0, :], t["wu_bot"][0:P, :])
                load(v.wu_bot[0:32, 1, :], t["wu_bot"][P:D, :])
                load(v.wu_s[:], t["wu_top"][0:S, :])
                load(v.wu_v[:], t["wu_top"][S:D, :])
                load(v.bu[:], t["bu"])
                load(v.w_out0[:], t["w_out0"])
                load(v.w_out1[:], t["w_out1"])
                load(v.fc1[:], t["fc1"])
                load(v.fc2[:], t["fc2"])
                load(v.src_int[:], t["src_cols"])
                load(v.dst_int[:], t["dst_cols"])
                load(v.a_col[:], t["a_cols"])
                sp.wait_ge(zeroed, 1)
                for r in range(COPIES):
                    sp.dma_start(v.sums0[r].rearrange("(p a) d -> p (a d)", p=P), zeros[:]).then_inc(cleared, 16)
                    for h in range(3):
                        sp.dma_start(v.sums1[r].rearrange("(p a) d -> p (a d)", p=P)[:, h * 17 * UW:(h + 1) * 17 * UW],
                                     zeros[:, 0:17 * UW]).then_inc(cleared, 16)
                sp.wait_ge(cleared, 16 * COPIES * 4)

            @block.gpsimd
            def _(pool):
                pool.memset(v.ident[:], 0.0).then_inc(filled, 1)
                pool.memset(v.ones[:], 1.0).then_inc(filled, 1)
                pool.iota(v.dump_before[:], [[0, P]], base=DUMP, channel_multiplier=1,
                          allow_small_or_imprecise_dtypes=True).then_inc(filled, 1)
                pool.wait_ge(filled, 3)
                pool.affine_select(out=v.ident[:], in_=v.ident[:], compare_op=ALU.not_equal, fill=1.0,
                                   base=0, pattern=[[-1, P]], channel_multiplier=1).then_inc(filled, 1)
                pool.affine_select(out=v.dump_before[:], in_=v.dump_before[:], compare_op=ALU.is_gt, fill=0.0,
                                   base=0, pattern=[[-1, P]], channel_multiplier=1).then_inc(filled, 1)

            @block.vector
            def _(dve):
                dve.memset(zeros[:], 0.0).then_inc(zeroed, 1)
                dve.wait_ge(loaded, 16 * n_loads[0])
                dve.tensor_copy(v.src_col[:], v.src_int[:])
                dve.tensor_copy(v.dst_col[:], v.dst_int[:])
                for weight, k in ((v.w1, K1), (v.w2, K2), (v.w3, K3), (v.w4, K4),
                                (v.w_node0, 1.0 / math.sqrt(S)), (v.w_node1, 1.0 / math.sqrt(V)),
                                (v.w_out0, 0.125 / math.sqrt(96.0)), (v.w_out1, 0.125 / math.sqrt(96.0)),
                                (v.fc1, math.sqrt(2.0 / 10.0)), (v.fc2, 0.1)):
                    dve.tensor_scalar(weight[:], weight[:], k, None, ALU.mult).then_inc(scaled, 1)
                dve.wait_ge(scaled, 10)
                dve.tensor_scalar(v.fc2[:, 160:192], v.fc2[:, 160:192], 1.0 / math.sqrt(3.0), None, ALU.mult)
                dve.wait_ge(merged, 1)
                dve.tensor_copy(v.wmu_a[:], psum[:, 0, 0:D])
                dve.tensor_copy(v.wmu_b[:], psum[0:33, 1, 0:D])

            @block.tensor
            def _(pe):
                pe.wait_ge(loaded, 16 * n_loads[0])
                for m, (m0, m1) in enumerate(((0, P), (P, MW))):
                    pe.matmul(psum[0:m1 - m0, m, 0:D], v.wm_t[:, 0, m0:m1], v.wu_bot[:, 0, :], start=True, stop=False)
                    last = pe.matmul(psum[0:m1 - m0, m, 0:D], v.wm_t[0:32, 1, m0:m1], v.wu_bot[0:32, 1, :],
                                     start=False, stop=True)
                last.then_inc(merged, 1)


def products_phase(nc, t, v):
    with ExitStack() as local:
        xs = [v.sb(f"xs{k}", [S, P], F32, local) for k in range(2)]
        xv = [v.sb(f"xv{k}", [96, P], F32, local) for k in range(2)]
        g = [v.sb(f"g{k}", [P, NB, D], F32, local) for k in range(2)]
        bank = [v.ps(f"g_bank{k}", [P, 512], local) for k in range(8)]
        x_in = [v.sem(f"x_in{k}", local) for k in range(2)]
        banks_full = v.sem("banks_full", local)
        act_done = v.sem("act_done", local)
        dve_done = v.sem("dve_done", local)
        blank = v.sem("blank", local)
        g_free = v.sem("g_free", local)
        g_out = [v.sem(f"g_out{k}", local) for k in range(2)]
        with nc.Block() as block:

            @block.gpsimd
            def _(pool):
                for k in range(2):
                    pool.memset(g[k][:], 0.0).then_inc(blank, 1)

            @block.sync
            def _(sp):
                sp.wait_ge(blank, 2)
                sp.sem_inc(g_free, 2)
                with sp.Fori(0, BLOCKS // 2) as i:
                    for k in range(2):
                        b = i * 2 + k
                        sp.wait_ge(banks_full, b + 1)
                        sp.dma_start(xs[k][:], t["x_t"][0:S, bass.ds(b * P, P)]).then_inc(x_in[k], 16)
                        sp.dma_start(xv[k][:], t["x_t"][S:D, bass.ds(b * P, P)]).then_inc(x_in[k], 16)
                    for k in range(2):
                        b = i * 2 + k
                        sp.wait_ge(act_done, b + 2)
                        sp.wait_ge(dve_done, b + 2)
                        sp.dma_start(v.products[bass.ds(b * P, P), :], g[k][:].rearrange("p b d -> p (b d)")).then_inc(g_out[k], 16)
                        sp.wait_ge(g_out[k], i * 16 + 16)
                        sp.sem_inc(g_free, 1)

            @block.tensor
            def _(pe):
                pe.sem_inc(banks_full, 2)
                with pe.Fori(0, BLOCKS // 2) as i:
                    for k in range(2):
                        b = i * 2 + k
                        pe.wait_ge(x_in[k], i * 32 + 32)
                        pe.wait_ge(act_done, b + 1)
                        pe.wait_ge(dve_done, b + 1)
                        pe.matmul(bank[0][:], xs[k][:], v.w1[:], start=True, stop=True)
                        for c in range(3):
                            lo, hi = 32 * c, 32 * c + 32
                            pe.matmul(bank[1 + c][:], xv[k][lo:hi, :], v.w2[lo:hi, :], start=True, stop=True)
                            pe.matmul(bank[4 + c][:, 0:256], xv[k][lo:hi, :], v.w4[lo:hi, :], start=True, stop=True)
                        pe.matmul(bank[7][:, 0:256], xs[k][:], v.w3[:], start=True, stop=True).then_inc(banks_full, 1)

            @block.scalar
            def _(act):
                act.sem_inc(act_done, 1)
                with act.Fori(0, BLOCKS // 2) as i:
                    for k in range(2):
                        b = i * 2 + k
                        act.wait_ge(g_free, b + 1)
                        act.wait_ge(banks_full, b + 3)
                        for q in range(3):
                            last = act.copy(g[k][:, 8 * q:8 * q + 8, 0:S], bank[q][:].rearrange("p (b c) -> p b c", c=S))
                        last.then_inc(act_done, 1)

            @block.vector
            def _(dve):
                dve.sem_inc(dve_done, 1)
                with dve.Fori(0, BLOCKS // 2) as i:
                    for k in range(2):
                        b = i * 2 + k
                        dve.wait_ge(g_free, b + 1)
                        dve.wait_ge(banks_full, b + 3)
                        dve.tensor_copy(g[k][:, 24:32, 0:S], bank[3][:].rearrange("p (b c) -> p b c", c=S))
                        for c in range(3):
                            dve.tensor_copy(g[k][:, 0:8, S + 32 * c:S + 32 * c + 32],
                                            bank[4 + c][:, 0:256].rearrange("p (b c) -> p b c", c=V))
                        for c in range(3):
                            last = dve.tensor_copy(g[k][:, 8 + 8 * c:16 + 8 * c, S + 32 * c:S + 32 * c + 32],
                                                   bank[7][:, 0:256].rearrange("p (b c) -> p b c", c=V))
                        last.then_inc(dve_done, 1)


def layer0_edges_any_order(nc, t, v):
    with ExitStack() as local:
        U = COPIES
        rows = [v.sb(f"rows{k}", [P, NB, D], F32, local) for k in range(2)]
        e = v.sb("e", [P, U, NB], F32, local)
        targets = v.sb("targets", [P, U, P], I32, local)
        same = v.sb("same", [P, U, P], F32, local)
        scratch = v.sb("scratch", [P, U, P], F32, local)
        dup = v.sb("dup", [P, U], F32, local)
        msg = v.sb("msg", [P, U, MW], F32, local)
        total = v.sb("total", [P, U, MW], F32, local)
        source_idx = [v.sb(f"source_idx{k}", [P, 1], I32, local) for k in range(U)]
        target_idx = [v.sb(f"target_idx{k}", [P, 1], I32, local) for k in range(U)]
        summed = [v.ps(f"summed{k}", [P, 512], local) for k in range(U)]
        edges_in = [v.sem(f"edges_in{k}", local) for k in range(U)]
        rows_in = [v.sem(f"rows_in{k}", local) for k in range(U)]
        scattered = [v.sem(f"scattered{k}", local) for k in range(U)]
        idx_ready = v.sem("idx_ready", local)
        prepared = v.sem("prepared", local)
        messages = v.sem("messages", local)
        sums_ready = v.sem("sums_ready", local)
        totals = v.sem("totals", local)
        scatter_done = v.sem("scatter_done", local)
        passed = v.sem("passed", local)
        ones_set = v.sem("ones_set", local)
        STEPS = 5
        with nc.Block() as block:

            @block.sync
            def _(sp):
                with sp.Fori(0, TILES // U) as i:
                    for k in range(U):
                        tile = i * U + k
                        sp.wait_ge(sums_ready, tile + 1)
                        sp.dma_start(e[:, k, :], t["e32_cols"][:, bass.ds(tile, 1), :].rearrange("p a b -> p (a b)")).then_inc(edges_in[k], 16)
                        sp.dma_start(targets[:, k, :], t["src_rows"][bass.ds(tile, 1), :].broadcast_to([P, P])).then_inc(edges_in[k], 16)

            @block.gpsimd
            def _(pool):
                pool.sem_inc(scatter_done, U)

                def gather(i, k):
                    tile = i * U + k
                    pool.wait_ge(messages, tile + 1)
                    pool.wait_ge(idx_ready, tile + 1)
                    pool.sem_inc(passed, 1)
                    pool.indirect_dma_start(rows[k % 2][:].rearrange("p b d -> p (b d)"), None, v.products[:, :],
                                            bass.IndirectOffsetOnAxis(source_idx[k][:, 0:1], 0)).then_inc(rows_in[k], 16)

                def scatter(i, k):
                    tile = i * U + k
                    pool.wait_ge(totals, tile + 1)
                    pool.sem_inc(passed, 1)
                    pool.indirect_dma_start(v.sums0[k][:, :], bass.IndirectOffsetOnAxis(target_idx[k][:, 0:1], 0),
                                            total[:, k, :], None, compute_op=ALU.add).then_inc(scattered[k], 16)
                    pool.wait_ge(scattered[k], i * 16 + 16)
                    pool.sem_inc(scatter_done, 1)

                with pool.Fori(0, TILES // U) as i:
                    for k in range(U):
                        gather(i, k)
                        if k:
                            scatter(i, k - 1)
                    scatter(i, U - 1)

            @block.vector
            def _(dve):
                dve.memset(msg[:, :, D:MW], 1.0).then_inc(ones_set, 1)
                dve.wait_ge(ones_set, 1)
                dve.sem_inc(messages, 2)
                with dve.Fori(0, TILES // U) as i:
                    for k in range(U):
                        tile = i * U + k
                        chain = Chain(dve, prepared, tile * STEPS)
                        dve.wait_ge(scatter_done, tile + 1)
                        dve.tensor_copy(source_idx[k][:], v.dst_int[:, bass.ds(tile, 1)]).then_inc(idx_ready, 1)
                        dve.wait_ge(edges_in[k], i * 32 + 32)
                        chain.link(dve.tensor_scalar(same[:, k, :], targets[:, k, :], v.src_col[:, bass.ds(tile, 1)], None, ALU.is_equal))
                        chain.link(dve.tensor_tensor(scratch[:, k, :], same[:, k, :], v.dump_before[:], ALU.mult))
                        chain.link(dve.tensor_reduce(dup[:, k:k + 1], scratch[:, k, :], AX.X, ALU.max))
                        chain.step(dve.tensor_tensor(target_idx[k][:], dup[:, k:k + 1], v.src_col[:, bass.ds(tile, 1)], ALU.max))
                        dve.wait_ge(rows_in[k], i * 16 + 16)
                        chain.link(dve.tensor_tensor(rows[k % 2][:], rows[k % 2][:],
                                                     e[:, k, :].unsqueeze(2).broadcast_to([P, NB, D]), ALU.mult))
                        assert chain.n == STEPS
                        dve.tensor_reduce(msg[:, k, 0:D], rows[k % 2][:].rearrange("p b c -> p c b"), AX.X, ALU.add).then_inc(messages, 1)

            @block.tensor
            def _(pe):
                pe.sem_inc(sums_ready, U)
                with pe.Fori(0, TILES // U) as i:
                    for k in range(U):
                        tile = i * U + k
                        pe.wait_ge(messages, tile + 3)
                        pe.matmul(summed[k][:, 0:MW], same[:, k, :], msg[:, k, :], start=True, stop=True).then_inc(sums_ready, 1)

            @block.scalar
            def _(act):
                with act.Fori(0, TILES // U) as i:
                    for k in range(U):
                        tile = i * U + k
                        act.wait_ge(scatter_done, tile + 1)
                        act.wait_ge(sums_ready, tile + 5)
                        act.copy(total[:, k, :], summed[k][:, 0:MW]).then_inc(totals, 1)


def normalise(dve, act_wait, chain, raw, stats, outs, signal, passed):
    chain.link(dve.bn_stats(stats[:, 0:6], raw))
    dve.sem_inc(passed, 1)
    chain.link(dve.bn_aggr(stats[:, 6:8], stats[:, 0:6]))
    dve.tensor_scalar_add(stats[:, 8:9], stats[:, 7:8], EPS).then_inc(signal, 1)
    act_wait()
    chain.link(dve.reciprocal(stats[:, 10:11], stats[:, 9:10]))
    for out_view, in_view in outs:
        chain.step(dve.tensor_scalar(out_view, in_view, stats[:, 6:7], stats[:, 10:11], ALU.subtract, ALU.mult))
    chain.settle()


def layer0_nodes(nc, t, v):
    with ExitStack() as local:
        sb = lambda name, shape: [v.sb(f"{name}{k}", shape, F32, local) for k in range(2)]
        x, xs, xv = sb("n_x", [P, D]), sb("n_xs", [S, P]), sb("n_xv", [96, P])
        sums = sb("n_sums", [P, COPIES, MW])
        at_a, at_b = sb("at_a", [P, P]), sb("at_b", [33, P])
        raw, stats, xn, xn_parts = sb("raw", [P, D]), sb("stats", [P, 12]), sb("xn", [P, D]), sb("xn_parts", [P, D])
        xn_s, xn_v = sb("xn_s", [S, P]), sb("xn_v", [V, 3, P])
        y, own = sb("y", [P, D]), sb("own", [P, D])
        p_sums = [v.ps(f"p_sums{k}", [P, 2, P], local) for k in range(2)]
        p_h = [v.ps(f"p_h{k}", [P, D], local) for k in range(2)]
        p_xn = [v.ps(f"p_xn{k}", [S, 4, P], local) for k in range(2)]
        p_out = [v.ps(f"p_out{k}", [P, 320], local) for k in range(2)]
        loads = [v.sem(f"n_loads{k}", local) for k in range(2)]
        stores = [v.sem(f"n_stores{k}", local) for k in range(2)]
        stored = v.sem("n_stored", local)
        pe_steps = v.sem("n_pe_steps", local)
        act_steps = v.sem("n_act_steps", local)
        dve_chain = v.sem("n_dve_chain", local)
        var_ready = v.sem("n_var_ready", local)
        passed = v.sem("n_passed", local)
        xn_ready = v.sem("n_xn_ready", local)
        outs_ready = v.sem("n_outs_ready", local)
        STEPS = 6
        LOADS = 3 + COPIES
        with nc.Block() as block:

            @block.sync
            def _(sp):
                sp.sem_inc(stored, 2)
                with sp.Fori(0, BLOCKS // 2) as i:
                    for k in range(2):
                        at = bass.ds((i * 2 + k) * P, P)
                        sp.wait_ge(stored, i * 2 + k + 1)
                        sp.dma_start(x[k][:], t["x"][at, :]).then_inc(loads[k], 16)
                        sp.dma_start(xs[k][:], t["x_t"][0:S, at]).then_inc(loads[k], 16)
                        sp.dma_start(xv[k][:], t["x_t"][S:D, at]).then_inc(loads[k], 16)
                        for r in range(COPIES):
                            sp.dma_start(sums[k][:, r, :], v.sums0[r][at, :]).then_inc(loads[k], 16)
                    for k in range(2):
                        at = bass.ds((i * 2 + k) * P, P)
                        sp.wait_ge(outs_ready, i * 2 + k + 1)
                        sp.dma_start(v.y_table[at, :], y[k][:]).then_inc(stores[k], 16)
                        sp.dma_start(v.base_table[at, :], own[k][:]).then_inc(stores[k], 16)
                        sp.wait_ge(stores[k], i * 32 + 32)
                        sp.sem_inc(stored, 1)

            @block.tensor
            def _(pe):
                with pe.Fori(0, BLOCKS // 2) as i:
                    for k in range(2):
                        b = i * 2 + k
                        pe.wait_ge(loads[k], i * 16 * LOADS + 16 * LOADS)
                        for r in range(COPIES):
                            pe.matmul(p_sums[k][:, 0, :], sums[k][:, r, 0:P], v.ident[:], start=(r == 0), stop=(r == COPIES - 1))
                        for r in range(COPIES):
                            last = pe.matmul(p_sums[k][0:33, 1, :], sums[k][:, r, P:MW], v.ident[:], start=(r == 0), stop=(r == COPIES - 1))
                        last.then_inc(pe_steps, 1)
                        pe.matmul(p_h[k][:], xs[k][:], v.wu_s[:], start=True, stop=False)
                        pe.matmul(p_h[k][:], xv[k][:], v.wu_v[:], start=False, stop=False)
                        pe.matmul(p_h[k][:], v.ones[0:1, :], v.bu[:], start=False, stop=False)
                        pe.wait_ge(act_steps, b * 3 + 1)
                        pe.matmul(p_h[k][:], at_a[k][:], v.wmu_a[:], start=False, stop=False)
                        pe.matmul(p_h[k][:], at_b[k][:], v.wmu_b[:], start=False, stop=True).then_inc(pe_steps, 1)
                        pe.wait_ge(xn_ready, b + 1)
                        pe.sem_inc(passed, 1)
                        pe.transpose(p_xn[k][0:S, 0, :], xn_parts[k][:, 0:S], v.ident[:])
                        for c in range(3):
                            last = pe.transpose(p_xn[k][0:V, 1 + c, :], xn_parts[k][:, S + 32 * c:S + 32 * c + 32], v.ident[:])
                        last.then_inc(pe_steps, 1)
                        pe.wait_ge(act_steps, b * 3 + 3)
                        pe.matmul(p_out[k][:, 0:128], xn_s[k][:], v.w_node0[:], start=True, stop=True)
                        for c in range(3):
                            last = pe.matmul(p_out[k][:, 128 + 64 * c:192 + 64 * c], xn_v[k][:, c, :], v.w_node1[:], start=True, stop=True)
                        last.then_inc(pe_steps, 1)

            @block.scalar
            def _(act):
                with act.Fori(0, BLOCKS // 2) as i:
                    for k in range(2):
                        b = i * 2 + k
                        act.wait_ge(pe_steps, b * 4 + 1)
                        act.copy(at_a[k][:], p_sums[k][:, 0, :])
                        act.copy(at_b[k][:], p_sums[k][0:33, 1, :]).then_inc(act_steps, 1)
                        act.wait_ge(var_ready, b + 1)
                        act.activation(stats[k][:, 9:10], stats[k][:, 8:9], ACT.Sqrt).then_inc(act_steps, 1)
                        act.wait_ge(pe_steps, b * 4 + 3)
                        act.copy(xn_s[k][:], p_xn[k][0:S, 0, :])
                        act.copy(xn_v[k][:], p_xn[k][0:V, 1:4, :]).then_inc(act_steps, 1)

            @block.vector
            def _(dve):
                with dve.Fori(0, BLOCKS // 2) as i:
                    for k in range(2):
                        b = i * 2 + k
                        a = v.a_col[:, bass.ds(b, 1)]
                        chain = Chain(dve, dve_chain, b * STEPS)
                        dve.wait_ge(pe_steps, b * 4 + 2)
                        chain.link(dve.scalar_tensor_tensor(raw[k][:], x[k][:], 2.0, p_h[k][:], ALU.mult, ALU.add))
                        normalise(dve, lambda: dve.wait_ge(act_steps, b * 3 + 2), chain, raw[k][:], stats[k],
                                  [(xn_parts[k][:, 0:S], raw[k][:, 0:S]),
                                   (xn_parts[k][:, S:D].rearrange("p (i c) -> p i c", i=3),
                                    raw[k][:, S:D].rearrange("p (c i) -> p i c", i=3))], var_ready, passed)
                        dve.sem_inc(xn_ready, 1)
                        dve.wait_ge(pe_steps, b * 4 + 4)
                        parts = p_out[k][:, 128:320].rearrange("p (i w) -> p i w", i=3)
                        dve.tensor_scalar(y[k][:, 0:S], p_out[k][:, 0:S], a, None, ALU.mult)
                        dve.tensor_scalar(y[k][:, S:D].rearrange("p (i c) -> p i c", i=3), parts[:, :, 0:V], a, None, ALU.mult)
                        dve.scalar_tensor_tensor(own[k][:, 0:S], p_out[k][:, S:128], a, xn_parts[k][:, 0:S], ALU.mult, ALU.add)
                        dve.scalar_tensor_tensor(own[k][:, S:D].rearrange("p (c i) -> p i c", i=3), parts[:, :, V:64], a,
                                                 xn_parts[k][:, S:D].rearrange("p (i c) -> p i c", i=3), ALU.mult, ALU.add).then_inc(outs_ready, 1)
                        assert chain.n == STEPS, chain.n


def layer1_edges_any_order(nc, t, v):
    with ExitStack() as local:
        U = COPIES
        y = v.sb("e_y", [P, U, D], F32, local)
        lengths = v.sb("lengths", [10, U, P], F32, local)
        attr = v.sb("attr", [P, U, 4], F32, local)
        targets = v.sb("e_targets", [P, U, P], I32, local)
        same = v.sb("e_same", [P, U, P], F32, local)
        scratch = v.sb("e_scratch", [P, U, P], F32, local)
        dup = v.sb("e_dup", [P, U], F32, local)
        hidden = v.sb("hidden", [100, U, P], F32, local)
        prod = v.sb("prod", [P, U, 2, S], F32, local)
        w2e = v.sb("w2e", [P, U, V], F32, local)
        dot = v.sb("dot", [P, U, 3, V], F32, local)
        msg = v.sb("e_msg", [P, U, 4, 96], F32, local)
        total = v.sb("e_total", [P, U, UW], F32, local)
        source_idx = [v.sb(f"e_source_idx{k}", [P, 1], I32, local) for k in range(U)]
        target_idx = [v.sb(f"e_target_idx{k}", [P, 1], I32, local) for k in range(U)]
        p_hid = [v.ps(f"p_hid{k}", [P, 512], local) for k in range(2)]
        p_w = [v.ps(f"p_w{k}", [P, 512], local) for k in range(2)]
        p_sum = [v.ps(f"p_sum{k}", [P, 512], local) for k in range(4)]
        edges_in = [v.sem(f"e_edges_in{k}", local) for k in range(U)]
        rows_in = [v.sem(f"e_rows_in{k}", local) for k in range(U)]
        scattered = [v.sem(f"e_scattered{k}", local) for k in range(U)]
        idx_ready = v.sem("e_idx_ready", local)
        dve_chain = v.sem("e_dve_chain", local)
        act_chain = v.sem("e_act_chain", local)
        hidden_psum = v.sem("e_hidden_psum", local)
        hidden_ready = v.sem("e_hidden_ready", local)
        weights_psum = v.sem("e_weights_psum", local)
        prod_ready = v.sem("e_prod_ready", local)
        dve_part = v.sem("e_dve_part", local)
        act_part = v.sem("e_act_part", local)
        sums_ready = v.sem("e_sums_ready", local)
        totals = v.sem("e_totals", local)
        scatter_done = v.sem("e_scatter_done", local)
        passed = v.sem("e_passed", local)
        STEPS = 9
        with nc.Block() as block:

            @block.sync
            def _(sp):
                with sp.Fori(0, TILES // U) as i:
                    for k in range(U):
                        tile = i * U + k
                        sp.wait_ge(sums_ready, tile + 1)
                        sp.dma_start(attr[:, k, :], t["e4_cols"][:, bass.ds(tile, 1), :].rearrange("p a b -> p (a b)")).then_inc(edges_in[k], 16)
                        sp.dma_start(lengths[:, k, :], t["e10_t"][:, bass.ds(tile * P, P)]).then_inc(edges_in[k], 16)
                        sp.dma_start(targets[:, k, :], t["dst_rows"][bass.ds(tile, 1), :].broadcast_to([P, P])).then_inc(edges_in[k], 16)

            @block.gpsimd
            def _(pool):
                pool.sem_inc(scatter_done, U)

                def gather(i, k):
                    pool.wait_ge(sums_ready, i * U + k + 1)
                    pool.wait_ge(idx_ready, i * U + k + 1)
                    pool.sem_inc(passed, 1)
                    pool.indirect_dma_start(y[:, k, :], None, v.y_table[:, :],
                                            bass.IndirectOffsetOnAxis(source_idx[k][:, 0:1], 0)).then_inc(rows_in[k], 16)

                def scatter(i, k):
                    pool.wait_ge(totals, i * U + k + 1)
                    pool.sem_inc(passed, 1)
                    pool.indirect_dma_start(v.sums1[k][:, :], bass.IndirectOffsetOnAxis(target_idx[k][:, 0:1], 0),
                                            total[:, k, :], None, compute_op=ALU.add).then_inc(scattered[k], 16)

                def landed(i, k):
                    pool.wait_ge(scattered[k], i * 16 + 16)
                    pool.sem_inc(scatter_done, 1)

                with pool.Fori(0, TILES // U) as i:
                    for k in range(U):
                        gather(i, k)
                        if k > 0:
                            scatter(i, k - 1)
                        if k > 1:
                            landed(i, k - 2)
                    scatter(i, U - 1)
                    landed(i, U - 2)
                    landed(i, U - 1)

            @block.vector
            def _(dve):
                dve.sem_inc(dve_part, 2)
                with dve.Fori(0, TILES // U) as i:
                    for k in range(U):
                        tile = i * U + k
                        chain = Chain(dve, dve_chain, tile * STEPS)
                        dve.wait_ge(scatter_done, tile + 1)
                        dve.tensor_copy(source_idx[k][:], v.src_int[:, bass.ds(tile, 1)]).then_inc(idx_ready, 1)
                        dve.wait_ge(edges_in[k], i * 48 + 48)
                        dve.wait_ge(sums_ready, tile + 1)
                        chain.link(dve.tensor_scalar(same[:, k, :], targets[:, k, :], v.dst_col[:, bass.ds(tile, 1)], None, ALU.is_equal))
                        chain.link(dve.tensor_tensor(scratch[:, k, :], same[:, k, :], v.dump_before[:], ALU.mult))
                        chain.link(dve.tensor_reduce(dup[:, k:k + 1], scratch[:, k, :], AX.X, ALU.max))
                        chain.step(dve.tensor_tensor(target_idx[k][:], dup[:, k:k + 1], v.dst_col[:, bass.ds(tile, 1)], ALU.max))
                        dve.wait_ge(rows_in[k], i * 16 + 16)
                        dve.wait_ge(weights_psum, tile + 1)
                        w = p_w[k % 2]
                        y1 = y[:, k, S:D].rearrange("p (i c) -> p i c", i=3)
                        e0 = attr[:, k, 0:1]
                        dve.tensor_tensor(prod[:, k, :, :], w[:, 0:128].rearrange("p (g c) -> p g c", g=2),
                                          y[:, k, 0:S].unsqueeze(1).broadcast_to([P, 2, S]), ALU.mult).then_inc(prod_ready, 1)
                        chain.step(dve.tensor_scalar(w2e[:, k, :], w[:, 128:160], e0, None, ALU.mult))
                        chain.link(dve.tensor_scalar(dot[:, k, 0, :], y1[:, 0, :], attr[:, k, 1:2], None, ALU.mult))
                        chain.step(dve.tensor_tensor(msg[:, k, 1:4, S:96], y1, w2e[:, k, :].unsqueeze(1).broadcast_to([P, 3, V]), ALU.mult))
                        chain.link(dve.scalar_tensor_tensor(dot[:, k, 1, :], y1[:, 1, :], attr[:, k, 2:3], dot[:, k, 0, :], ALU.mult, ALU.add))
                        chain.link(dve.scalar_tensor_tensor(dot[:, k, 2, :], y1[:, 2, :], attr[:, k, 3:4], dot[:, k, 1, :], ALU.mult, ALU.add))
                        dve.tensor_tensor(msg[:, k, 0, S:96], dot[:, k, 2, :], w[:, 160:192], ALU.mult).then_inc(dve_part, 1)
                        assert chain.n == STEPS, chain.n

            @block.tensor
            def _(pe):
                pe.sem_inc(sums_ready, U)

                def radial(i, k):
                    tile = i * U + k
                    pe.wait_ge(edges_in[k], i * 48 + 48)
                    pe.matmul(p_hid[k % 2][0:100, 0:P], v.fc1[:], lengths[:, k, :], start=True, stop=True).then_inc(hidden_psum, 1)
                    pe.wait_ge(hidden_ready, tile + 1)
                    pe.wait_ge(dve_part, tile + 1)
                    pe.matmul(p_w[k % 2][:, 0:192], hidden[:, k, :], v.fc2[:], start=True, stop=True).then_inc(weights_psum, 1)

                with pe.Fori(0, TILES // U) as i:
                    for k in range(U):
                        tile = i * U + k
                        radial(i, k)
                        pe.wait_ge(act_part, tile + 1)
                        pe.wait_ge(dve_part, tile + 3)
                        pe.matmul(p_sum[k][:, 0:UW], same[:, k, :], msg[:, k, :, :].rearrange("p g c -> p (g c)"), start=True, stop=True).then_inc(sums_ready, 1)

            @block.scalar
            def _(act):
                with act.Fori(0, TILES // U) as i:
                    for k in range(U):
                        tile = i * U + k
                        act.wait_ge(hidden_psum, tile + 1)
                        act.activation(hidden[:, k, :], p_hid[k % 2][0:100, 0:P], ACT.Relu).then_inc(hidden_ready, 1)
                        act.wait_ge(prod_ready, tile + 1)
                        act.activation(msg[:, k, 0, 0:S], prod[:, k, 0, :], ACT.Copy, scale=attr[:, k, 0:1])
                        for c in range(3):
                            last = act.activation(msg[:, k, 1 + c, 0:S], prod[:, k, 1, :], ACT.Copy, scale=attr[:, k, 1 + c:2 + c])
                        last.then_inc(act_part, 1)
                        act.wait_ge(scatter_done, tile + 1)
                        act.wait_ge(sums_ready, tile + 5)
                        act.copy(total[:, k, :], p_sum[k][:, 0:UW]).then_inc(totals, 1)


def layer1_nodes(nc, t, v, out):
    with ExitStack() as local:
        sb = lambda name, shape: [v.sb(f"{name}{k}", shape, F32, local) for k in range(2)]
        own, sums, sums_t = sb("f_own", [P, D]), sb("f_sums", [P, COPIES, UW]), sb("f_sums_t", [96, 512])
        raw, stats, res = sb("f_raw", [P, D]), sb("f_stats", [P, 12]), sb("f_res", [P, D])
        p_t = [v.ps(f"f_p_t{k}", [P, 512], local) for k in range(2)]
        p_o = [v.ps(f"f_p_o{k}", [P, D], local) for k in range(2)]
        loads = [v.sem(f"f_loads{k}", local) for k in range(2)]
        stores = [v.sem(f"f_stores{k}", local) for k in range(2)]
        stored = v.sem("f_stored", local)
        pe_steps = v.sem("f_pe_steps", local)
        act_steps = v.sem("f_act_steps", local)
        dve_chain = v.sem("f_dve_chain", local)
        var_ready = v.sem("f_var_ready", local)
        passed = v.sem("f_passed", local)
        res_ready = v.sem("f_res_ready", local)
        STEPS = 6
        LOADS = 1 + COPIES
        FULL = NODES // P
        with nc.Block() as block:

            def blocks(eng, body):
                with eng.Fori(0, FULL // 2) as i:
                    body(i, (0, 1))
                body(FULL // 2, (0,))

            @block.sync
            def _(sp):
                sp.sem_inc(stored, 2)

                def body(i, ks):
                    for k in ks:
                        at = bass.ds((i * 2 + k) * P, P)
                        sp.wait_ge(stored, i * 2 + k + 1)
                        sp.dma_start(own[k][:], v.base_table[at, :]).then_inc(loads[k], 16)
                        for r in range(COPIES):
                            sp.dma_start(sums[k][:, r, :], v.sums1[r][at, :]).then_inc(loads[k], 16)
                    for k in ks:
                        sp.wait_ge(res_ready, i * 2 + k + 1)
                        rows = P if len(ks) == 2 else NODES - FULL * P
                        sp.dma_start(out[bass.ds((i * 2 + k) * P, rows), :], res[k][0:rows, :]).then_inc(stores[k], 16)
                        sp.wait_ge(stores[k], i * 16 + 16)
                        sp.sem_inc(stored, 1)

                blocks(sp, body)

            @block.tensor
            def _(pe):
                def body(i, ks):
                    for k in ks:
                        b = i * 2 + k
                        pe.wait_ge(loads[k], i * 16 * LOADS + 16 * LOADS)
                        for g in range(4):
                            for r in range(COPIES):
                                last = pe.matmul(p_t[k][0:96, P * g:P * g + P], sums[k][:, r, 96 * g:96 * g + 96], v.ident[:],
                                                 start=(r == 0), stop=(r == COPIES - 1))
                        last.then_inc(pe_steps, 1)
                        pe.wait_ge(act_steps, b * 2 + 1)
                        pe.matmul(p_o[k][:, 0:S], sums_t[k][:, 0:P], v.w_out0[:], start=True, stop=True)
                        for c in range(3):
                            last = pe.matmul(p_o[k][:, S + 32 * c:S + 32 * c + 32], sums_t[k][:, P * (c + 1):P * (c + 2)], v.w_out1[:],
                                             start=True, stop=True)
                        last.then_inc(pe_steps, 1)

                blocks(pe, body)

            @block.scalar
            def _(act):
                def body(i, ks):
                    for k in ks:
                        b = i * 2 + k
                        act.wait_ge(pe_steps, b * 2 + 1)
                        act.copy(sums_t[k][:], p_t[k][0:96, :]).then_inc(act_steps, 1)
                        act.wait_ge(var_ready, b + 1)
                        act.activation(stats[k][:, 9:10], stats[k][:, 8:9], ACT.Sqrt).then_inc(act_steps, 1)

                blocks(act, body)

            @block.vector
            def _(dve):
                def body(i, ks):
                    for k in ks:
                        b = i * 2 + k
                        a = v.a_col[:, bass.ds(b, 1)]
                        chain = Chain(dve, dve_chain, b * STEPS)
                        dve.wait_ge(pe_steps, b * 2 + 2)
                        chain.step(dve.scalar_tensor_tensor(raw[k][:, 0:S], p_o[k][:, 0:S], a, own[k][:, 0:S], ALU.mult, ALU.add))
                        chain.link(dve.scalar_tensor_tensor(raw[k][:, S:D].rearrange("p (c i) -> p i c", i=3),
                                                            p_o[k][:, S:D].rearrange("p (i c) -> p i c", i=3), a,
                                                            own[k][:, S:D].rearrange("p (c i) -> p i c", i=3), ALU.mult, ALU.add))
                        normalise(dve, lambda: dve.wait_ge(act_steps, b * 2 + 2), chain, raw[k][:], stats[k],
                                  [(res[k][:], raw[k][:])], var_ready, passed)
                        dve.sem_inc(res_ready, 1)
                        assert chain.n == STEPS, chain.n

                blocks(dve, body)


def kernel(**inputs):
    import numpy as np
    import concourse.bacc as bacc
    from concourse.bass_utils import run_bass_kernel_spmd

    a = {k: np.ascontiguousarray(w) for k, w in inputs.items()}

    def padded(w, rows, fill=0):
        p = np.full((rows,) + w.shape[1:], fill, w.dtype)
        p[:w.shape[0]] = w
        return p

    def parts_first(w):
        return np.concatenate([w[:S], w[S:].reshape(V, 3, -1).transpose(1, 0, 2).reshape(96, -1)])

    EP = TILES * P
    x = padded(a["x"], NODE_ROWS)
    src, dst = padded(a["src"], EP, PAD_NODE), padded(a["dst"], EP, PAD_NODE)
    e32 = padded(a["edge_attr_32"], EP)
    e32 = np.concatenate([e32[:, :8], e32[:, 8:].reshape(EP, 8, 3).transpose(0, 2, 1).reshape(EP, 24)], axis=1)
    w1, w2, w3, w4 = (a[f"L0_gnn_W{n}"] for n in (1, 2, 3, 4))
    arrays = {
        "x": x,
        "x_t": parts_first(np.ascontiguousarray(x.T)),
        "src_rows": src.reshape(TILES, P), "dst_rows": dst.reshape(TILES, P),
        "src_cols": src.reshape(TILES, P).T, "dst_cols": dst.reshape(TILES, P).T,
        "e32_cols": e32.reshape(TILES, P, NB).transpose(1, 0, 2),
        "e4_cols": padded(a["edge_attr_4"], EP).reshape(TILES, P, 4).transpose(1, 0, 2),
        "e10_t": padded(a["edge_attr_10"], EP).T,
        "a_cols": padded(a["node_vec1"], NODE_ROWS).reshape(BLOCKS, P).T,
        "w1": w1.reshape(S, 512), "w2": w2.reshape(V, 512), "w3": w3.reshape(S, 256), "w4": w4.reshape(V, 256),
        "wm_t": np.concatenate([parts_first(a["L0_gnn_Wm"]), a["L0_gnn_bm"].reshape(1, D)]).T,
        "wu_top": parts_first(a["L0_gnn_Wu"][:D]), "wu_bot": a["L0_gnn_Wu"][D:], "bu": a["L0_gnn_bu"].reshape(1, D),
        "w_node0": np.concatenate([a["L1_gnn_W_l1_0"], a["L1_gnn_W_si0"]], axis=1),
        "w_node1": np.concatenate([a["L1_gnn_W_l1_1"], a["L1_gnn_W_si1"]], axis=1),
        "w_out0": np.concatenate([a["L1_gnn_W_l2_00"], a["L1_gnn_W_l2_10"]]),
        "w_out1": np.concatenate([a["L1_gnn_W_l2_01"], a["L1_gnn_W_l2_11"]]),
        "fc1": a["L1_gnn_W_fc1"], "fc2": a["L1_gnn_W_fc2"],
    }
    arrays = {f"in_{k}": np.ascontiguousarray(w) for k, w in arrays.items()}
    nc = bacc.Bacc("TRN2", target_bir_lowering=False, num_devices=1)
    t = {k[3:]: nc.dram_tensor(k, w.shape, mybir.dt.from_np(w.dtype), kind="ExternalInput").ap() for k, w in arrays.items()}
    out = nc.dram_tensor("out_0", (NODES, D), F32, kind="ExternalOutput").ap()
    build_program(nc, t, out)
    return run_bass_kernel_spmd(nc, [arrays], core_ids=[0]).results[0]["out_0"]
```

```python
import math
from contextlib import ExitStack

import concourse.bass as bass
from concourse import mybir

F32 = mybir.dt.float32
I32 = mybir.dt.int32
BF16 = mybir.dt.bfloat16
ALU = mybir.AluOpType
ACT = mybir.ActivationFunctionType
AX = mybir.AxisListType

P = 128
NODES, EDGES = 6250, 100000
BLOCKS = 50
NODE_ROWS = BLOCKS * P
TILES = 784
PAD_NODE = NODES
CHUNK = 16
CHUNKS = TILES // CHUNK
WINDOW = 4
SPAN = 40
TABLE_ROWS = NODE_ROWS + P
DUMP = NODE_ROWS
S, V, D = 64, 32, 160
NB = 32
GW = NB * D
MW = D + 1
UW = 384
COPIES = 4
EPS = 1e-5

K1 = 1.0 / math.sqrt(S * 8) / math.sqrt(2.0)
K2 = 1.0 / (math.sqrt(3.0) * math.sqrt(V * 8)) / math.sqrt(2.0)
K3 = 1.0 / math.sqrt(S * 8) / math.sqrt(2.0)
K4 = 1.0 / math.sqrt(V * 8) / math.sqrt(2.0)


class Chain:

    def __init__(self, eng, sem, base=0):
        self.eng, self.sem, self.base, self.n = eng, sem, base, 0

    def step(self, ins):
        self.n += 1
        return ins.then_inc(self.sem, 1)

    def settle(self):
        self.eng.wait_ge(self.sem, self.base + self.n)

    def link(self, ins):
        self.step(ins)
        self.settle()


def skewed(eng, loops, unroll, *stages, at_body=None):
    most = max(lead for lead, _ in stages)
    for step in range(-most, 0):
        for lead, fn in stages:
            if step + lead >= 0:
                fn(0, step + lead)
    with eng.Fori(0, loops - 1) as i:
        if at_body:
            at_body(i)
        for k in range(unroll):
            for lead, fn in stages:
                fn(i + (k + lead) // unroll, (k + lead) % unroll)
    if at_body:
        at_body(loops - 1)
    for k in range(unroll):
        for lead, fn in stages:
            if k + lead < unroll:
                fn(loops - 1, k + lead)


class Shared:
    pass


def build_program(nc, t, out):
    ctx = ExitStack()
    with ctx:
        def sb(name, shape, dt=F32, where=ctx):
            return where.enter_context(nc.sbuf_tensor(name, shape, dt))

        def ps(name, shape, where=ctx):
            return where.enter_context(nc.psum_tensor(name, shape, F32))

        def sem(name, where=ctx):
            return where.enter_context(nc.semaphore(name))

        def dram(name, shape):
            return nc.dram_tensor(name, shape, F32).ap()

        v = Shared()
        v.sb, v.ps, v.sem = sb, ps, sem
        v.products = dram("products", (NODE_ROWS, GW))
        v.sums0 = [dram(f"sums0_{r}", (TABLE_ROWS, MW)) for r in range(COPIES)]
        v.sums1 = [dram(f"sums1_{r}", (TABLE_ROWS, UW)) for r in range(COPIES)]
        v.y_table = dram("y_table", (NODE_ROWS, D))
        v.base_table = dram("base_table", (NODE_ROWS, D))

        v.chunk_group = nc.dram_tensor("chunk_group", (CHUNKS + 1, 1), I32).ap()
        v.tile_slot = nc.dram_tensor("tile_slot", (1, TILES + 4), I32).ap()
        v.split_rows = nc.dram_tensor("split_rows", (2, 2, TILES * P), BF16).ap()
        v.tile_base = dram("tile_base", (CHUNKS, CHUNK))

        v.ident = sb("ident", [P, P])
        v.ones = sb("ones", [P, P])
        v.ones2 = sb("ones2", [2, P], BF16)
        v.dump_before = sb("dump_before", [P, P])
        v.w1 = sb("w1", [S, 512])
        v.w2 = sb("w2", [96, 512])
        v.w3 = sb("w3", [S, 256])
        v.w4 = sb("w4", [96, 256])
        v.wm_t = sb("wm_t", [P, 2, MW])
        v.wu_bot = sb("wu_bot", [P, 2, D])
        v.wu_s = sb("wu_s", [S, D])
        v.wu_v = sb("wu_v", [96, D])
        v.bu = sb("bu", [1, D])
        v.wmu_a = sb("wmu_a", [P, D])
        v.wmu_b = sb("wmu_b", [33, D])
        v.w_node0 = sb("w_node0", [S, 128])
        v.w_node1 = sb("w_node1", [V, 64])
        v.w_out0 = sb("w_out0", [96, S])
        v.w_out1 = sb("w_out1", [96, V])
        v.fc1 = sb("fc1", [10, 100])
        v.fc2 = sb("fc2", [100, 192])
        v.src_col = sb("src_col", [P, TILES])
        v.dst_col = sb("dst_col", [P, TILES])
        v.src_int = sb("src_int", [P, TILES], I32)
        v.dst_int = sb("dst_int", [P, TILES], I32)
        v.window_node = sb("window_node", [P, WINDOW, TILES])
        v.scattered_order = sb("scattered_order", [1, 1], I32)
        v.a_col = sb("a_col", [P, BLOCKS])

        setup_phase(nc, t, v)
        products_phase(nc, t, v)
        windows_phase(nc, t, v)
        layer0_edges(nc, t, v)
        layer0_nodes(nc, t, v)
        layer1_edges_any_order(nc, t, v)
        layer1_nodes(nc, t, v, out)


def setup_phase(nc, t, v):
    with ExitStack() as local:
        sb = lambda name, shape, dt=F32: v.sb(name, shape, dt, local)
        zeros = sb("zeros", [P, 51 * MW])
        psum = v.ps("setup_psum", [P, 2, 512], local)
        loaded = v.sem("setup_loaded", local)
        cleared = v.sem("setup_cleared", local)
        zeroed = v.sem("setup_zeroed", local)
        filled = v.sem("setup_filled", local)
        scaled = v.sem("setup_scaled", local)
        merged = v.sem("setup_merged", local)
        n_loads = [0]
        with nc.Block() as block:

            @block.sync
            def _(sp):
                def load(dst, src):
                    n_loads[0] += 1
                    sp.dma_start(dst, src).then_inc(loaded, 16)

                load(v.w1[:], t["w1"])
                load(v.w3[:], t["w3"])
                load(v.w_node0[:], t["w_node0"])
                load(v.w_node1[:], t["w_node1"])
                for i in range(3):
                    load(v.w2[32 * i:32 * i + 32, :], t["w2"])
                    load(v.w4[32 * i:32 * i + 32, :], t["w4"])
                load(v.wm_t[:, 0, :], t["wm_t"][0:P, :])
                load(v.wm_t[0:32, 1, :], t["wm_t"][P:D, :])
                load(v.wu_bot[:, 0, :], t["wu_bot"][0:P, :])
                load(v.wu_bot[0:32, 1, :], t["wu_bot"][P:D, :])
                load(v.wu_s[:], t["wu_top"][0:S, :])
                load(v.wu_v[:], t["wu_top"][S:D, :])
                load(v.bu[:], t["bu"])
                load(v.w_out0[:], t["w_out0"])
                load(v.w_out1[:], t["w_out1"])
                load(v.fc1[:], t["fc1"])
                load(v.fc2[:], t["fc2"])
                load(v.src_int[:], t["src_cols"])
                load(v.dst_int[:], t["dst_cols"])
                load(v.a_col[:], t["a_cols"])
                sp.wait_ge(zeroed, 1)
                for r in range(COPIES):
                    sp.dma_start(v.sums0[r].rearrange("(p a) d -> p (a d)", p=P), zeros[:]).then_inc(cleared, 16)
                    for h in range(3):
                        sp.dma_start(v.sums1[r].rearrange("(p a) d -> p (a d)", p=P)[:, h * 17 * UW:(h + 1) * 17 * UW],
                                     zeros[:, 0:17 * UW]).then_inc(cleared, 16)
                sp.wait_ge(cleared, 16 * COPIES * 4)

            @block.gpsimd
            def _(pool):
                pool.memset(v.ident[:], 0.0).then_inc(filled, 1)
                pool.memset(v.ones[:], 1.0).then_inc(filled, 1)
                pool.memset(v.ones2[:], 1.0)
                pool.iota(v.dump_before[:], [[0, P]], base=DUMP, channel_multiplier=1,
                          allow_small_or_imprecise_dtypes=True).then_inc(filled, 1)
                pool.wait_ge(filled, 3)
                pool.affine_select(out=v.ident[:], in_=v.ident[:], compare_op=ALU.not_equal, fill=1.0,
                                   base=0, pattern=[[-1, P]], channel_multiplier=1).then_inc(filled, 1)
                pool.affine_select(out=v.dump_before[:], in_=v.dump_before[:], compare_op=ALU.is_gt, fill=0.0,
                                   base=0, pattern=[[-1, P]], channel_multiplier=1).then_inc(filled, 1)

            @block.vector
            def _(dve):
                dve.memset(zeros[:], 0.0).then_inc(zeroed, 1)
                dve.wait_ge(loaded, 16 * n_loads[0])
                dve.tensor_copy(v.src_col[:], v.src_int[:])
                dve.tensor_copy(v.dst_col[:], v.dst_int[:])
                for weight, k in ((v.w1, K1), (v.w2, K2), (v.w3, K3), (v.w4, K4),
                                (v.w_node0, 1.0 / math.sqrt(S)), (v.w_node1, 1.0 / math.sqrt(V)),
                                (v.w_out0, 0.125 / math.sqrt(96.0)), (v.w_out1, 0.125 / math.sqrt(96.0)),
                                (v.fc1, math.sqrt(2.0 / 10.0)), (v.fc2, 0.1)):
                    dve.tensor_scalar(weight[:], weight[:], k, None, ALU.mult).then_inc(scaled, 1)
                dve.wait_ge(scaled, 10)
                dve.tensor_scalar(v.fc2[:, 160:192], v.fc2[:, 160:192], 1.0 / math.sqrt(3.0), None, ALU.mult)
                dve.wait_ge(merged, 1)
                dve.tensor_copy(v.wmu_a[:], psum[:, 0, 0:D])
                dve.tensor_copy(v.wmu_b[:], psum[0:33, 1, 0:D])

            @block.tensor
            def _(pe):
                pe.wait_ge(loaded, 16 * n_loads[0])
                for m, (m0, m1) in enumerate(((0, P), (P, MW))):
                    pe.matmul(psum[0:m1 - m0, m, 0:D], v.wm_t[:, 0, m0:m1], v.wu_bot[:, 0, :], start=True, stop=False)
                    last = pe.matmul(psum[0:m1 - m0, m, 0:D], v.wm_t[0:32, 1, m0:m1], v.wu_bot[0:32, 1, :],
                                     start=False, stop=True)
                last.then_inc(merged, 1)


def products_phase(nc, t, v):
    with ExitStack() as local:
        xs = [v.sb(f"xs{k}", [S, P], F32, local) for k in range(2)]
        xv = [v.sb(f"xv{k}", [96, P], F32, local) for k in range(2)]
        g = [v.sb(f"g{k}", [P, NB, D], F32, local) for k in range(2)]
        bank = [v.ps(f"g_bank{k}", [P, 512], local) for k in range(8)]
        x_in = [v.sem(f"x_in{k}", local) for k in range(2)]
        banks_full = v.sem("banks_full", local)
        act_done = v.sem("act_done", local)
        dve_done = v.sem("dve_done", local)
        blank = v.sem("blank", local)
        g_free = v.sem("g_free", local)
        g_out = [v.sem(f"g_out{k}", local) for k in range(2)]
        with nc.Block() as block:

            @block.gpsimd
            def _(pool):
                for k in range(2):
                    pool.memset(g[k][:], 0.0).then_inc(blank, 1)

            @block.sync
            def _(sp):
                sp.wait_ge(blank, 2)
                sp.sem_inc(g_free, 2)
                with sp.Fori(0, BLOCKS // 2) as i:
                    for k in range(2):
                        b = i * 2 + k
                        sp.wait_ge(banks_full, b + 1)
                        sp.dma_start(xs[k][:], t["x_t"][0:S, bass.ds(b * P, P)]).then_inc(x_in[k], 16)
                        sp.dma_start(xv[k][:], t["x_t"][S:D, bass.ds(b * P, P)]).then_inc(x_in[k], 16)
                    for k in range(2):
                        b = i * 2 + k
                        sp.wait_ge(act_done, b + 2)
                        sp.wait_ge(dve_done, b + 2)
                        sp.dma_start(v.products[bass.ds(b * P, P), :], g[k][:].rearrange("p b d -> p (b d)")).then_inc(g_out[k], 16)
                        sp.wait_ge(g_out[k], i * 16 + 16)
                        sp.sem_inc(g_free, 1)

            @block.tensor
            def _(pe):
                pe.sem_inc(banks_full, 2)
                with pe.Fori(0, BLOCKS // 2) as i:
                    for k in range(2):
                        b = i * 2 + k
                        pe.wait_ge(x_in[k], i * 32 + 32)
                        pe.wait_ge(act_done, b + 1)
                        pe.wait_ge(dve_done, b + 1)
                        pe.matmul(bank[0][:], xs[k][:], v.w1[:], start=True, stop=True)
                        for c in range(3):
                            lo, hi = 32 * c, 32 * c + 32
                            pe.matmul(bank[1 + c][:], xv[k][lo:hi, :], v.w2[lo:hi, :], start=True, stop=True)
                            pe.matmul(bank[4 + c][:, 0:256], xv[k][lo:hi, :], v.w4[lo:hi, :], start=True, stop=True)
                        pe.matmul(bank[7][:, 0:256], xs[k][:], v.w3[:], start=True, stop=True).then_inc(banks_full, 1)

            @block.scalar
            def _(act):
                act.sem_inc(act_done, 1)
                with act.Fori(0, BLOCKS // 2) as i:
                    for k in range(2):
                        b = i * 2 + k
                        act.wait_ge(g_free, b + 1)
                        act.wait_ge(banks_full, b + 3)
                        for q in range(3):
                            last = act.copy(g[k][:, 8 * q:8 * q + 8, 0:S], bank[q][:].rearrange("p (b c) -> p b c", c=S))
                        last.then_inc(act_done, 1)

            @block.vector
            def _(dve):
                dve.sem_inc(dve_done, 1)
                with dve.Fori(0, BLOCKS // 2) as i:
                    for k in range(2):
                        b = i * 2 + k
                        dve.wait_ge(g_free, b + 1)
                        dve.wait_ge(banks_full, b + 3)
                        dve.tensor_copy(g[k][:, 24:32, 0:S], bank[3][:].rearrange("p (b c) -> p b c", c=S))
                        for c in range(3):
                            dve.tensor_copy(g[k][:, 0:8, S + 32 * c:S + 32 * c + 32],
                                            bank[4 + c][:, 0:256].rearrange("p (b c) -> p b c", c=V))
                        for c in range(3):
                            last = dve.tensor_copy(g[k][:, 8 + 8 * c:16 + 8 * c, S + 32 * c:S + 32 * c + 32],
                                                   bank[7][:, 0:256].rearrange("p (b c) -> p b c", c=V))
                        last.then_inc(dve_done, 1)


def windows_phase(nc, t, v):
    with ExitStack() as local:
        grid = v.sb("grid", [CHUNKS, CHUNK, P], I32, local)
        source_grid = v.sb("source_grid", [CHUNKS, CHUNK * P], I32, local)
        part_int = v.sb("part_int", [CHUNKS, 4, CHUNK * P], I32, local)
        part = v.sb("part", [CHUNKS, 4, CHUNK * P], BF16, local)
        zero_slots = v.sb("zero_slots", [1, 4], I32, local)
        parts_ready = v.sem("parts_ready", local)
        small = v.sb("small", [CHUNKS, 8, CHUNK], F32, local)
        least, most, base, over, rel = (small[:, n, :] for n in range(5))
        ints = v.sb("ints", [CHUNKS, 3, CHUNK], I32, local)
        chunk = v.sb("chunk", [CHUNKS, 4], F32, local)
        chunk_int = v.sb("chunk_int", [CHUNKS, 2], I32, local)
        zero_int = v.sb("zero_int", [1, 1], I32, local)
        odd = v.sb("odd", [CHUNKS, 1], I32, local)
        quarter = v.sb("quarter", [P, 1], I32, local)
        quarter_f = v.sb("quarter_f", [P, 1], F32, local)
        base_all = v.sb("base_all", [P, TILES], F32, local)
        violations = v.ps("violations", [P, 512], local)
        grid_in = v.sem("grid_in", local)
        iotas = v.sem("iotas", local)
        chain_sem = v.sem("w_chain", local)
        tables_ready = v.sem("tables_ready", local)
        tables_out = v.sem("tables_out", local)
        counted = v.sem("counted", local)
        violations_summed = v.sem("violations_summed", local)
        with nc.Block() as block:

            @block.sync
            def _(sp):
                sp.dma_start(grid[:], t["dst_rows"].rearrange("(c j) e -> c j e", j=CHUNK)).then_inc(grid_in, 16)
                sp.dma_start(source_grid[:], t["src_rows"].rearrange("(c j) e -> c (j e)", j=CHUNK)).then_inc(grid_in, 16)
                sp.wait_ge(tables_ready, 1)
                sp.dma_start(v.chunk_group[0:CHUNKS, :], chunk_int[:, 0:1]).then_inc(tables_out, 16)
                sp.dma_start(v.chunk_group[CHUNKS:, :], zero_int[:]).then_inc(tables_out, 16)
                sp.dma_start(v.tile_slot[:, 3:3 + TILES].rearrange("a (c j) -> (a c) j", j=CHUNK), ints[:, 2, :]).then_inc(tables_out, 16)
                sp.dma_start(v.tile_slot[:, 0:3], zero_slots[:, 0:3]).then_inc(tables_out, 16)
                sp.dma_start(v.tile_slot[:, 3 + TILES:], zero_slots[:, 3:4]).then_inc(tables_out, 16)
                sp.dma_start(v.tile_base, base).then_inc(tables_out, 16)
                sp.wait_ge(parts_ready, 4)
                for n in range(4):
                    sp.dma_start(v.split_rows[n // 2, n % 2, :].rearrange("(c e) -> c e", c=CHUNKS), part[:, n, :]).then_inc(tables_out, 16)
                sp.wait_ge(tables_out, 160)
                sp.dma_start(base_all[:], v.tile_base.rearrange("(a c) j -> a (c j)", a=1).broadcast_to([P, TILES])).then_inc(tables_out, 16)

            @block.gpsimd
            def _(pool):
                pool.iota(odd[:], [[0, 1]], base=0, channel_multiplier=1).then_inc(iotas, 1)
                pool.iota(quarter[:], [[0, 1]], base=0, channel_multiplier=1).then_inc(iotas, 1)

            @block.vector
            def _(dve):
                chain = Chain(dve, chain_sem)
                chain.step(dve.memset(zero_int[:], 0))
                chain.step(dve.memset(zero_slots[:], 0))
                dve.wait_ge(grid_in, 32)
                nodes = grid[:].rearrange("c j e -> c (j e)")
                for n, (ids, mask) in enumerate(((nodes, -64), (source_grid[:], -64), (nodes, 63), (source_grid[:], 63))):
                    chain.step(dve.tensor_scalar(part_int[:, n, :], ids, mask, None, ALU.bitwise_and))
                chain.settle()
                for n in range(4):
                    dve.tensor_copy(part[:, n, :], part_int[:, n, :]).then_inc(parts_ready, 1)
                chain.step(dve.tensor_reduce(least, grid[:], AX.X, ALU.min))
                chain.link(dve.tensor_reduce(most, grid[:], AX.X, ALU.max))
                chain.link(dve.tensor_copy(ints[:, 0, :], least))
                chain.link(dve.tensor_scalar(ints[:, 1, :], ints[:, 0, :], -4, None, ALU.bitwise_and))
                chain.link(dve.tensor_copy(base, ints[:, 1, :]))
                chain.link(dve.tensor_reduce(chunk[:, 0:1], base, AX.X, ALU.min))
                chain.link(dve.tensor_scalar(chunk[:, 1:2], chunk[:, 0:1], float(NODE_ROWS - 4 * SPAN), None, ALU.min))
                chain.step(dve.tensor_scalar(chunk_int[:, 0:1], chunk[:, 1:2], 0.25, None, ALU.mult))
                chain.link(dve.tensor_scalar(rel, base, chunk[:, 1:2], 0.25, ALU.subtract, ALU.mult))
                chain.step(dve.tensor_scalar(small[:, 5, :], rel, float(SPAN - WINDOW), 0.0, ALU.subtract, ALU.max))
                chain.link(dve.tensor_tensor(over, most, base, ALU.subtract))
                chain.link(dve.tensor_scalar(small[:, 6, :], over, float(4 * WINDOW - 1), 0.0, ALU.subtract, ALU.max))
                chain.link(dve.tensor_tensor(small[:, 7, :], small[:, 5, :], small[:, 6, :], ALU.add))
                chain.step(dve.tensor_reduce(chunk[:, 2:3], small[:, 7, :], AX.X, ALU.add))
                dve.wait_ge(iotas, 2)
                chain.link(dve.tensor_scalar(chunk_int[:, 1:2], odd[:], 1, None, ALU.bitwise_and))
                dve.sem_inc(counted, 1)
                chain.step(dve.tensor_scalar(chunk[:, 3:4], chunk_int[:, 1:2], float(SPAN), None, ALU.mult))
                chain.link(dve.tensor_scalar(small[:, 5, :], rel, float(SPAN - WINDOW), None, ALU.min))
                dve.tensor_scalar(ints[:, 2, :], small[:, 5, :], chunk[:, 3:4], None, ALU.add).then_inc(tables_ready, 1)
                chain.link(dve.tensor_scalar(quarter[:], quarter[:], 5, None, ALU.logical_shift_right))
                chain.link(dve.tensor_copy(quarter_f[:], quarter[:]))
                dve.wait_ge(tables_out, 176)
                for j in range(WINDOW):
                    dve.tensor_scalar(v.window_node[:, j, :], base_all[:], quarter_f[:], float(4 * j), ALU.add, ALU.add)
                dve.wait_ge(violations_summed, 1)
                dve.tensor_scalar(v.scattered_order[:], violations[0:1, 0:1], 0.0, None, ALU.is_gt)

            @block.tensor
            def _(pe):
                pe.wait_ge(counted, 1)
                pe.matmul(violations[0:1, 0:1], chunk[:, 2:3], v.ones[0:CHUNKS, 0:1], start=True, stop=True).then_inc(violations_summed, 1)


def layer0_edges(nc, t, v):
    with ExitStack() as local:
        U = COPIES
        big = v.sb("big", [P, 2 * SPAN, D], F32, local)
        windows = big
        rows = [big[:, NB * k:NB * k + NB, :] for k in range(2)]
        features = [v.sb(f"features{h}", [P, 4, P], F32, local) for h in range(4)]
        id_rows = [v.sb(f"id_rows{h}", [2, 2, 4 * P], BF16, local) for h in range(4)]
        spread = v.sb("spread", [P, 4, WINDOW, P], F32, local)
        e = v.sb("e", [P, U, NB], F32, local)
        targets = v.sb("targets", [P, U, P], I32, local)
        same = v.sb("same", [P, U, P], F32, local)
        scratch = v.sb("scratch", [P, U, P], F32, local)
        dup = v.sb("dup", [P, U], F32, local)
        msg = v.sb("msg", [P, U, MW], F32, local)
        total = v.sb("total", [P, U, MW], F32, local)
        source_idx = [v.sb(f"source_idx{k}", [P, 1], I32, local) for k in range(U)]
        target_idx = [v.sb(f"target_idx{k}", [P, 1], I32, local) for k in range(8)]
        summed = [v.ps(f"summed{k}", [P, 512], local) for k in range(U)]
        p_msg, p_sum = summed[0:2], summed[2:4]
        p_node = [v.ps(f"p_node{h}", [P, 4, P], local) for h in range(2)]
        p_target = [v.ps(f"p_target{h}", [P, 4, P], local) for h in range(2)]
        batch_in = [v.sem(f"batch_in{h}", local) for h in range(4)]
        ids_spread = v.sem("ids_spread", local)
        chunk_landed = v.sem("chunk_landed", local)
        chunk_ready = v.sem("chunk_ready", local)
        dve_steps = v.sem("dve_steps", local)
        f_scattered = [v.sem(f"f_scattered{k}", local) for k in range(U)]
        built = v.sem("built", local)
        expanded = v.sem("expanded", local)
        copied = v.sem("copied", local)
        f_summed = v.sem("f_summed", local)
        f_totals = v.sem("f_totals", local)
        f_done = v.sem("f_done", local)
        edges_in = [v.sem(f"edges_in{k}", local) for k in range(U)]
        rows_in = [v.sem(f"rows_in{k}", local) for k in range(U)]
        scattered = [v.sem(f"scattered{k}", local) for k in range(U)]
        idx_ready = v.sem("idx_ready", local)
        prepared = v.sem("prepared", local)
        messages = v.sem("messages", local)
        sums_ready = v.sem("sums_ready", local)
        totals = v.sem("totals", local)
        scatter_done = v.sem("scatter_done", local)
        passed = v.sem("passed", local)
        ones_set = v.sem("ones_set", local)
        STEPS = 5
        def choose(eng, fast, slow):
            order = eng.value_load(v.scattered_order[0:1, 0:1], min_val=0, max_val=1)
            with eng.If(order == 0):
                fast(eng)
            with eng.Else():
                slow(eng)

        with nc.Block() as block:

            def fast_sync(sp):
                def load_chunk(c, free=None):
                    group = sp.value_load(v.chunk_group[bass.ds(c, 1), :], min_val=0, max_val=NODE_ROWS // 4 - SPAN)
                    if free is not None:
                        sp.wait_ge(expanded, free)
                    half = (c % 2) * SPAN
                    sp.dma_start(windows[:, bass.ds(half, SPAN), :],
                                 v.products.rearrange("(g n) (b c) -> (n b) g c", n=4, b=NB)[:, bass.ds(group, SPAN), :]).then_inc(chunk_landed, 16)

                def load_batch(i, h):
                    sp.wait_ge(built, i * CHUNK + 4 * h + 4)
                    edges = bass.ds(i * (CHUNK * P) + h * (4 * P), 4 * P)
                    sp.dma_start(id_rows[h][:], v.split_rows[:, :, edges]).then_inc(batch_in[h], 16)
                    for n in range(4):
                        sp.dma_start(features[h][32 * n:32 * n + 32, :, :].rearrange("p a b -> p (a b)"), t["e32_t"][:, edges]).then_inc(batch_in[h], 16)

                load_chunk(0)
                sp.wait_ge(chunk_landed, 16)
                sp.sem_inc(chunk_ready, 1)
                with sp.Fori(0, CHUNKS) as c:
                    for h in range(2):
                        load_batch(c, h)
                    load_chunk(c + 1, c * CHUNK + CHUNK)
                    for h in range(2, 4):
                        load_batch(c, h)
                    sp.wait_ge(chunk_landed, c * 16 + 32)
                    sp.sem_inc(chunk_ready, 1)

            def slow_sync(sp):
                with sp.Fori(0, TILES // U) as i:
                    for k in range(U):
                        tile = i * U + k
                        sp.wait_ge(sums_ready, tile + 1)
                        sp.dma_start(e[:, k, :], t["e32_cols"][:, bass.ds(tile, 1), :].rearrange("p a b -> p (a b)")).then_inc(edges_in[k], 16)
                        sp.dma_start(targets[:, k, :], t["src_rows"][bass.ds(tile, 1), :].broadcast_to([P, P])).then_inc(edges_in[k], 16)

            @block.sync
            def _(sp):
                choose(sp, fast_sync, slow_sync)

            def fast_gpsimd(pool):
                pool.sem_inc(f_done, 8)

                def scatter(i, k):
                    pool.wait_ge(f_totals, i * CHUNK + k + 3)
                    pool.wait_ge(built, i * CHUNK + k + 17)
                    pool.sem_inc(passed, 1)
                    pool.indirect_dma_start(v.sums0[k % 4][:, :], bass.IndirectOffsetOnAxis(target_idx[k % 8][:, 0:1], 0),
                                            total[:, k % 4, :], None, compute_op=ALU.add).then_inc(f_scattered[k % 4], 16)

                def landed(i, k):
                    pool.wait_ge(f_scattered[k % 4], i * 64 + 16 * (k // 4) + 16)
                    pool.sem_inc(f_done, 1)

                skewed(pool, CHUNKS, CHUNK, (3, scatter), (0, landed))

            def slow_gpsimd(pool):
                pool.sem_inc(scatter_done, U)

                def gather(i, k):
                    tile = i * U + k
                    pool.wait_ge(messages, tile + 1)
                    pool.wait_ge(idx_ready, tile + 1)
                    pool.sem_inc(passed, 1)
                    pool.indirect_dma_start(rows[k % 2].rearrange("p b d -> p (b d)"), None, v.products[:, :],
                                            bass.IndirectOffsetOnAxis(source_idx[k][:, 0:1], 0)).then_inc(rows_in[k], 16)

                def scatter(i, k):
                    tile = i * U + k
                    pool.wait_ge(totals, tile + 1)
                    pool.sem_inc(passed, 1)
                    pool.indirect_dma_start(v.sums0[k][:, :], bass.IndirectOffsetOnAxis(target_idx[k][:, 0:1], 0),
                                            total[:, k, :], None, compute_op=ALU.add).then_inc(scattered[k], 16)
                    pool.wait_ge(scattered[k], i * 16 + 16)
                    pool.sem_inc(scatter_done, 1)

                with pool.Fori(0, TILES // U) as i:
                    for k in range(U):
                        gather(i, k)
                        if k:
                            scatter(i, k - 1)
                    scatter(i, U - 1)

            @block.gpsimd
            def _(pool):
                choose(pool, fast_gpsimd, slow_gpsimd)

            def fast_vector(dve):
                STEPS = 2
                dve.memset(msg[:, :, D:MW], 1.0).then_inc(ones_set, 1)
                dve.wait_ge(ones_set, 1)
                dve.sem_inc(built, 16)

                def build(i, k):
                    tile, h, q = i * CHUNK + k, k // 4, k % 4
                    chain = Chain(dve, dve_steps, tile * STEPS)

                    def spread_window(j):
                        return dve.scalar_tensor_tensor(spread[:, q, j, :], p_node[h % 2][:, q, :], v.window_node[:, j, bass.ds(tile, 1)],
                                                        features[h][:, q, :], ALU.is_equal, ALU.mult)

                    dve.wait_ge(batch_in[h], i * 80 + 80)
                    dve.wait_ge(ids_spread, i * 4 + h + 1)
                    dve.wait_ge(f_summed, tile + 1)
                    chain.step(dve.tensor_scalar(same[:, q, :], p_target[h % 2][:, q, :], v.src_col[:, bass.ds(tile, 1)], None, ALU.is_equal))
                    dve.wait_ge(expanded, tile + 13)
                    spread_window(0)
                    chain.settle()
                    spread_window(1)
                    chain.step(dve.tensor_tensor_reduce(out=scratch[:, q, :], in0=same[:, q, :], in1=v.dump_before[:], scale=1.0, scalar=0.0,
                                                        op0=ALU.mult, op1=ALU.max, accum_out=dup[:, q:q + 1]))
                    spread_window(2)
                    spread_window(3)
                    dve.wait_ge(f_done, tile + 1)
                    chain.settle()
                    dve.tensor_tensor(target_idx[k % 8][:], dup[:, q:q + 1], v.src_col[:, bass.ds(tile, 1)], ALU.max).then_inc(built, 1)

                skewed(dve, CHUNKS, CHUNK, (0, build))

            def slow_vector(dve):
                dve.memset(msg[:, :, D:MW], 1.0).then_inc(ones_set, 1)
                dve.wait_ge(ones_set, 1)
                dve.sem_inc(messages, 2)
                with dve.Fori(0, TILES // U) as i:
                    for k in range(U):
                        tile = i * U + k
                        chain = Chain(dve, prepared, tile * STEPS)
                        dve.wait_ge(scatter_done, tile + 1)
                        dve.tensor_copy(source_idx[k][:], v.dst_int[:, bass.ds(tile, 1)]).then_inc(idx_ready, 1)
                        dve.wait_ge(edges_in[k], i * 32 + 32)
                        chain.link(dve.tensor_scalar(same[:, k, :], targets[:, k, :], v.src_col[:, bass.ds(tile, 1)], None, ALU.is_equal))
                        chain.link(dve.tensor_tensor(scratch[:, k, :], same[:, k, :], v.dump_before[:], ALU.mult))
                        chain.link(dve.tensor_reduce(dup[:, k:k + 1], scratch[:, k, :], AX.X, ALU.max))
                        chain.step(dve.tensor_tensor(target_idx[k][:], dup[:, k:k + 1], v.src_col[:, bass.ds(tile, 1)], ALU.max))
                        dve.wait_ge(rows_in[k], i * 16 + 16)
                        chain.link(dve.tensor_tensor(rows[k % 2], rows[k % 2],
                                                     e[:, k, :].unsqueeze(2).broadcast_to([P, NB, D]), ALU.mult))
                        assert chain.n == STEPS
                        dve.tensor_reduce(msg[:, k, 0:D], rows[k % 2].rearrange("p b c -> p c b"), AX.X, ALU.add).then_inc(messages, 1)

            @block.vector
            def _(dve):
                choose(dve, fast_vector, slow_vector)

            def fast_tensor(pe):
                slots = [0] * CHUNK

                def load_slots(i):
                    _, slots[:] = nc.values_load_multi_w_load_instructions(
                        v.tile_slot[:, bass.ds(i * CHUNK + 4, CHUNK)], engines=(mybir.EngineType.PE,), min_val=0, max_val=2 * SPAN - WINDOW)

                def spread_ids(i, k):
                    if k % 4:
                        return
                    h = k // 4
                    pe.wait_ge(batch_in[h], i * 80 + 80)
                    pe.wait_ge(built, i * CHUNK + 4 * h + 12)
                    pe.matmul(p_node[h % 2][:].rearrange("p a b -> p (a b)"), v.ones2[:], id_rows[h][:, 0, :], start=True, stop=True)
                    pe.matmul(p_target[h % 2][:].rearrange("p a b -> p (a b)"), v.ones2[:], id_rows[h][:, 1, :], start=True, stop=True).then_inc(ids_spread, 1)

                slots[CHUNK - 1] = pe.value_load(v.tile_slot[:, 3:4], min_val=0, max_val=2 * SPAN - WINDOW)
                pe.sem_inc(expanded, CHUNK)
                pe.sem_inc(f_summed, 4)

                def expand(i, k):
                    tile, q = i * CHUNK + k, k % 4
                    slot = slots[(k - 1) % CHUNK]
                    pe.wait_ge(chunk_ready, i + 1)
                    pe.wait_ge(built, tile + 17)
                    pe.wait_ge(copied, tile + 1)
                    for j in range(WINDOW):
                        last = pe.matmul(p_msg[q % 2][:, 0:D], spread[:, q, j, :], windows[:, bass.ds(slot + j, 1), :].rearrange("p a b -> p (a b)"),
                                         start=(j == 0), stop=(j == WINDOW - 1))
                    last.then_inc(expanded, 1)

                def add_up(i, k):
                    tile, q = i * CHUNK + k, k % 4
                    pe.wait_ge(copied, tile + 3)
                    pe.wait_ge(f_totals, tile + 1)
                    pe.matmul(p_sum[q % 2][:, 0:MW], same[:, q, :], msg[:, q, :], start=True, stop=True).then_inc(f_summed, 1)

                skewed(pe, CHUNKS, CHUNK, (5, spread_ids), (1, expand), (0, add_up), at_body=load_slots)

            def slow_tensor(pe):
                pe.sem_inc(sums_ready, U)
                with pe.Fori(0, TILES // U) as i:
                    for k in range(U):
                        tile = i * U + k
                        pe.wait_ge(messages, tile + 3)
                        pe.matmul(summed[k][:, 0:MW], same[:, k, :], msg[:, k, :], start=True, stop=True).then_inc(sums_ready, 1)

            @block.tensor
            def _(pe):
                choose(pe, fast_tensor, slow_tensor)

            def fast_scalar(act):
                act.sem_inc(copied, 2)
                act.sem_inc(f_totals, 2)

                def copy_messages(i, k):
                    tile, q = i * CHUNK + k, k % 4
                    act.wait_ge(f_summed, tile + 1)
                    act.wait_ge(expanded, tile + CHUNK + 1)
                    act.copy(msg[:, q, 0:D], p_msg[q % 2][:, 0:D]).then_inc(copied, 1)

                def copy_totals(i, k):
                    tile, q = i * CHUNK + k, k % 4
                    act.wait_ge(f_done, tile + 5)
                    act.wait_ge(f_summed, tile + 5)
                    act.copy(total[:, q, :], p_sum[q % 2][:, 0:MW]).then_inc(f_totals, 1)

                skewed(act, CHUNKS, CHUNK, (1, copy_messages), (0, copy_totals))

            def slow_scalar(act):
                with act.Fori(0, TILES // U) as i:
                    for k in range(U):
                        tile = i * U + k
                        act.wait_ge(scatter_done, tile + 1)
                        act.wait_ge(sums_ready, tile + 5)
                        act.copy(total[:, k, :], summed[k][:, 0:MW]).then_inc(totals, 1)

            @block.scalar
            def _(act):
                choose(act, fast_scalar, slow_scalar)


def normalise(dve, act_wait, chain, raw, stats, outs, signal, passed):
    chain.link(dve.bn_stats(stats[:, 0:6], raw))
    dve.sem_inc(passed, 1)
    chain.link(dve.bn_aggr(stats[:, 6:8], stats[:, 0:6]))
    dve.tensor_scalar_add(stats[:, 8:9], stats[:, 7:8], EPS).then_inc(signal, 1)
    act_wait()
    chain.link(dve.reciprocal(stats[:, 10:11], stats[:, 9:10]))
    for out_view, in_view in outs:
        chain.step(dve.tensor_scalar(out_view, in_view, stats[:, 6:7], stats[:, 10:11], ALU.subtract, ALU.mult))
    chain.settle()


def layer0_nodes(nc, t, v):
    with ExitStack() as local:
        sb = lambda name, shape: [v.sb(f"{name}{k}", shape, F32, local) for k in range(2)]
        x, xs, xv = sb("n_x", [P, D]), sb("n_xs", [S, P]), sb("n_xv", [96, P])
        sums = sb("n_sums", [P, COPIES, MW])
        at_a, at_b = sb("at_a", [P, P]), sb("at_b", [33, P])
        raw, stats, xn, xn_parts = sb("raw", [P, D]), sb("stats", [P, 12]), sb("xn", [P, D]), sb("xn_parts", [P, D])
        xn_s, xn_v = sb("xn_s", [S, P]), sb("xn_v", [V, 3, P])
        y, own = sb("y", [P, D]), sb("own", [P, D])
        p_sums = [v.ps(f"p_sums{k}", [P, 2, P], local) for k in range(2)]
        p_h = [v.ps(f"p_h{k}", [P, D], local) for k in range(2)]
        p_xn = [v.ps(f"p_xn{k}", [S, 4, P], local) for k in range(2)]
        p_out = [v.ps(f"p_out{k}", [P, 320], local) for k in range(2)]
        loads = [v.sem(f"n_loads{k}", local) for k in range(2)]
        stores = [v.sem(f"n_stores{k}", local) for k in range(2)]
        stored = v.sem("n_stored", local)
        pe_steps = v.sem("n_pe_steps", local)
        act_steps = v.sem("n_act_steps", local)
        dve_chain = v.sem("n_dve_chain", local)
        var_ready = v.sem("n_var_ready", local)
        passed = v.sem("n_passed", local)
        xn_ready = v.sem("n_xn_ready", local)
        outs_ready = v.sem("n_outs_ready", local)
        STEPS = 6
        LOADS = 3 + COPIES
        with nc.Block() as block:

            @block.sync
            def _(sp):
                sp.sem_inc(stored, 2)
                with sp.Fori(0, BLOCKS // 2) as i:
                    for k in range(2):
                        at = bass.ds((i * 2 + k) * P, P)
                        sp.wait_ge(stored, i * 2 + k + 1)
                        sp.dma_start(x[k][:], t["x"][at, :]).then_inc(loads[k], 16)
                        sp.dma_start(xs[k][:], t["x_t"][0:S, at]).then_inc(loads[k], 16)
                        sp.dma_start(xv[k][:], t["x_t"][S:D, at]).then_inc(loads[k], 16)
                        for r in range(COPIES):
                            sp.dma_start(sums[k][:, r, :], v.sums0[r][at, :]).then_inc(loads[k], 16)
                    for k in range(2):
                        at = bass.ds((i * 2 + k) * P, P)
                        sp.wait_ge(outs_ready, i * 2 + k + 1)
                        sp.dma_start(v.y_table[at, :], y[k][:]).then_inc(stores[k], 16)
                        sp.dma_start(v.base_table[at, :], own[k][:]).then_inc(stores[k], 16)
                        sp.wait_ge(stores[k], i * 32 + 32)
                        sp.sem_inc(stored, 1)

            @block.tensor
            def _(pe):
                with pe.Fori(0, BLOCKS // 2) as i:
                    for k in range(2):
                        b = i * 2 + k
                        pe.wait_ge(loads[k], i * 16 * LOADS + 16 * LOADS)
                        for r in range(COPIES):
                            pe.matmul(p_sums[k][:, 0, :], sums[k][:, r, 0:P], v.ident[:], start=(r == 0), stop=(r == COPIES - 1))
                        for r in range(COPIES):
                            last = pe.matmul(p_sums[k][0:33, 1, :], sums[k][:, r, P:MW], v.ident[:], start=(r == 0), stop=(r == COPIES - 1))
                        last.then_inc(pe_steps, 1)
                        pe.matmul(p_h[k][:], xs[k][:], v.wu_s[:], start=True, stop=False)
                        pe.matmul(p_h[k][:], xv[k][:], v.wu_v[:], start=False, stop=False)
                        pe.matmul(p_h[k][:], v.ones[0:1, :], v.bu[:], start=False, stop=False)
                        pe.wait_ge(act_steps, b * 3 + 1)
                        pe.matmul(p_h[k][:], at_a[k][:], v.wmu_a[:], start=False, stop=False)
                        pe.matmul(p_h[k][:], at_b[k][:], v.wmu_b[:], start=False, stop=True).then_inc(pe_steps, 1)
                        pe.wait_ge(xn_ready, b + 1)
                        pe.sem_inc(passed, 1)
                        pe.transpose(p_xn[k][0:S, 0, :], xn_parts[k][:, 0:S], v.ident[:])
                        for c in range(3):
                            last = pe.transpose(p_xn[k][0:V, 1 + c, :], xn_parts[k][:, S + 32 * c:S + 32 * c + 32], v.ident[:])
                        last.then_inc(pe_steps, 1)
                        pe.wait_ge(act_steps, b * 3 + 3)
                        pe.matmul(p_out[k][:, 0:128], xn_s[k][:], v.w_node0[:], start=True, stop=True)
                        for c in range(3):
                            last = pe.matmul(p_out[k][:, 128 + 64 * c:192 + 64 * c], xn_v[k][:, c, :], v.w_node1[:], start=True, stop=True)
                        last.then_inc(pe_steps, 1)

            @block.scalar
            def _(act):
                with act.Fori(0, BLOCKS // 2) as i:
                    for k in range(2):
                        b = i * 2 + k
                        act.wait_ge(pe_steps, b * 4 + 1)
                        act.copy(at_a[k][:], p_sums[k][:, 0, :])
                        act.copy(at_b[k][:], p_sums[k][0:33, 1, :]).then_inc(act_steps, 1)
                        act.wait_ge(var_ready, b + 1)
                        act.activation(stats[k][:, 9:10], stats[k][:, 8:9], ACT.Sqrt).then_inc(act_steps, 1)
                        act.wait_ge(pe_steps, b * 4 + 3)
                        act.copy(xn_s[k][:], p_xn[k][0:S, 0, :])
                        act.copy(xn_v[k][:], p_xn[k][0:V, 1:4, :]).then_inc(act_steps, 1)

            @block.vector
            def _(dve):
                with dve.Fori(0, BLOCKS // 2) as i:
                    for k in range(2):
                        b = i * 2 + k
                        a = v.a_col[:, bass.ds(b, 1)]
                        chain = Chain(dve, dve_chain, b * STEPS)
                        dve.wait_ge(pe_steps, b * 4 + 2)
                        chain.link(dve.scalar_tensor_tensor(raw[k][:], x[k][:], 2.0, p_h[k][:], ALU.mult, ALU.add))
                        normalise(dve, lambda: dve.wait_ge(act_steps, b * 3 + 2), chain, raw[k][:], stats[k],
                                  [(xn_parts[k][:, 0:S], raw[k][:, 0:S]),
                                   (xn_parts[k][:, S:D].rearrange("p (i c) -> p i c", i=3),
                                    raw[k][:, S:D].rearrange("p (c i) -> p i c", i=3))], var_ready, passed)
                        dve.sem_inc(xn_ready, 1)
                        dve.wait_ge(pe_steps, b * 4 + 4)
                        parts = p_out[k][:, 128:320].rearrange("p (i w) -> p i w", i=3)
                        dve.tensor_scalar(y[k][:, 0:S], p_out[k][:, 0:S], a, None, ALU.mult)
                        dve.tensor_scalar(y[k][:, S:D].rearrange("p (i c) -> p i c", i=3), parts[:, :, 0:V], a, None, ALU.mult)
                        dve.scalar_tensor_tensor(own[k][:, 0:S], p_out[k][:, S:128], a, xn_parts[k][:, 0:S], ALU.mult, ALU.add)
                        dve.scalar_tensor_tensor(own[k][:, S:D].rearrange("p (c i) -> p i c", i=3), parts[:, :, V:64], a,
                                                 xn_parts[k][:, S:D].rearrange("p (i c) -> p i c", i=3), ALU.mult, ALU.add).then_inc(outs_ready, 1)
                        assert chain.n == STEPS, chain.n


def layer1_edges_any_order(nc, t, v):
    with ExitStack() as local:
        U = COPIES
        y = v.sb("e_y", [P, U, D], F32, local)
        lengths = v.sb("lengths", [10, U, P], F32, local)
        attr = v.sb("attr", [P, U, 4], F32, local)
        targets = v.sb("e_targets", [P, U, P], I32, local)
        same = v.sb("e_same", [P, U, P], F32, local)
        scratch = v.sb("e_scratch", [P, U, P], F32, local)
        dup = v.sb("e_dup", [P, U], F32, local)
        hidden = v.sb("hidden", [100, U, P], F32, local)
        prod = v.sb("prod", [P, U, 2, S], F32, local)
        w2e = v.sb("w2e", [P, U, V], F32, local)
        dot = v.sb("dot", [P, U, 3, V], F32, local)
        msg = v.sb("e_msg", [P, U, 4, 96], F32, local)
        total = v.sb("e_total", [P, U, UW], F32, local)
        source_idx = [v.sb(f"e_source_idx{k}", [P, 1], I32, local) for k in range(U)]
        target_idx = [v.sb(f"e_target_idx{k}", [P, 1], I32, local) for k in range(U)]
        p_hid = [v.ps(f"p_hid{k}", [P, 512], local) for k in range(2)]
        p_w = [v.ps(f"p_w{k}", [P, 512], local) for k in range(2)]
        p_sum = [v.ps(f"p_sum{k}", [P, 512], local) for k in range(4)]
        edges_in = [v.sem(f"e_edges_in{k}", local) for k in range(U)]
        rows_in = [v.sem(f"e_rows_in{k}", local) for k in range(U)]
        scattered = [v.sem(f"e_scattered{k}", local) for k in range(U)]
        idx_ready = v.sem("e_idx_ready", local)
        dve_chain = v.sem("e_dve_chain", local)
        prep_chain = v.sem("e_prep_chain", local)
        act_chain = v.sem("e_act_chain", local)
        hidden_psum = v.sem("e_hidden_psum", local)
        hidden_ready = v.sem("e_hidden_ready", local)
        weights_psum = v.sem("e_weights_psum", local)
        prod_ready = v.sem("e_prod_ready", local)
        dve_part = v.sem("e_dve_part", local)
        act_part = v.sem("e_act_part", local)
        sums_ready = v.sem("e_sums_ready", local)
        totals = v.sem("e_totals", local)
        scatter_done = v.sem("e_scatter_done", local)
        passed = v.sem("e_passed", local)
        STEPS = 5
        with nc.Block() as block:

            @block.sync
            def _(sp):
                with sp.Fori(0, TILES // U) as i:
                    for k in range(U):
                        tile = i * U + k
                        sp.wait_ge(sums_ready, tile + 1)
                        sp.dma_start(attr[:, k, :], t["e4_cols"][:, bass.ds(tile, 1), :].rearrange("p a b -> p (a b)")).then_inc(edges_in[k], 16)
                        sp.dma_start(lengths[:, k, :], t["e10_t"][:, bass.ds(tile * P, P)]).then_inc(edges_in[k], 16)
                        sp.dma_start(targets[:, k, :], t["dst_rows"][bass.ds(tile, 1), :].broadcast_to([P, P])).then_inc(edges_in[k], 16)

            @block.gpsimd
            def _(pool):
                pool.sem_inc(scatter_done, U)

                def gather(i, k):
                    pool.wait_ge(sums_ready, i * U + k + 1)
                    pool.wait_ge(idx_ready, i * U + k + 1)
                    pool.sem_inc(passed, 1)
                    pool.indirect_dma_start(y[:, k, :], None, v.y_table[:, :],
                                            bass.IndirectOffsetOnAxis(source_idx[k][:, 0:1], 0)).then_inc(rows_in[k], 16)

                def scatter(i, k):
                    pool.wait_ge(totals, i * U + k + 1)
                    pool.sem_inc(passed, 1)
                    pool.indirect_dma_start(v.sums1[k][:, :], bass.IndirectOffsetOnAxis(target_idx[k][:, 0:1], 0),
                                            total[:, k, :], None, compute_op=ALU.add).then_inc(scattered[k], 16)

                def landed(i, k):
                    pool.wait_ge(scattered[k], i * 16 + 16)
                    pool.sem_inc(scatter_done, 1)

                skewed(pool, TILES // U, U, (3, gather), (1, scatter), (0, landed))

            @block.vector
            def _(dve):
                dve.sem_inc(dve_part, 2)
                def prepare(i, k):
                    tile = i * U + k
                    chain = Chain(dve, prep_chain, tile * 3)
                    dve.wait_ge(scatter_done, tile + 1)
                    dve.wait_ge(edges_in[k], i * 48 + 48)
                    dve.wait_ge(sums_ready, tile + 1)
                    chain.link(dve.tensor_scalar(same[:, k, :], targets[:, k, :], v.dst_col[:, bass.ds(tile, 1)], None, ALU.is_equal))
                    dve.tensor_copy(source_idx[k][:], v.src_int[:, bass.ds(tile, 1)]).then_inc(idx_ready, 1)
                    chain.link(dve.tensor_tensor_reduce(out=scratch[:, k, :], in0=same[:, k, :], in1=v.dump_before[:], scale=1.0, scalar=0.0,
                                                        op0=ALU.mult, op1=ALU.max, accum_out=dup[:, k:k + 1]))
                    chain.step(dve.tensor_tensor(target_idx[k][:], dup[:, k:k + 1], v.dst_col[:, bass.ds(tile, 1)], ALU.max))

                def weigh(i, k):
                    tile = i * U + k
                    chain = Chain(dve, dve_chain, tile * STEPS)
                    dve.wait_ge(rows_in[k], i * 16 + 16)
                    dve.wait_ge(weights_psum, tile + 1)
                    w = p_w[k % 2]
                    y1 = y[:, k, S:D].rearrange("p (i c) -> p i c", i=3)
                    e0 = attr[:, k, 0:1]
                    dve.tensor_tensor(prod[:, k, :, :], w[:, 0:128].rearrange("p (g c) -> p g c", g=2),
                                      y[:, k, 0:S].unsqueeze(1).broadcast_to([P, 2, S]), ALU.mult).then_inc(prod_ready, 1)
                    chain.step(dve.tensor_scalar(w2e[:, k, :], w[:, 128:160], e0, None, ALU.mult))
                    chain.link(dve.tensor_scalar(dot[:, k, 0, :], y1[:, 0, :], attr[:, k, 1:2], None, ALU.mult))
                    chain.step(dve.tensor_tensor(msg[:, k, 1:4, S:96], y1, w2e[:, k, :].unsqueeze(1).broadcast_to([P, 3, V]), ALU.mult))
                    chain.link(dve.scalar_tensor_tensor(dot[:, k, 1, :], y1[:, 1, :], attr[:, k, 2:3], dot[:, k, 0, :], ALU.mult, ALU.add))
                    chain.link(dve.scalar_tensor_tensor(dot[:, k, 2, :], y1[:, 2, :], attr[:, k, 3:4], dot[:, k, 1, :], ALU.mult, ALU.add))
                    dve.tensor_tensor(msg[:, k, 0, S:96], dot[:, k, 2, :], w[:, 160:192], ALU.mult).then_inc(dve_part, 1)
                    assert chain.n == STEPS, chain.n

                skewed(dve, TILES // U, U, (1, prepare), (0, weigh))

            @block.tensor
            def _(pe):
                pe.sem_inc(sums_ready, U)

                def hide(i, k):
                    pe.wait_ge(edges_in[k], i * 48 + 48)
                    pe.wait_ge(hidden_ready, i * U + k + 1)
                    pe.matmul(p_hid[k % 2][0:100, 0:P], v.fc1[:], lengths[:, k, :], start=True, stop=True).then_inc(hidden_psum, 1)

                def radial(i, k):
                    tile = i * U + k
                    pe.wait_ge(hidden_ready, tile + 3)
                    pe.wait_ge(dve_part, tile + 1)
                    pe.matmul(p_w[k % 2][:, 0:192], hidden[:, k, :], v.fc2[:], start=True, stop=True).then_inc(weights_psum, 1)

                def add_up(i, k):
                    tile = i * U + k
                    pe.wait_ge(prep_chain, tile * 3 + 3)
                    pe.wait_ge(act_part, tile + 1)
                    pe.wait_ge(dve_part, tile + 3)
                    pe.matmul(p_sum[k][:, 0:UW], same[:, k, :], msg[:, k, :, :].rearrange("p g c -> p (g c)"), start=True, stop=True).then_inc(sums_ready, 1)

                skewed(pe, TILES // U, U, (2, hide), (1, radial), (0, add_up))

            @block.scalar
            def _(act):
                act.sem_inc(hidden_ready, 2)

                def rectify(i, k):
                    tile = i * U + k
                    act.wait_ge(hidden_psum, tile + 1)
                    act.wait_ge(sums_ready, tile + 1)
                    act.activation(hidden[:, k, :], p_hid[k % 2][0:100, 0:P], ACT.Relu).then_inc(hidden_ready, 1)

                def weigh(i, k):
                    tile = i * U + k
                    act.wait_ge(prod_ready, tile + 1)
                    act.activation(msg[:, k, 0, 0:S], prod[:, k, 0, :], ACT.Copy, scale=attr[:, k, 0:1])
                    for c in range(3):
                        last = act.activation(msg[:, k, 1 + c, 0:S], prod[:, k, 1, :], ACT.Copy, scale=attr[:, k, 1 + c:2 + c])
                    last.then_inc(act_part, 1)

                def copy_totals(i, k):
                    tile = i * U + k
                    act.wait_ge(scatter_done, tile + 1)
                    act.wait_ge(sums_ready, tile + 5)
                    act.copy(total[:, k, :], p_sum[k][:, 0:UW]).then_inc(totals, 1)

                skewed(act, TILES // U, U, (3, rectify), (1, weigh), (0, copy_totals))


def layer1_nodes(nc, t, v, out):
    with ExitStack() as local:
        sb = lambda name, shape: [v.sb(f"{name}{k}", shape, F32, local) for k in range(2)]
        own, sums, sums_t = sb("f_own", [P, D]), sb("f_sums", [P, COPIES, UW]), sb("f_sums_t", [96, 512])
        raw, stats, res = sb("f_raw", [P, D]), sb("f_stats", [P, 12]), sb("f_res", [P, D])
        p_t = [v.ps(f"f_p_t{k}", [P, 512], local) for k in range(2)]
        p_o = [v.ps(f"f_p_o{k}", [P, D], local) for k in range(2)]
        loads = [v.sem(f"f_loads{k}", local) for k in range(2)]
        stores = [v.sem(f"f_stores{k}", local) for k in range(2)]
        stored = v.sem("f_stored", local)
        pe_steps = v.sem("f_pe_steps", local)
        act_steps = v.sem("f_act_steps", local)
        dve_chain = v.sem("f_dve_chain", local)
        var_ready = v.sem("f_var_ready", local)
        passed = v.sem("f_passed", local)
        res_ready = v.sem("f_res_ready", local)
        STEPS = 6
        LOADS = 1 + COPIES
        FULL = NODES // P
        with nc.Block() as block:

            def blocks(eng, body):
                with eng.Fori(0, FULL // 2) as i:
                    body(i, (0, 1))
                body(FULL // 2, (0,))

            @block.sync
            def _(sp):
                sp.sem_inc(stored, 2)

                def body(i, ks):
                    for k in ks:
                        at = bass.ds((i * 2 + k) * P, P)
                        sp.wait_ge(stored, i * 2 + k + 1)
                        sp.dma_start(own[k][:], v.base_table[at, :]).then_inc(loads[k], 16)
                        for r in range(COPIES):
                            sp.dma_start(sums[k][:, r, :], v.sums1[r][at, :]).then_inc(loads[k], 16)
                    for k in ks:
                        sp.wait_ge(res_ready, i * 2 + k + 1)
                        rows = P if len(ks) == 2 else NODES - FULL * P
                        sp.dma_start(out[bass.ds((i * 2 + k) * P, rows), :], res[k][0:rows, :]).then_inc(stores[k], 16)
                        sp.wait_ge(stores[k], i * 16 + 16)
                        sp.sem_inc(stored, 1)

                blocks(sp, body)

            @block.tensor
            def _(pe):
                def body(i, ks):
                    for k in ks:
                        b = i * 2 + k
                        pe.wait_ge(loads[k], i * 16 * LOADS + 16 * LOADS)
                        for g in range(4):
                            for r in range(COPIES):
                                last = pe.matmul(p_t[k][0:96, P * g:P * g + P], sums[k][:, r, 96 * g:96 * g + 96], v.ident[:],
                                                 start=(r == 0), stop=(r == COPIES - 1))
                        last.then_inc(pe_steps, 1)
                        pe.wait_ge(act_steps, b * 2 + 1)
                        pe.matmul(p_o[k][:, 0:S], sums_t[k][:, 0:P], v.w_out0[:], start=True, stop=True)
                        for c in range(3):
                            last = pe.matmul(p_o[k][:, S + 32 * c:S + 32 * c + 32], sums_t[k][:, P * (c + 1):P * (c + 2)], v.w_out1[:],
                                             start=True, stop=True)
                        last.then_inc(pe_steps, 1)

                blocks(pe, body)

            @block.scalar
            def _(act):
                def body(i, ks):
                    for k in ks:
                        b = i * 2 + k
                        act.wait_ge(pe_steps, b * 2 + 1)
                        act.copy(sums_t[k][:], p_t[k][0:96, :]).then_inc(act_steps, 1)
                        act.wait_ge(var_ready, b + 1)
                        act.activation(stats[k][:, 9:10], stats[k][:, 8:9], ACT.Sqrt).then_inc(act_steps, 1)

                blocks(act, body)

            @block.vector
            def _(dve):
                def body(i, ks):
                    for k in ks:
                        b = i * 2 + k
                        a = v.a_col[:, bass.ds(b, 1)]
                        chain = Chain(dve, dve_chain, b * STEPS)
                        dve.wait_ge(pe_steps, b * 2 + 2)
                        chain.step(dve.scalar_tensor_tensor(raw[k][:, 0:S], p_o[k][:, 0:S], a, own[k][:, 0:S], ALU.mult, ALU.add))
                        chain.link(dve.scalar_tensor_tensor(raw[k][:, S:D].rearrange("p (c i) -> p i c", i=3),
                                                            p_o[k][:, S:D].rearrange("p (i c) -> p i c", i=3), a,
                                                            own[k][:, S:D].rearrange("p (c i) -> p i c", i=3), ALU.mult, ALU.add))
                        normalise(dve, lambda: dve.wait_ge(act_steps, b * 2 + 2), chain, raw[k][:], stats[k],
                                  [(res[k][:], raw[k][:])], var_ready, passed)
                        dve.sem_inc(res_ready, 1)
                        assert chain.n == STEPS, chain.n

                blocks(dve, body)


def kernel(**inputs):
    import numpy as np
    import concourse.bacc as bacc
    from concourse.bass_utils import run_bass_kernel_spmd

    a = {k: np.ascontiguousarray(w) for k, w in inputs.items()}

    def padded(w, rows, fill=0):
        p = np.full((rows,) + w.shape[1:], fill, w.dtype)
        p[:w.shape[0]] = w
        return p

    def parts_first(w):
        return np.concatenate([w[:S], w[S:].reshape(V, 3, -1).transpose(1, 0, 2).reshape(96, -1)])

    EP = TILES * P
    x = padded(a["x"], NODE_ROWS)
    src, dst = padded(a["src"], EP, PAD_NODE), padded(a["dst"], EP, PAD_NODE)
    e32 = padded(a["edge_attr_32"], EP)
    e32 = np.concatenate([e32[:, :8], e32[:, 8:].reshape(EP, 8, 3).transpose(0, 2, 1).reshape(EP, 24)], axis=1)
    w1, w2, w3, w4 = (a[f"L0_gnn_W{n}"] for n in (1, 2, 3, 4))
    arrays = {
        "x": x,
        "x_t": parts_first(np.ascontiguousarray(x.T)),
        "src_rows": src.reshape(TILES, P), "dst_rows": dst.reshape(TILES, P),
        "src_cols": src.reshape(TILES, P).T, "dst_cols": dst.reshape(TILES, P).T,
        "e32_t": e32.T,
        "e32_cols": e32.reshape(TILES, P, NB).transpose(1, 0, 2),
        "e4_cols": padded(a["edge_attr_4"], EP).reshape(TILES, P, 4).transpose(1, 0, 2),
        "e10_t": padded(a["edge_attr_10"], EP).T,
        "a_cols": padded(a["node_vec1"], NODE_ROWS).reshape(BLOCKS, P).T,
        "w1": w1.reshape(S, 512), "w2": w2.reshape(V, 512), "w3": w3.reshape(S, 256), "w4": w4.reshape(V, 256),
        "wm_t": np.concatenate([parts_first(a["L0_gnn_Wm"]), a["L0_gnn_bm"].reshape(1, D)]).T,
        "wu_top": parts_first(a["L0_gnn_Wu"][:D]), "wu_bot": a["L0_gnn_Wu"][D:], "bu": a["L0_gnn_bu"].reshape(1, D),
        "w_node0": np.concatenate([a["L1_gnn_W_l1_0"], a["L1_gnn_W_si0"]], axis=1),
        "w_node1": np.concatenate([a["L1_gnn_W_l1_1"], a["L1_gnn_W_si1"]], axis=1),
        "w_out0": np.concatenate([a["L1_gnn_W_l2_00"], a["L1_gnn_W_l2_10"]]),
        "w_out1": np.concatenate([a["L1_gnn_W_l2_01"], a["L1_gnn_W_l2_11"]]),
        "fc1": a["L1_gnn_W_fc1"], "fc2": a["L1_gnn_W_fc2"],
    }
    arrays = {f"in_{k}": np.ascontiguousarray(w) for k, w in arrays.items()}
    nc = bacc.Bacc("TRN2", target_bir_lowering=False, num_devices=1)
    t = {k[3:]: nc.dram_tensor(k, w.shape, mybir.dt.from_np(w.dtype), kind="ExternalInput").ap() for k, w in arrays.items()}
    out = nc.dram_tensor("out_0", (NODES, D), F32, kind="ExternalOutput").ap()
    build_program(nc, t, out)
    return run_bass_kernel_spmd(nc, [arrays], core_ids=[0]).results[0]["out_0"]
```

```python
import math
from contextlib import ExitStack

import concourse.bass as bass
from concourse import mybir

F32 = mybir.dt.float32
I32 = mybir.dt.int32
BF16 = mybir.dt.bfloat16
ALU = mybir.AluOpType
ACT = mybir.ActivationFunctionType
AX = mybir.AxisListType

P = 128
NODES, EDGES = 6250, 100000
BLOCKS = 50
NODE_ROWS = BLOCKS * P
TILES = 784
PAD_NODE = NODES
CHUNK = 16
CHUNKS = TILES // CHUNK
WINDOW = 4
SPAN = 40
FAST_BLOCKS = -(-NODES // P)
TPB = 18
BLOCK_EDGES = TPB * P
TABLE_ROWS = NODE_ROWS + P
DUMP = NODE_ROWS
S, V, D = 64, 32, 160
NB = 32
GW = NB * D
MW = D + 1
UW = 384
COPIES = 4
EPS = 1e-5

K1 = 1.0 / math.sqrt(S * 8) / math.sqrt(2.0)
K2 = 1.0 / (math.sqrt(3.0) * math.sqrt(V * 8)) / math.sqrt(2.0)
K3 = 1.0 / math.sqrt(S * 8) / math.sqrt(2.0)
K4 = 1.0 / math.sqrt(V * 8) / math.sqrt(2.0)


class Chain:

    def __init__(self, eng, sem, base=0):
        self.eng, self.sem, self.base, self.n = eng, sem, base, 0

    def step(self, ins):
        self.n += 1
        return ins.then_inc(self.sem, 1)

    def settle(self):
        self.eng.wait_ge(self.sem, self.base + self.n)

    def link(self, ins):
        self.step(ins)
        self.settle()


def skewed(eng, tiles, unroll, *stages, at_body=None):
    most = max(lead for lead, _ in stages)
    loops = (tiles - max(most, 1)) // unroll
    for step in range(-most, 0):
        for lead, fn in stages:
            if step + lead >= 0:
                fn((step + lead) // unroll, (step + lead) % unroll)
    with eng.Fori(0, loops) as i:
        if at_body:
            at_body(i)
        for k in range(unroll):
            for lead, fn in stages:
                fn(i + (k + lead) // unroll, (k + lead) % unroll)
    for step in range(loops * unroll, tiles):
        if at_body and step % unroll == 0:
            at_body(step // unroll)
        for lead, fn in stages:
            if step + lead < tiles:
                fn((step + lead) // unroll, (step + lead) % unroll)


def choose(eng, order, fast, slow):
    odd = eng.value_load(order[0:1, 0:1], min_val=0, max_val=1)
    with eng.If(odd == 0):
        fast(eng)
    with eng.Else():
        slow(eng)


class Shared:
    pass


def build_program(nc, t, out):
    ctx = ExitStack()
    with ctx:
        def sb(name, shape, dt=F32, where=ctx):
            return where.enter_context(nc.sbuf_tensor(name, shape, dt))

        def ps(name, shape, where=ctx):
            return where.enter_context(nc.psum_tensor(name, shape, F32))

        def sem(name, where=ctx):
            return where.enter_context(nc.semaphore(name))

        def dram(name, shape):
            return nc.dram_tensor(name, shape, F32).ap()

        v = Shared()
        v.sb, v.ps, v.sem = sb, ps, sem
        v.products = dram("products", (NODE_ROWS, GW))
        v.sums0 = [dram(f"sums0_{r}", (TABLE_ROWS, MW)) for r in range(COPIES)]
        v.sums1 = [dram(f"sums1_{r}", (TABLE_ROWS, UW)) for r in range(COPIES)]
        v.y_table = dram("y_table", (NODE_ROWS, D))
        v.block_start = nc.dram_tensor("block_start", (FAST_BLOCKS, 1), I32).ap()

        v.chunk_group = nc.dram_tensor("chunk_group", (CHUNKS + 1, 1), I32).ap()
        v.tile_slot = nc.dram_tensor("tile_slot", (1, TILES + 4), I32).ap()
        v.split_rows = nc.dram_tensor("split_rows", (2, 2, TILES * P), BF16).ap()
        v.tile_base = dram("tile_base", (CHUNKS, CHUNK))

        v.ident = sb("ident", [P, P])
        v.ones = sb("ones", [P, P])
        v.ones2 = sb("ones2", [2, P], BF16)
        v.dump_before = sb("dump_before", [P, P])
        v.w1 = sb("w1", [S, 512])
        v.w2 = sb("w2", [96, 512])
        v.w3 = sb("w3", [S, 256])
        v.w4 = sb("w4", [96, 256])
        v.wm_t = sb("wm_t", [P, 2, MW])
        v.wu_bot = sb("wu_bot", [P, 2, D])
        v.wu_s = sb("wu_s", [S, D])
        v.wu_v = sb("wu_v", [96, D])
        v.bu = sb("bu", [1, D])
        v.wmu_a = sb("wmu_a", [P, D])
        v.wmu_b = sb("wmu_b", [33, D])
        v.w_node0 = sb("w_node0", [S, 128])
        v.w_node1 = sb("w_node1", [V, 64])
        v.w_out0 = sb("w_out0", [96, S])
        v.w_out1 = sb("w_out1", [96, V])
        v.fc1 = sb("fc1", [10, 100])
        v.fc2 = sb("fc2", [100, 192])
        v.minus_src = sb("minus_src", [P, TILES])
        v.src_col = sb("src_col", [P, TILES])
        v.dst_col = sb("dst_col", [P, TILES])
        v.src_int = sb("src_int", [P, TILES], I32)
        v.dst_int = sb("dst_int", [P, TILES], I32)
        v.window_node = sb("window_node", [P, WINDOW, TILES])
        v.scattered_order = sb("scattered_order", [1, 1], I32)
        v.unblocked_order = sb("unblocked_order", [1, 1], I32)
        v.own = sb("own", [P, BLOCKS, D])
        v.moments = sb("moments", [P, BLOCKS, 2])
        v.count_row = sb("count_row", [P, P])
        v.block_base = sb("block_base", [P, FAST_BLOCKS])
        v.a_col = sb("a_col", [P, BLOCKS])

        setup_phase(nc, t, v)
        products_phase(nc, t, v)
        windows_phase(nc, t, v)
        layer0_edges(nc, t, v)
        layer0_nodes(nc, t, v)
        layer1_edges(nc, t, v)
        layer1_nodes(nc, t, v, out)


def setup_phase(nc, t, v):
    with ExitStack() as local:
        sb = lambda name, shape, dt=F32: v.sb(name, shape, dt, local)
        zeros = sb("zeros", [P, 51 * MW])
        psum = v.ps("setup_psum", [P, 2, 512], local)
        loaded = v.sem("setup_loaded", local)
        cleared = v.sem("setup_cleared", local)
        zeroed = v.sem("setup_zeroed", local)
        filled = v.sem("setup_filled", local)
        scaled = v.sem("setup_scaled", local)
        merged = v.sem("setup_merged", local)
        n_loads = [0]
        with nc.Block() as block:

            @block.sync
            def _(sp):
                def load(dst, src):
                    n_loads[0] += 1
                    sp.dma_start(dst, src).then_inc(loaded, 16)

                load(v.w1[:], t["w1"])
                load(v.w3[:], t["w3"])
                load(v.w_node0[:], t["w_node0"])
                load(v.w_node1[:], t["w_node1"])
                for i in range(3):
                    load(v.w2[32 * i:32 * i + 32, :], t["w2"])
                    load(v.w4[32 * i:32 * i + 32, :], t["w4"])
                load(v.wm_t[:, 0, :], t["wm_t"][0:P, :])
                load(v.wm_t[0:32, 1, :], t["wm_t"][P:D, :])
                load(v.wu_bot[:, 0, :], t["wu_bot"][0:P, :])
                load(v.wu_bot[0:32, 1, :], t["wu_bot"][P:D, :])
                load(v.wu_s[:], t["wu_top"][0:S, :])
                load(v.wu_v[:], t["wu_top"][S:D, :])
                load(v.bu[:], t["bu"])
                load(v.w_out0[:], t["w_out0"])
                load(v.w_out1[:], t["w_out1"])
                load(v.fc1[:], t["fc1"])
                load(v.fc2[:], t["fc2"])
                load(v.src_int[:], t["src_cols"])
                load(v.dst_int[:], t["dst_cols"])
                load(v.a_col[:], t["a_cols"])
                sp.wait_ge(zeroed, 1)
                for r in range(COPIES):
                    sp.dma_start(v.sums0[r].rearrange("(p a) d -> p (a d)", p=P), zeros[:]).then_inc(cleared, 16)
                sp.wait_ge(cleared, 16 * COPIES)

            @block.gpsimd
            def _(pool):
                pool.memset(v.ident[:], 0.0).then_inc(filled, 1)
                pool.memset(v.ones[:], 1.0).then_inc(filled, 1)
                pool.memset(v.ones2[:], 1.0)
                pool.iota(v.count_row[:], [[1, P]], base=0, channel_multiplier=0, allow_small_or_imprecise_dtypes=True)
                pool.iota(v.block_base[:], [[P, FAST_BLOCKS]], base=0, channel_multiplier=0, allow_small_or_imprecise_dtypes=True)
                pool.iota(v.dump_before[:], [[0, P]], base=DUMP, channel_multiplier=1,
                          allow_small_or_imprecise_dtypes=True).then_inc(filled, 1)
                pool.wait_ge(filled, 3)
                pool.affine_select(out=v.ident[:], in_=v.ident[:], compare_op=ALU.not_equal, fill=1.0,
                                   base=0, pattern=[[-1, P]], channel_multiplier=1).then_inc(filled, 1)
                pool.affine_select(out=v.dump_before[:], in_=v.dump_before[:], compare_op=ALU.is_gt, fill=0.0,
                                   base=0, pattern=[[-1, P]], channel_multiplier=1).then_inc(filled, 1)

            @block.vector
            def _(dve):
                dve.memset(zeros[:], 0.0).then_inc(zeroed, 1)
                dve.wait_ge(loaded, 16 * n_loads[0])
                dve.tensor_copy(v.src_col[:], v.src_int[:])
                dve.tensor_scalar(v.minus_src[:], v.src_int[:], -1.0, None, ALU.mult)
                dve.tensor_copy(v.dst_col[:], v.dst_int[:])
                for weight, k in ((v.w1, K1), (v.w2, K2), (v.w3, K3), (v.w4, K4),
                                (v.w_node0, 1.0 / math.sqrt(S)), (v.w_node1, 1.0 / math.sqrt(V)),
                                (v.w_out0, 0.125 / math.sqrt(96.0)), (v.w_out1, 0.125 / math.sqrt(96.0)),
                                (v.fc1, math.sqrt(2.0 / 10.0)), (v.fc2, 0.1)):
                    dve.tensor_scalar(weight[:], weight[:], k, None, ALU.mult).then_inc(scaled, 1)
                dve.wait_ge(scaled, 10)
                dve.tensor_scalar(v.fc2[:, 160:192], v.fc2[:, 160:192], 1.0 / math.sqrt(3.0), None, ALU.mult)
                dve.wait_ge(merged, 1)
                dve.tensor_copy(v.wmu_a[:], psum[:, 0, 0:D])
                dve.tensor_copy(v.wmu_b[:], psum[0:33, 1, 0:D])

            @block.tensor
            def _(pe):
                pe.wait_ge(loaded, 16 * n_loads[0])
                for m, (m0, m1) in enumerate(((0, P), (P, MW))):
                    pe.matmul(psum[0:m1 - m0, m, 0:D], v.wm_t[:, 0, m0:m1], v.wu_bot[:, 0, :], start=True, stop=False)
                    last = pe.matmul(psum[0:m1 - m0, m, 0:D], v.wm_t[0:32, 1, m0:m1], v.wu_bot[0:32, 1, :],
                                     start=False, stop=True)
                last.then_inc(merged, 1)


def products_phase(nc, t, v):
    with ExitStack() as local:
        xs = [v.sb(f"xs{k}", [S, P], F32, local) for k in range(2)]
        xv = [v.sb(f"xv{k}", [96, P], F32, local) for k in range(2)]
        g = [v.sb(f"g{k}", [P, NB, D], F32, local) for k in range(2)]
        bank = [v.ps(f"g_bank{k}", [P, 512], local) for k in range(8)]
        x_in = [v.sem(f"x_in{k}", local) for k in range(2)]
        banks_full = v.sem("banks_full", local)
        act_done = v.sem("act_done", local)
        dve_done = v.sem("dve_done", local)
        blank = v.sem("blank", local)
        g_free = v.sem("g_free", local)
        g_out = [v.sem(f"g_out{k}", local) for k in range(2)]
        with nc.Block() as block:

            @block.gpsimd
            def _(pool):
                for k in range(2):
                    pool.memset(g[k][:], 0.0).then_inc(blank, 1)

            @block.sync
            def _(sp):
                sp.wait_ge(blank, 2)
                sp.sem_inc(g_free, 2)

                def load(i, k):
                    b = i * 2 + k
                    sp.wait_ge(banks_full, b * 2 + 2)
                    sp.dma_start(xs[k][:], t["x_t"][0:S, bass.ds(b * P, P)]).then_inc(x_in[k], 16)
                    sp.dma_start(xv[k][:], t["x_t"][S:D, bass.ds(b * P, P)]).then_inc(x_in[k], 16)

                def store(i, k):
                    b = i * 2 + k
                    sp.wait_ge(act_done, b * 2 + 4)
                    sp.wait_ge(dve_done, b * 2 + 4)
                    sp.dma_start(v.products[bass.ds(b * P, P), :], g[k][:].rearrange("p b d -> p (b d)")).then_inc(g_out[k], 16)

                def landed(i, k):
                    sp.wait_ge(g_out[k], i * 16 + 16)
                    sp.sem_inc(g_free, 1)

                skewed(sp, BLOCKS, 2, (3, load), (1, store), (0, landed))

            @block.tensor
            def _(pe):
                pe.sem_inc(banks_full, 4)
                with pe.Fori(0, BLOCKS // 2) as i:
                    for k in range(2):
                        b = i * 2 + k
                        pe.wait_ge(x_in[k], i * 32 + 32)
                        pe.wait_ge(act_done, b * 2 + 1)
                        pe.wait_ge(dve_done, b * 2 + 1)
                        pe.matmul(bank[0][:], xs[k][:], v.w1[:], start=True, stop=True)
                        for c in range(3):
                            last = pe.matmul(bank[1 + c][:], xv[k][32 * c:32 * c + 32, :], v.w2[32 * c:32 * c + 32, :], start=True, stop=True)
                        last.then_inc(banks_full, 1)
                        pe.wait_ge(act_done, b * 2 + 2)
                        pe.wait_ge(dve_done, b * 2 + 2)
                        for c in range(3):
                            pe.matmul(bank[4 + c][:, 0:256], xv[k][32 * c:32 * c + 32, :], v.w4[32 * c:32 * c + 32, :], start=True, stop=True)
                        pe.matmul(bank[7][:, 0:256], xs[k][:], v.w3[:], start=True, stop=True).then_inc(banks_full, 1)

            def place_scalars(copy, q, k):
                return copy(g[k][:, 8 * q:8 * q + 8, 0:S], bank[q][:].rearrange("p (b c) -> p b c", c=S))

            def place_component(copy, c, k):
                return copy(g[k][:, 0:8, S + 32 * c:S + 32 * c + 32], bank[4 + c][:, 0:256].rearrange("p (b c) -> p b c", c=V))

            @block.scalar
            def _(act):
                act.sem_inc(act_done, 2)
                with act.Fori(0, BLOCKS // 2) as i:
                    for k in range(2):
                        b = i * 2 + k
                        act.wait_ge(g_free, b + 1)
                        act.wait_ge(banks_full, b * 2 + 5)
                        place_scalars(act.copy, 0, k)
                        place_scalars(act.copy, 1, k).then_inc(act_done, 1)
                        act.wait_ge(banks_full, b * 2 + 6)
                        place_component(act.copy, 0, k)
                        place_component(act.copy, 1, k).then_inc(act_done, 1)

            @block.vector
            def _(dve):
                dve.sem_inc(dve_done, 2)
                with dve.Fori(0, BLOCKS // 2) as i:
                    for k in range(2):
                        b = i * 2 + k
                        dve.wait_ge(g_free, b + 1)
                        dve.wait_ge(banks_full, b * 2 + 5)
                        place_scalars(dve.tensor_copy, 2, k)
                        place_scalars(dve.tensor_copy, 3, k).then_inc(dve_done, 1)
                        dve.wait_ge(banks_full, b * 2 + 6)
                        place_component(dve.tensor_copy, 2, k)
                        for c in range(3):
                            last = dve.tensor_copy(g[k][:, 8 + 8 * c:16 + 8 * c, S + 32 * c:S + 32 * c + 32],
                                                   bank[7][:, 0:256].rearrange("p (b c) -> p b c", c=V))
                        last.then_inc(dve_done, 1)


def windows_phase(nc, t, v):
    with ExitStack() as local:
        grid = v.sb("grid", [CHUNKS, CHUNK, P], I32, local)
        source_grid = v.sb("source_grid", [CHUNKS, CHUNK * P], I32, local)
        part_int = v.sb("part_int", [CHUNKS, 4, CHUNK * P], I32, local)
        part = v.sb("part", [CHUNKS, 4, CHUNK * P], BF16, local)
        next_first = v.sb("next_first", [CHUNKS, 1], I32, local)
        falls = v.sb("falls", [CHUNKS, CHUNK * P], F32, local)
        fall = v.sb("fall", [CHUNKS, 4], F32, local)
        below = v.sb("below", [P, FAST_BLOCKS + 1], F32, local)
        in_block = v.sb("in_block", [P, FAST_BLOCKS], F32, local)
        junk = v.sb("junk", [P, TILES], F32, local)
        start_int = v.sb("start_int", [FAST_BLOCKS, 1], I32, local)
        excess = v.sb("excess", [FAST_BLOCKS, 2], F32, local)
        below_ready = v.sem("below_ready", local)
        starts_summed = v.sem("starts_summed", local)
        excess_ready = v.sem("excess_ready", local)
        starts_out = v.sem("starts_out", local)
        start_ready = v.sem("start_ready", local)
        order_summed = v.sem("order_summed", local)
        zero_slots = v.sb("zero_slots", [1, 4], I32, local)
        parts_ready = v.sem("parts_ready", local)
        small = v.sb("small", [CHUNKS, 8, CHUNK], F32, local)
        least, most, base, over, rel = (small[:, n, :] for n in range(5))
        ints = v.sb("ints", [CHUNKS, 3, CHUNK], I32, local)
        chunk = v.sb("chunk", [CHUNKS, 4], F32, local)
        chunk_int = v.sb("chunk_int", [CHUNKS, 2], I32, local)
        zero_int = v.sb("zero_int", [1, 1], I32, local)
        odd = v.sb("odd", [CHUNKS, 1], I32, local)
        quarter = v.sb("quarter", [P, 1], I32, local)
        quarter_f = v.sb("quarter_f", [P, 1], F32, local)
        base_all = v.sb("base_all", [P, TILES], F32, local)
        violations = v.ps("violations", [P, 512], local)
        grid_in = v.sem("grid_in", local)
        iotas = v.sem("iotas", local)
        chain_sem = v.sem("w_chain", local)
        tables_ready = v.sem("tables_ready", local)
        tables_out = v.sem("tables_out", local)
        counted = v.sem("counted", local)
        violations_summed = v.sem("violations_summed", local)
        with nc.Block() as block:

            @block.sync
            def _(sp):
                sp.dma_start(grid[:], t["dst_rows"].rearrange("(c j) e -> c j e", j=CHUNK)).then_inc(grid_in, 16)
                sp.dma_start(next_first[:], t["dst_flat"][CHUNK * P:CHUNK * P * (CHUNKS + 1), :].rearrange("(c e) a -> c (e a)", c=CHUNKS)[:, 0:1], allow_slow_non_contiguous=True).then_inc(grid_in, 16)
                sp.dma_start(source_grid[:], t["src_rows"].rearrange("(c j) e -> c (j e)", j=CHUNK)).then_inc(grid_in, 16)
                sp.wait_ge(tables_ready, 1)
                sp.dma_start(v.chunk_group[0:CHUNKS, :], chunk_int[:, 0:1]).then_inc(tables_out, 16)
                sp.dma_start(v.chunk_group[CHUNKS:, :], zero_int[:]).then_inc(tables_out, 16)
                sp.dma_start(v.tile_slot[:, 3:3 + TILES].rearrange("a (c j) -> (a c) j", j=CHUNK), ints[:, 2, :]).then_inc(tables_out, 16)
                sp.dma_start(v.tile_slot[:, 0:3], zero_slots[:, 0:3]).then_inc(tables_out, 16)
                sp.dma_start(v.tile_slot[:, 3 + TILES:], zero_slots[:, 3:4]).then_inc(tables_out, 16)
                sp.dma_start(v.tile_base, base).then_inc(tables_out, 16)
                sp.wait_ge(parts_ready, 4)
                for n in range(4):
                    sp.dma_start(v.split_rows[n // 2, n % 2, :].rearrange("(c e) -> c e", c=CHUNKS), part[:, n, :]).then_inc(tables_out, 16)
                sp.wait_ge(tables_out, 160)
                sp.dma_start(base_all[:], v.tile_base.rearrange("(a c) j -> a (c j)", a=1).broadcast_to([P, TILES])).then_inc(tables_out, 16)
                sp.wait_ge(start_ready, 1)
                sp.dma_start(v.block_start, start_int[:]).then_inc(starts_out, 16)
                sp.wait_ge(starts_out, 16)

            @block.gpsimd
            def _(pool):
                pool.iota(odd[:], [[0, 1]], base=0, channel_multiplier=1).then_inc(iotas, 1)
                pool.iota(quarter[:], [[0, 1]], base=0, channel_multiplier=1).then_inc(iotas, 1)

            @block.vector
            def _(dve):
                chain = Chain(dve, chain_sem)
                chain.step(dve.memset(zero_int[:], 0))
                chain.step(dve.memset(zero_slots[:], 0))
                dve.wait_ge(grid_in, 48)
                nodes = grid[:].rearrange("c j e -> c (j e)")
                for n, (ids, mask) in enumerate(((nodes, -64), (source_grid[:], -64), (nodes, 63), (source_grid[:], 63))):
                    chain.step(dve.tensor_scalar(part_int[:, n, :], ids, mask, None, ALU.bitwise_and))
                chain.settle()
                for n in range(4):
                    dve.tensor_copy(part[:, n, :], part_int[:, n, :]).then_inc(parts_ready, 1)
                chain.step(dve.tensor_reduce(least, grid[:], AX.X, ALU.min))
                chain.link(dve.tensor_reduce(most, grid[:], AX.X, ALU.max))
                chain.link(dve.tensor_copy(ints[:, 0, :], least))
                chain.link(dve.tensor_scalar(ints[:, 1, :], ints[:, 0, :], -4, None, ALU.bitwise_and))
                chain.link(dve.tensor_copy(base, ints[:, 1, :]))
                chain.link(dve.tensor_reduce(chunk[:, 0:1], base, AX.X, ALU.min))
                chain.link(dve.tensor_scalar(chunk[:, 1:2], chunk[:, 0:1], float(NODE_ROWS - 4 * SPAN), None, ALU.min))
                chain.step(dve.tensor_scalar(chunk_int[:, 0:1], chunk[:, 1:2], 0.25, None, ALU.mult))
                chain.link(dve.tensor_scalar(rel, base, chunk[:, 1:2], 0.25, ALU.subtract, ALU.mult))
                chain.step(dve.tensor_scalar(small[:, 5, :], rel, float(SPAN - WINDOW), 0.0, ALU.subtract, ALU.max))
                chain.link(dve.tensor_tensor(over, most, base, ALU.subtract))
                chain.link(dve.tensor_scalar(small[:, 6, :], over, float(4 * WINDOW - 1), 0.0, ALU.subtract, ALU.max))
                chain.link(dve.tensor_tensor(small[:, 7, :], small[:, 5, :], small[:, 6, :], ALU.add))
                chain.step(dve.tensor_reduce(chunk[:, 2:3], small[:, 7, :], AX.X, ALU.add))
                dve.wait_ge(iotas, 2)
                chain.link(dve.tensor_scalar(chunk_int[:, 1:2], odd[:], 1, None, ALU.bitwise_and))
                dve.sem_inc(counted, 1)
                chain.step(dve.tensor_scalar(chunk[:, 3:4], chunk_int[:, 1:2], float(SPAN), None, ALU.mult))
                chain.link(dve.tensor_scalar(small[:, 5, :], rel, float(SPAN - WINDOW), None, ALU.min))
                dve.tensor_scalar(ints[:, 2, :], small[:, 5, :], chunk[:, 3:4], None, ALU.add).then_inc(tables_ready, 1)
                chain.link(dve.tensor_scalar(quarter[:], quarter[:], 5, None, ALU.logical_shift_right))
                chain.link(dve.tensor_copy(quarter_f[:], quarter[:]))
                dve.wait_ge(tables_out, 176)
                for j in range(WINDOW):
                    dve.tensor_scalar(v.window_node[:, j, :], base_all[:], quarter_f[:], float(4 * j), ALU.add, ALU.add)
                chain.step(dve.tensor_tensor(falls[:, 0:CHUNK * P - 1], nodes[:, 0:CHUNK * P - 1], nodes[:, 1:], ALU.is_gt))
                chain.link(dve.tensor_tensor(fall[:, 0:1], nodes[:, CHUNK * P - 1:], next_first[:], ALU.is_gt))
                chain.link(dve.tensor_reduce(fall[:, 1:2], falls[:, 0:CHUNK * P - 1], AX.X, ALU.max))
                chain.step(dve.tensor_tensor(fall[:, 2:3], fall[:, 0:1], fall[:, 1:2], ALU.add))
                chain.step(dve.memset(below[:, FAST_BLOCKS:], float(TILES)))
                for b in range(FAST_BLOCKS):
                    chain.link(dve.tensor_scalar(junk[:], v.dst_col[:], float(P * b), None, ALU.is_lt, ALU.add, accum_out=below[:, b:b + 1]))
                chain.settle()
                dve.tensor_tensor(in_block[:], below[:, 1:], below[:, 0:FAST_BLOCKS], ALU.subtract).then_inc(below_ready, 1)
                dve.wait_ge(starts_summed, 1)
                dve.tensor_copy(start_int[:], violations[0:FAST_BLOCKS, 4:5]).then_inc(start_ready, 1)
                dve.tensor_scalar(excess[:, 0:1], violations[0:FAST_BLOCKS, 5:6], float(BLOCK_EDGES), 0.0, ALU.subtract, ALU.max).then_inc(excess_ready, 1)
                dve.wait_ge(order_summed, 1)
                dve.tensor_scalar(v.unblocked_order[:], violations[0:1, 8:9], 0.0, None, ALU.is_gt)
                dve.wait_ge(violations_summed, 1)
                dve.tensor_scalar(v.scattered_order[:], violations[0:1, 0:1], 0.0, None, ALU.is_gt)

            @block.tensor
            def _(pe):
                pe.wait_ge(counted, 1)
                pe.matmul(violations[0:1, 0:1], chunk[:, 2:3], v.ones[0:CHUNKS, 0:1], start=True, stop=True).then_inc(violations_summed, 1)
                pe.wait_ge(below_ready, 1)
                pe.matmul(violations[0:FAST_BLOCKS, 4:5], below[:, 0:FAST_BLOCKS], v.ones[:, 0:1], start=True, stop=True)
                pe.matmul(violations[0:FAST_BLOCKS, 5:6], in_block[:], v.ones[:, 0:1], start=True, stop=True).then_inc(starts_summed, 1)
                pe.wait_ge(excess_ready, 1)
                pe.matmul(violations[0:1, 8:9], excess[:, 0:1], v.ones[0:FAST_BLOCKS, 0:1], start=True, stop=False)
                pe.matmul(violations[0:1, 8:9], fall[:, 2:3], v.ones[0:CHUNKS, 0:1], start=False, stop=True).then_inc(order_summed, 1)


def layer0_edges(nc, t, v):
    with ExitStack() as local:
        U = COPIES
        big = v.sb("big", [P, 2 * SPAN, D], F32, local)
        windows = big
        rows = [big[:, NB * k:NB * k + NB, :] for k in range(2)]
        features = [v.sb(f"features{h}", [P, 4, P], F32, local) for h in range(4)]
        id_rows = [v.sb(f"id_rows{h}", [2, 2, 4 * P], BF16, local) for h in range(4)]
        spread = v.sb("spread", [P, 4, WINDOW, P], F32, local)
        e = v.sb("e", [P, U, NB], F32, local)
        targets = v.sb("targets", [P, U, P], I32, local)
        same = v.sb("same", [P, 8, P], F32, local)
        apart = v.sb("apart", [P, U, P], F32, local)
        scratch = v.sb("scratch", [P, U, P], F32, local)
        dup = v.sb("dup", [P, U], F32, local)
        msg = v.sb("msg", [P, U, MW], F32, local)
        total = v.sb("total", [P, U, MW], F32, local)
        source_idx = [v.sb(f"source_idx{k}", [P, 1], I32, local) for k in range(U)]
        target_idx = [v.sb(f"target_idx{k}", [P, 1], I32, local) for k in range(8)]
        summed = [v.ps(f"summed{k}", [P, 512], local) for k in range(U)]
        p_msg, p_sum = summed[0:2], summed[2:4]
        p_node = [v.ps(f"p_node{h}", [P, 4, P], local) for h in range(2)]
        p_target = [v.ps(f"p_target{h}", [P, 4, P], local) for h in range(2)]
        ids_spread = v.sem("ids_spread", local)
        chunk_landed = v.sem("chunk_landed", local)
        chunk_ready = v.sem("chunk_ready", local)
        dve_steps = v.sem("dve_steps", local)
        sames = v.sem("sames", local)
        built = v.sem("built", local)
        expanded = v.sem("expanded", local)
        copied = v.sem("copied", local)
        f_summed = v.sem("f_summed", local)
        f_totals = v.sem("f_totals", local)
        f_done = v.sem("f_done", local)
        edges_in = [v.sem(f"edges_in{k}", local) for k in range(U)]
        rows_in = [v.sem(f"rows_in{k}", local) for k in range(U)]
        scattered = [v.sem(f"scattered{k}", local) for k in range(U)]
        idx_ready = v.sem("idx_ready", local)
        prepared = v.sem("prepared", local)
        messages = v.sem("messages", local)
        sums_ready = v.sem("sums_ready", local)
        totals = v.sem("totals", local)
        scatter_done = v.sem("scatter_done", local)
        passed = v.sem("passed", local)
        ones_set = v.sem("ones_set", local)
        STEPS = 5
        with nc.Block() as block:

            def fast_sync(sp):
                def load_chunk(c, free=None):
                    group = sp.value_load(v.chunk_group[bass.ds(c, 1), :], min_val=0, max_val=NODE_ROWS // 4 - SPAN)
                    if free is not None:
                        sp.wait_ge(expanded, free)
                    half = (c % 2) * SPAN
                    sp.dma_start(windows[:, bass.ds(half, SPAN), :],
                                 v.products.rearrange("(g n) (b c) -> (n b) g c", n=4, b=NB)[:, bass.ds(group, SPAN), :]).then_inc(chunk_landed, 16)

                def load_batch(i, h):
                    sp.wait_ge(built, i * CHUNK + 4 * h + 4)
                    edges = bass.ds(i * (CHUNK * P) + h * (4 * P), 4 * P)
                    sp.dma_start(id_rows[h][:], v.split_rows[:, :, edges]).then_inc(edges_in[h], 16)
                    for n in range(4):
                        sp.dma_start(features[h][32 * n:32 * n + 32, :, :].rearrange("p a b -> p (a b)"), t["e32_t"][:, edges]).then_inc(edges_in[h], 16)

                load_chunk(0)
                sp.wait_ge(chunk_landed, 16)
                sp.sem_inc(chunk_ready, 1)
                for h in range(2):
                    load_batch(0, h)
                with sp.Fori(0, CHUNKS - 1) as c:
                    for h in range(2, 4):
                        load_batch(c, h)
                    load_chunk(c + 1, c * CHUNK + CHUNK)
                    for h in range(2):
                        load_batch(c + 1, h)
                    sp.wait_ge(chunk_landed, c * 16 + 32)
                    sp.sem_inc(chunk_ready, 1)
                for h in range(2, 4):
                    load_batch(CHUNKS - 1, h)

            def slow_sync(sp):
                with sp.Fori(0, TILES // U) as i:
                    for k in range(U):
                        tile = i * U + k
                        sp.wait_ge(sums_ready, tile + 1)
                        sp.dma_start(e[:, k, :], t["e32_cols"][:, bass.ds(tile, 1), :].rearrange("p a b -> p (a b)")).then_inc(edges_in[k], 16)
                        sp.dma_start(targets[:, k, :], t["src_rows"][bass.ds(tile, 1), :].broadcast_to([P, P])).then_inc(edges_in[k], 16)

            @block.sync
            def _(sp):
                choose(sp, v.scattered_order, fast_sync, slow_sync)

            def fast_gpsimd(pool):
                pool.sem_inc(f_done, 8)

                def scatter(i, k):
                    pool.wait_ge(f_totals, i * CHUNK + k + 3)
                    pool.wait_ge(built, i * CHUNK + k + 17)
                    pool.sem_inc(passed, 1)
                    pool.indirect_dma_start(v.sums0[k % 4][:, :], bass.IndirectOffsetOnAxis(target_idx[k % 8][:, 0:1], 0),
                                            total[:, k % 4, :], None, compute_op=ALU.add).then_inc(scattered[k % 4], 16)

                def landed(i, k):
                    pool.wait_ge(scattered[k % 4], i * 64 + 16 * (k // 4) + 16)
                    pool.sem_inc(f_done, 1)

                skewed(pool, TILES, CHUNK, (3, scatter), (0, landed))

            def slow_gpsimd(pool):
                pool.sem_inc(scatter_done, U)

                def gather(i, k):
                    tile = i * U + k
                    pool.wait_ge(messages, tile + 1)
                    pool.wait_ge(idx_ready, tile + 1)
                    pool.sem_inc(passed, 1)
                    pool.indirect_dma_start(rows[k % 2].rearrange("p b d -> p (b d)"), None, v.products[:, :],
                                            bass.IndirectOffsetOnAxis(source_idx[k][:, 0:1], 0)).then_inc(rows_in[k], 16)

                def scatter(i, k):
                    tile = i * U + k
                    pool.wait_ge(totals, tile + 1)
                    pool.sem_inc(passed, 1)
                    pool.indirect_dma_start(v.sums0[k][:, :], bass.IndirectOffsetOnAxis(target_idx[k][:, 0:1], 0),
                                            total[:, k, :], None, compute_op=ALU.add).then_inc(scattered[k], 16)
                    pool.wait_ge(scattered[k], i * 16 + 16)
                    pool.sem_inc(scatter_done, 1)

                with pool.Fori(0, TILES // U) as i:
                    for k in range(U):
                        gather(i, k)
                        if k:
                            scatter(i, k - 1)
                    scatter(i, U - 1)

            @block.gpsimd
            def _(pool):
                choose(pool, v.scattered_order, fast_gpsimd, slow_gpsimd)

            def fast_vector(dve):
                STEPS = 1
                dve.memset(msg[:, :, D:MW], 1.0).then_inc(ones_set, 1)
                dve.wait_ge(ones_set, 1)
                dve.sem_inc(built, 16)

                def build(i, k):
                    tile, h, q = i * CHUNK + k, k // 4, k % 4
                    chain = Chain(dve, dve_steps, tile * STEPS)

                    def spread_window(j):
                        return dve.scalar_tensor_tensor(spread[:, q, j, :], p_node[h % 2][:, q, :], v.window_node[:, j, bass.ds(tile, 1)],
                                                        features[h][:, q, :], ALU.is_equal, ALU.mult)

                    dve.wait_ge(edges_in[h], i * 80 + 80)
                    dve.wait_ge(ids_spread, i * 4 + h + 1)
                    dve.wait_ge(expanded, tile + 13)
                    spread_window(0)
                    dve.wait_ge(sames, tile * 2 + 2)
                    spread_window(1)
                    chain.step(dve.tensor_tensor_reduce(out=scratch[:, q, :], in0=same[:, k % 8, :], in1=v.dump_before[:], scale=1.0, scalar=0.0,
                                                        op0=ALU.mult, op1=ALU.max, accum_out=dup[:, q:q + 1]))
                    spread_window(2)
                    spread_window(3)
                    dve.wait_ge(f_done, tile + 1)
                    chain.settle()
                    dve.tensor_tensor(target_idx[k % 8][:], dup[:, q:q + 1], v.src_col[:, bass.ds(tile, 1)], ALU.max).then_inc(built, 1)

                skewed(dve, TILES, CHUNK, (0, build))

            def slow_vector(dve):
                dve.memset(msg[:, :, D:MW], 1.0).then_inc(ones_set, 1)
                dve.wait_ge(ones_set, 1)
                dve.sem_inc(messages, 2)
                with dve.Fori(0, TILES // U) as i:
                    for k in range(U):
                        tile = i * U + k
                        chain = Chain(dve, prepared, tile * STEPS)
                        dve.wait_ge(scatter_done, tile + 1)
                        dve.tensor_copy(source_idx[k][:], v.dst_int[:, bass.ds(tile, 1)]).then_inc(idx_ready, 1)
                        dve.wait_ge(edges_in[k], i * 32 + 32)
                        chain.link(dve.tensor_scalar(same[:, k, :], targets[:, k, :], v.src_col[:, bass.ds(tile, 1)], None, ALU.is_equal))
                        chain.link(dve.tensor_tensor(scratch[:, k, :], same[:, k, :], v.dump_before[:], ALU.mult))
                        chain.link(dve.tensor_reduce(dup[:, k:k + 1], scratch[:, k, :], AX.X, ALU.max))
                        chain.step(dve.tensor_tensor(target_idx[k][:], dup[:, k:k + 1], v.src_col[:, bass.ds(tile, 1)], ALU.max))
                        dve.wait_ge(rows_in[k], i * 16 + 16)
                        chain.link(dve.tensor_tensor(rows[k % 2], rows[k % 2],
                                                     e[:, k, :].unsqueeze(2).broadcast_to([P, NB, D]), ALU.mult))
                        assert chain.n == STEPS
                        dve.tensor_reduce(msg[:, k, 0:D], rows[k % 2].rearrange("p b c -> p c b"), AX.X, ALU.add).then_inc(messages, 1)

            @block.vector
            def _(dve):
                choose(dve, v.scattered_order, fast_vector, slow_vector)

            def fast_tensor(pe):
                slots = [0] * CHUNK

                def load_slots(i):
                    _, slots[:] = nc.values_load_multi_w_load_instructions(
                        v.tile_slot[:, bass.ds(i * CHUNK + 4, CHUNK)], engines=(mybir.EngineType.PE,), min_val=0, max_val=2 * SPAN - WINDOW)

                def spread_ids(i, k):
                    if k % 4:
                        return
                    h = k // 4
                    pe.wait_ge(edges_in[h], i * 80 + 80)
                    pe.wait_ge(built, i * CHUNK + 4 * h + 12)
                    pe.matmul(p_node[h % 2][:].rearrange("p a b -> p (a b)"), v.ones2[:], id_rows[h][:, 0, :], start=True, stop=True)
                    pe.matmul(p_target[h % 2][:].rearrange("p a b -> p (a b)"), v.ones2[:], id_rows[h][:, 1, :], start=True, stop=True).then_inc(ids_spread, 1)

                slots[CHUNK - 1] = pe.value_load(v.tile_slot[:, 3:4], min_val=0, max_val=2 * SPAN - WINDOW)
                pe.sem_inc(expanded, CHUNK)
                pe.sem_inc(f_summed, 8)

                def expand(i, k):
                    tile, q = i * CHUNK + k, k % 4
                    slot = slots[(k - 1) % CHUNK]
                    pe.wait_ge(chunk_ready, i + 1)
                    pe.wait_ge(built, tile + 17)
                    pe.wait_ge(copied, tile + 1)
                    for j in range(WINDOW):
                        last = pe.matmul(p_msg[q % 2][:, 0:D], spread[:, q, j, :], windows[:, bass.ds(slot + j, 1), :].rearrange("p a b -> p (a b)"),
                                         start=(j == 0), stop=(j == WINDOW - 1))
                    last.then_inc(expanded, 1)

                def add_up(i, k):
                    tile, q = i * CHUNK + k, k % 4
                    pe.wait_ge(copied, tile + 3)
                    pe.wait_ge(f_totals, tile + 1)
                    pe.matmul(p_sum[q % 2][:, 0:MW], same[:, k % 8, :], msg[:, q, :], start=True, stop=True).then_inc(f_summed, 1)

                skewed(pe, TILES, CHUNK, (6, spread_ids), (1, expand), (0, add_up), at_body=load_slots)

            def slow_tensor(pe):
                pe.sem_inc(sums_ready, U)
                with pe.Fori(0, TILES // U) as i:
                    for k in range(U):
                        tile = i * U + k
                        pe.wait_ge(messages, tile + 3)
                        pe.matmul(summed[k][:, 0:MW], same[:, k, :], msg[:, k, :], start=True, stop=True).then_inc(sums_ready, 1)

            @block.tensor
            def _(pe):
                choose(pe, v.scattered_order, fast_tensor, slow_tensor)

            def fast_scalar(act):
                act.sem_inc(copied, 2)
                act.sem_inc(f_totals, 2)

                def compare(i, k):
                    tile, h, q = i * CHUNK + k, k // 4, k % 4
                    act.wait_ge(ids_spread, i * 4 + h + 1)
                    act.wait_ge(f_summed, tile + 1)
                    act.activation(apart[:, q, :], p_target[h % 2][:, q, :], ACT.Abs, bias=v.minus_src[:, bass.ds(tile, 1)]).then_inc(sames, 1)
                    act.wait_ge(sames, tile * 2 + 1)
                    act.activation(same[:, k % 8, :], apart[:, q, :], ACT.Relu, bias=v.ones[:, 0:1], scale=-2.0).then_inc(sames, 1)

                def copy_messages(i, k):
                    tile, q = i * CHUNK + k, k % 4
                    act.wait_ge(f_summed, tile + 5)
                    act.wait_ge(expanded, tile + CHUNK + 1)
                    act.copy(msg[:, q, 0:D], p_msg[q % 2][:, 0:D]).then_inc(copied, 1)

                def copy_totals(i, k):
                    tile, q = i * CHUNK + k, k % 4
                    act.wait_ge(f_done, tile + 5)
                    act.wait_ge(f_summed, tile + 9)
                    act.copy(total[:, q, :], p_sum[q % 2][:, 0:MW]).then_inc(f_totals, 1)

                skewed(act, TILES, CHUNK, (5, compare), (1, copy_messages), (0, copy_totals))

            def slow_scalar(act):
                with act.Fori(0, TILES // U) as i:
                    for k in range(U):
                        tile = i * U + k
                        act.wait_ge(scatter_done, tile + 1)
                        act.wait_ge(sums_ready, tile + 5)
                        act.copy(total[:, k, :], summed[k][:, 0:MW]).then_inc(totals, 1)

            @block.scalar
            def _(act):
                choose(act, v.scattered_order, fast_scalar, slow_scalar)


def normalise(dve, act_wait, chain, raw, stats, outs, signal, passed):
    chain.link(dve.bn_stats(stats[:, 0:6], raw))
    dve.sem_inc(passed, 1)
    chain.link(dve.bn_aggr(stats[:, 6:8], stats[:, 0:6]))
    dve.tensor_scalar_add(stats[:, 8:9], stats[:, 7:8], EPS).then_inc(signal, 1)
    act_wait()
    chain.link(dve.reciprocal(stats[:, 10:11], stats[:, 9:10]))
    for out_view, in_view in outs:
        chain.step(dve.tensor_scalar(out_view, in_view, stats[:, 6:7], stats[:, 10:11], ALU.subtract, ALU.mult))
    chain.settle()


def layer0_nodes(nc, t, v):
    with ExitStack() as local:
        N = 6
        sb = lambda name, shape: [v.sb(f"{name}{k}", shape, F32, local) for k in range(N)]
        x, xs, xv = sb("n_x", [P, D]), sb("n_xs", [S, P]), sb("n_xv", [96, P])
        sums = sb("n_sums", [P, COPIES, MW])
        at_a, at_b = sb("at_a", [P, P]), sb("at_b", [33, P])
        raw, stats, xn_parts = sb("raw", [P, D]), sb("stats", [P, 12]), sb("xn_parts", [P, D])
        xn_s, xn_v = sb("xn_s", [S, P]), sb("xn_v", [V, 3, P])
        y = sb("y", [P, D])
        p_sums = [v.ps(f"p_sums{k}", [P, 2, P], local) for k in range(2)]
        p_h = [v.ps(f"p_h{k}", [P, D], local) for k in range(2)]
        p_xn = [v.ps(f"p_xn{k}", [S, 4, P], local) for k in range(2)]
        p_out = [v.ps(f"p_out{k}", [P, 320], local) for k in range(2)]
        loads = [v.sem(f"n_loads{k}", local) for k in range(N)]
        stores = [v.sem(f"n_stores{k}", local) for k in range(N)]
        stored = v.sem("n_stored", local)
        sums_full = v.sem("n_sums_full", local)
        h_full = v.sem("n_h_full", local)
        xn_full = v.sem("n_xn_full", local)
        outs_full = v.sem("n_outs_full", local)
        sums_turned = v.sem("n_sums_turned", local)
        rooted = v.sem("n_rooted", local)
        xn_turned = v.sem("n_xn_turned", local)
        raw_chain = v.sem("n_raw_chain", local)
        norm_chain = v.sem("n_norm_chain", local)
        var_ready = v.sem("n_var_ready", local)
        passed = v.sem("n_passed", local)
        passed_pe = v.sem("n_passed_pe", local)
        xn_ready = v.sem("n_xn_ready", local)
        outs_ready = v.sem("n_outs_ready", local)
        LOADS = 3 + COPIES
        with nc.Block() as block:

            @block.sync
            def _(sp):
                sp.sem_inc(stored, N)

                def load(i, k):
                    at = bass.ds((i * N + k) * P, P)
                    sp.wait_ge(stored, i * N + k + 1)
                    sp.dma_start(x[k][:], t["x"][at, :]).then_inc(loads[k], 16)
                    sp.dma_start(xs[k][:], t["x_t"][0:S, at]).then_inc(loads[k], 16)
                    sp.dma_start(xv[k][:], t["x_t"][S:D, at]).then_inc(loads[k], 16)
                    for r in range(COPIES):
                        sp.dma_start(sums[k][:, r, :], v.sums0[r][at, :]).then_inc(loads[k], 16)

                def store(i, k):
                    sp.wait_ge(outs_ready, i * N + k + 3)
                    sp.dma_start(v.y_table[bass.ds((i * N + k) * P, P), :], y[k][:]).then_inc(stores[k], 16)

                def landed(i, k):
                    sp.wait_ge(stores[k], i * 16 + 16)
                    sp.sem_inc(stored, 1)

                skewed(sp, BLOCKS, N, (5, load), (1, store), (0, landed))

            @block.tensor
            def _(pe):

                def turn_sums(i, k):
                    b = i * N + k
                    pe.wait_ge(loads[k], i * 16 * LOADS + 16 * LOADS)
                    pe.wait_ge(sums_turned, b + 1)
                    for r in range(COPIES):
                        pe.matmul(p_sums[k % 2][:, 0, :], sums[k][:, r, 0:P], v.ident[:], start=(r == 0), stop=(r == COPIES - 1))
                    for r in range(COPIES):
                        last = pe.matmul(p_sums[k % 2][0:33, 1, :], sums[k][:, r, P:MW], v.ident[:], start=(r == 0), stop=(r == COPIES - 1))
                    last.then_inc(sums_full, 1)
                    pe.wait_ge(raw_chain, b * 3 + 1)
                    pe.matmul(p_h[k % 2][:], xs[k][:], v.wu_s[:], start=True, stop=False)
                    pe.matmul(p_h[k % 2][:], xv[k][:], v.wu_v[:], start=False, stop=False)
                    pe.matmul(p_h[k % 2][:], v.ones[0:1, :], v.bu[:], start=False, stop=False)

                def update(i, k):
                    pe.wait_ge(sums_turned, i * N + k + 3)
                    pe.matmul(p_h[k % 2][:], at_a[k][:], v.wmu_a[:], start=False, stop=False)
                    pe.matmul(p_h[k % 2][:], at_b[k][:], v.wmu_b[:], start=False, stop=True).then_inc(h_full, 1)

                def turn_xn(i, k):
                    b = i * N + k
                    pe.wait_ge(xn_turned, b + 1)
                    pe.wait_ge(xn_ready, b + 1)
                    pe.sem_inc(passed_pe, 1)
                    pe.transpose(p_xn[k % 2][0:S, 0, :], xn_parts[k][:, 0:S], v.ident[:])
                    for c in range(3):
                        last = pe.transpose(p_xn[k % 2][0:V, 1 + c, :], xn_parts[k][:, S + 32 * c:S + 32 * c + 32], v.ident[:])
                    last.then_inc(xn_full, 1)

                def outputs(i, k):
                    b = i * N + k
                    pe.wait_ge(xn_turned, b + 3)
                    pe.wait_ge(outs_ready, b + 1)
                    pe.matmul(p_out[k % 2][:, 0:128], xn_s[k][:], v.w_node0[:], start=True, stop=True)
                    for c in range(3):
                        last = pe.matmul(p_out[k % 2][:, 128 + 64 * c:192 + 64 * c], xn_v[k][:, c, :], v.w_node1[:], start=True, stop=True)
                    last.then_inc(outs_full, 1)

                skewed(pe, BLOCKS, N, (3, turn_sums), (2, update), (1, turn_xn), (0, outputs))

            @block.scalar
            def _(act):
                act.sem_inc(sums_turned, 2)
                act.sem_inc(xn_turned, 2)

                def copy_sums(i, k):
                    act.wait_ge(sums_full, i * N + k + 1)
                    act.copy(at_a[k][:], p_sums[k % 2][:, 0, :])
                    act.copy(at_b[k][:], p_sums[k % 2][0:33, 1, :]).then_inc(sums_turned, 1)

                def root(i, k):
                    act.wait_ge(var_ready, i * N + k + 1)
                    act.activation(stats[k][:, 9:10], stats[k][:, 8:9], ACT.Sqrt).then_inc(rooted, 1)

                def copy_xn(i, k):
                    act.wait_ge(xn_full, i * N + k + 1)
                    act.copy(xn_s[k][:], p_xn[k % 2][0:S, 0, :])
                    act.copy(xn_v[k][:], p_xn[k % 2][0:V, 1:4, :]).then_inc(xn_turned, 1)

                skewed(act, BLOCKS, N, (3, copy_sums), (2, root), (1, copy_xn))

            @block.vector
            def _(dve):
                dve.sem_inc(raw_chain, 6)
                dve.sem_inc(outs_ready, 2)

                def measure(i, k):
                    b = i * N + k
                    chain = Chain(dve, raw_chain, b * 3 + 6)
                    dve.wait_ge(h_full, b + 1)
                    chain.link(dve.scalar_tensor_tensor(raw[k][:], x[k][:], 2.0, p_h[k % 2][:], ALU.mult, ALU.add))
                    chain.link(dve.bn_stats(stats[k][:, 0:6], raw[k][:]))
                    dve.sem_inc(passed, 1)
                    chain.link(dve.bn_aggr(stats[k][:, 6:8], stats[k][:, 0:6]))
                    dve.tensor_scalar_add(stats[k][:, 8:9], stats[k][:, 7:8], EPS).then_inc(var_ready, 1)

                def norm(i, k):
                    b = i * N + k
                    chain = Chain(dve, norm_chain, b * 3)
                    dve.wait_ge(rooted, b + 1)
                    chain.link(dve.reciprocal(stats[k][:, 10:11], stats[k][:, 9:10]))
                    mean, scale = stats[k][:, 6:7], stats[k][:, 10:11]
                    chain.step(dve.tensor_scalar(xn_parts[k][:, 0:S], raw[k][:, 0:S], mean, scale, ALU.subtract, ALU.mult))
                    chain.step(dve.tensor_scalar(xn_parts[k][:, S:D].rearrange("p (i c) -> p i c", i=3),
                                                 raw[k][:, S:D].rearrange("p (c i) -> p i c", i=3), mean, scale, ALU.subtract, ALU.mult))
                    chain.settle()
                    dve.sem_inc(xn_ready, 1)

                def finish(i, k):
                    b = i * N + k
                    a = v.a_col[:, bass.ds(b, 1)]
                    dve.wait_ge(outs_full, b + 1)
                    out = p_out[k % 2]
                    parts = out[:, 128:320].rearrange("p (i w) -> p i w", i=3)
                    dve.tensor_scalar(y[k][:, 0:S], out[:, 0:S], a, None, ALU.mult)
                    dve.tensor_scalar(y[k][:, S:D].rearrange("p (i c) -> p i c", i=3), parts[:, :, 0:V], a, None, ALU.mult)
                    own = v.own[:, bass.ds(b, 1), :].rearrange("p a d -> p (a d)")
                    dve.scalar_tensor_tensor(own[:, 0:S], out[:, S:128], a, xn_parts[k][:, 0:S], ALU.mult, ALU.add)
                    dve.scalar_tensor_tensor(own[:, S:D].rearrange("p (c i) -> p i c", i=3), parts[:, :, V:64], a,
                                             xn_parts[k][:, S:D].rearrange("p (i c) -> p i c", i=3), ALU.mult, ALU.add).then_inc(outs_ready, 1)

                skewed(dve, BLOCKS, N, (1, norm), (2, measure), (0, finish))


def layer1_edges(nc, t, v):
    with ExitStack() as local:
        U = COPIES
        y = v.sb("e_y", [P, U, D], F32, local)
        lengths = v.sb("lengths", [10, U, P], F32, local)
        attr = v.sb("attr", [P, U, 4], F32, local)
        targets = v.sb("e_targets", [P, U, P], I32, local)
        same = v.sb("e_same", [P, U, P], F32, local)
        scratch = v.sb("e_scratch", [P, U, P], F32, local)
        dup = v.sb("e_dup", [P, U], F32, local)
        hidden = v.sb("hidden", [100, U, P], F32, local)
        R = 6
        b_lengths = [v.sb(f"b_lengths{q}", [10, BLOCK_EDGES], F32, local) for q in range(2)]
        b_hidden = [v.sb(f"b_hidden{q}", [100, BLOCK_EDGES], F32, local) for q in range(2)]
        b_source = [v.sb(f"b_source{q}", [P, TPB], I32, local) for q in range(2)]
        b_node = [v.sb(f"b_node{q}", [P, TPB], I32, local) for q in range(2)]
        b_attr = [v.sb(f"b_attr{q}", [P, TPB, 4], F32, local) for q in range(2)]
        b_column = [v.sb(f"b_column{q}", [P, TPB], F32, local) for q in range(2)]
        f_y = v.sb("f_y", [P, R, D], F32, local)
        f_hot = v.sb("f_hot", [P, R, P], F32, local)
        f_prod = v.sb("f_prod", [P, R, 2, S], F32, local)
        f_w2e = v.sb("f_w2e", [P, R, V], F32, local)
        f_dot = v.sb("f_dot", [P, R, 3, V], F32, local)
        f_msg = v.sb("f_msg", [P, R, 4, 96], F32, local)
        block_sums = v.sb("block_sums", [P, UW], F32, local)
        block_sums_t = v.sb("block_sums_t", [96, 512], F32, local)
        block_whole = v.sb("block_whole", [P, D], F32, local)
        block_stats = v.sb("block_stats", [P, 8], F32, local)
        prod = v.sb("prod", [P, U, 2, S], F32, local)
        w2e = v.sb("w2e", [P, U, V], F32, local)
        dot = v.sb("dot", [P, U, 3, V], F32, local)
        msg = v.sb("e_msg", [P, U, 4, 96], F32, local)
        total = v.sb("e_total", [P, U, UW], F32, local)
        source_idx = [v.sb(f"e_source_idx{k}", [P, 1], I32, local) for k in range(U)]
        target_idx = [v.sb(f"e_target_idx{k}", [P, 1], I32, local) for k in range(U)]
        p_hid = [v.ps(f"p_hid{k}", [P, 512], local) for k in range(2)]
        p_w = [v.ps(f"p_w{k}", [P, 512], local) for k in range(2)]
        p_sum = [v.ps(f"p_sum{k}", [P, 512], local) for k in range(4)]
        p_bhid, p_trans, p_rad, p_acc, p_res = p_hid[0], p_hid[1], p_w, p_sum[0:2], p_sum[2]
        y_in = [v.sem(f"y_in{k}", local) for k in range(R)]
        hid_full = v.sem("hid_full", local)
        hid_done = v.sem("hid_done", local)
        rad_full = v.sem("rad_full", local)
        hots = v.sem("hots", local)
        prods = v.sem("prods", local)
        parts_dve = v.sem("parts_dve", local)
        parts_act = v.sem("parts_act", local)
        added = v.sem("added", local)
        columns = v.sem("columns", local)
        f_chain = v.sem("f_chain", local)
        end_pe = v.sem("end_pe", local)
        end_act = v.sem("end_act", local)
        end_dve = v.sem("end_dve", local)
        edges_in = [v.sem(f"e_edges_in{k}", local) for k in range(U)]
        scattered = [v.sem(f"e_scattered{k}", local) for k in range(U)]
        idx_ready = v.sem("e_idx_ready", local)
        dve_chain = v.sem("e_dve_chain", local)
        prep_chain = v.sem("e_prep_chain", local)
        act_chain = v.sem("e_act_chain", local)
        hidden_psum = v.sem("e_hidden_psum", local)
        hidden_ready = v.sem("e_hidden_ready", local)
        sums_ready = v.sem("e_sums_ready", local)
        totals = v.sem("e_totals", local)
        scatter_done = v.sem("e_scatter_done", local)
        passed = v.sem("e_passed", local)
        passed_dve = v.sem("e_passed_dve", local)
        passed_pe = v.sem("e_passed_pe", local)
        passed_sp = v.sem("e_passed_sp", local)
        zeroed = v.sem("e_zeroed", local)
        cleared = v.sem("e_cleared", local)
        CLEARS = 16 * COPIES * (TABLE_ROWS // P // 3)
        STEPS = 5
        BODY = 2 * TPB
        ALL = FAST_BLOCKS * TPB
        HIDES = 6
        HC = BLOCK_EDGES // HIDES

        def block_end(fn):
            def at(i, k):
                if k % TPB == TPB - 1:
                    fn(i, k // TPB, i * 2 + k // TPB)
            return at

        with nc.Block() as block:

            def fast_sync(sp):
                def load_block(i, q):
                    b = i * 2 + q
                    sp.wait_ge(added, b * TPB + TPB)
                    sp.sem_inc(passed_sp, 1)
                    first = sp.value_load(v.block_start[bass.ds(b, 1), :], min_val=0, max_val=TILES * P)
                    edges = bass.ds(first, BLOCK_EDGES)
                    sp.dma_start(b_source[q][:], t["src_flat"][edges, :].rearrange("(p j) a -> p (j a)", p=P)).then_inc(edges_in[q], 16)
                    sp.dma_start(b_node[q][:], t["dst_flat"][edges, :].rearrange("(p j) a -> p (j a)", p=P)).then_inc(edges_in[q], 16)
                    sp.dma_start(b_attr[q][:].rearrange("p j a -> p (j a)"), t["e4_flat"][edges, :].rearrange("(p j) a -> p (j a)", p=P)).then_inc(edges_in[q], 16)
                    sp.dma_start(b_lengths[q][:], t["e10_t"][:, edges]).then_inc(edges_in[q], 16)

                skewed(sp, FAST_BLOCKS, 2, (0, load_block))

            def slow_sync(sp):
                sp.wait_ge(zeroed, 1)
                for r in range(COPIES):
                    for h in range(TABLE_ROWS // P // 3):
                        sp.dma_start(v.sums1[r].rearrange("(p a) d -> p (a d)", p=P)[:, h * 3 * UW:(h + 1) * 3 * UW],
                                     msg[:, 0:3, :, :].rearrange("p a g c -> p (a g c)")).then_inc(cleared, 16)
                with sp.Fori(0, TILES // U) as i:
                    for k in range(U):
                        tile = i * U + k
                        sp.wait_ge(sums_ready, tile + 1)
                        sp.dma_start(attr[:, k, :], t["e4_cols"][:, bass.ds(tile, 1), :].rearrange("p a b -> p (a b)")).then_inc(edges_in[k], 16)
                        sp.dma_start(lengths[:, k, :], t["e10_t"][:, bass.ds(tile * P, P)]).then_inc(edges_in[k], 16)
                        sp.dma_start(targets[:, k, :], t["dst_rows"][bass.ds(tile, 1), :].broadcast_to([P, P])).then_inc(edges_in[k], 16)

            @block.sync
            def _(sp):
                choose(sp, v.unblocked_order, fast_sync, slow_sync)

            def fast_gpsimd(pool):
                def gather(i, k):
                    q, j = k // TPB, k % TPB
                    pool.wait_ge(added, i * BODY + k + BODY - R + 1)
                    if j == 0:
                        pool.wait_ge(edges_in[q], i * 64 + 64)
                    pool.sem_inc(passed, 1)
                    pool.indirect_dma_start(f_y[:, k % R, :], None, v.y_table[:, :],
                                            bass.IndirectOffsetOnAxis(b_source[q][:, j:j + 1], 0)).then_inc(y_in[k % R], 16)

                skewed(pool, ALL, BODY, (0, gather))

            def slow_gpsimd(pool):
                pool.wait_ge(cleared, CLEARS)
                pool.sem_inc(scatter_done, U)

                def gather(i, k):
                    pool.wait_ge(sums_ready, i * U + k + 1)
                    pool.wait_ge(idx_ready, i * U + k + 1)
                    pool.sem_inc(passed, 1)
                    pool.indirect_dma_start(y[:, k, :], None, v.y_table[:, :],
                                            bass.IndirectOffsetOnAxis(source_idx[k][:, 0:1], 0)).then_inc(y_in[k], 16)

                def scatter(i, k):
                    pool.wait_ge(totals, i * U + k + 1)
                    pool.sem_inc(passed, 1)
                    pool.indirect_dma_start(v.sums1[k][:, :], bass.IndirectOffsetOnAxis(target_idx[k][:, 0:1], 0),
                                            total[:, k, :], None, compute_op=ALU.add).then_inc(scattered[k], 16)

                def landed(i, k):
                    pool.wait_ge(scattered[k], i * 16 + 16)
                    pool.sem_inc(scatter_done, 1)

                skewed(pool, TILES, U, (3, gather), (1, scatter), (0, landed))

            @block.gpsimd
            def _(pool):
                choose(pool, v.unblocked_order, fast_gpsimd, slow_gpsimd)

            def fast_vector(dve):
                STEPS = 4
                dve.sem_inc(parts_dve, 2)
                dve.sem_inc(end_dve, 6)

                def prepare(i, k):
                    q, j, tile = k // TPB, k % TPB, i * BODY + k
                    if isinstance(tile, int) and tile >= ALL:
                        return
                    if j == 0:
                        dve.wait_ge(edges_in[q], i * 64 + 64)
                        dve.tensor_scalar(b_column[q][:], b_node[q][:], v.block_base[:, bass.ds(i * 2 + q, 1)], None, ALU.subtract).then_inc(columns, 1)
                        dve.wait_ge(columns, i * 2 + q + 1)
                    dve.wait_ge(added, tile + BODY - R + 1)
                    dve.tensor_scalar(f_hot[:, k % R, :], v.count_row[:], b_column[q][:, j:j + 1], None, ALU.is_equal).then_inc(hots, 1)

                def weigh(i, k, between):
                    q, j, r, tile = k // TPB, k % TPB, k % R, i * BODY + k
                    chain = Chain(dve, f_chain, tile * STEPS)
                    w, e = p_rad[k % 2], b_attr[q]
                    y1 = f_y[:, r, S:D].rearrange("p (i c) -> p i c", i=3)
                    dve.wait_ge(y_in[r], i * (16 * BODY // R) + 16 * (k // R) + 16)
                    chain.step(dve.tensor_scalar(f_dot[:, r, 0, :], y1[:, 0, :], e[:, j, 1:2], None, ALU.mult))
                    dve.wait_ge(rad_full, tile + 1)
                    dve.tensor_tensor(f_prod[:, r, :, :], w[:, 0:128].rearrange("p (g c) -> p g c", g=2),
                                      f_y[:, r, 0:S].unsqueeze(1).broadcast_to([P, 2, S]), ALU.mult).then_inc(prods, 1)
                    chain.step(dve.tensor_scalar(f_w2e[:, r, :], w[:, 128:160], e[:, j, 0:1], None, ALU.mult))
                    dve.wait_ge(f_chain, chain.base + 1)
                    chain.step(dve.scalar_tensor_tensor(f_dot[:, r, 1, :], y1[:, 1, :], e[:, j, 2:3], f_dot[:, r, 0, :], ALU.mult, ALU.add))
                    dve.wait_ge(f_chain, chain.base + 2)
                    dve.tensor_tensor(f_msg[:, r, 1:4, S:96], y1, f_w2e[:, r, :].unsqueeze(1).broadcast_to([P, 3, V]), ALU.mult)
                    dve.wait_ge(f_chain, chain.base + 3)
                    chain.step(dve.scalar_tensor_tensor(f_dot[:, r, 2, :], y1[:, 2, :], e[:, j, 3:4], f_dot[:, r, 1, :], ALU.mult, ALU.add))
                    between()
                    chain.settle()
                    dve.tensor_tensor(f_msg[:, r, 0, S:96], f_dot[:, r, 2, :], w[:, 160:192], ALU.mult).then_inc(parts_dve, 1)
                    assert chain.n == STEPS, chain.n

                def weigh_and_prepare(i, k):
                    weigh(i, k, lambda: prepare(i + (k + 1) // BODY, (k + 1) % BODY))

                def finish(i, q, b):
                    chain = Chain(dve, end_dve, b * 6 + 6)
                    a = v.a_col[:, bass.ds(b, 1)]
                    own = v.own[:, bass.ds(b, 1), :].rearrange("p a d -> p (a d)")
                    vectors = own[:, S:D].rearrange("p (c i) -> p i c", i=3)
                    dve.wait_ge(end_pe, b * 2 + 2)
                    whole = block_whole[:, S:D].rearrange("p (c i) -> p i c", i=3)
                    chain.step(dve.scalar_tensor_tensor(block_whole[:, 0:S], p_res[:, 0:S], a, own[:, 0:S], ALU.mult, ALU.add))
                    chain.link(dve.scalar_tensor_tensor(whole, p_res[:, S:D].rearrange("p (i c) -> p i c", i=3), a, vectors, ALU.mult, ALU.add))
                    dve.sem_inc(passed_dve, 1)
                    chain.step(dve.tensor_copy(own, block_whole[:]))
                    chain.link(dve.bn_stats(block_stats[:, 0:6], block_whole[:]))
                    dve.sem_inc(passed_dve, 1)
                    chain.link(dve.bn_aggr(block_stats[:, 6:8], block_stats[:, 0:6]))
                    dve.sem_inc(passed_dve, 1)
                    chain.step(dve.tensor_copy(v.moments[:, bass.ds(b, 1), :].rearrange("p a d -> p (a d)"), block_stats[:, 6:8]))

                prepare(0, 0)
                skewed(dve, ALL, BODY, (11, weigh_and_prepare), (0, block_end(finish)))

            def slow_vector(dve):
                dve.memset(msg[:], 0.0).then_inc(zeroed, 1)
                dve.wait_ge(cleared, CLEARS)
                dve.sem_inc(parts_dve, 2)

                def prepare(i, k):
                    tile = i * U + k
                    chain = Chain(dve, prep_chain, tile * 3)
                    dve.wait_ge(scatter_done, tile + 1)
                    dve.wait_ge(edges_in[k], i * 48 + 48)
                    dve.wait_ge(sums_ready, tile + 1)
                    chain.link(dve.tensor_scalar(same[:, k, :], targets[:, k, :], v.dst_col[:, bass.ds(tile, 1)], None, ALU.is_equal))
                    dve.tensor_copy(source_idx[k][:], v.src_int[:, bass.ds(tile, 1)]).then_inc(idx_ready, 1)
                    chain.link(dve.tensor_tensor_reduce(out=scratch[:, k, :], in0=same[:, k, :], in1=v.dump_before[:], scale=1.0, scalar=0.0,
                                                        op0=ALU.mult, op1=ALU.max, accum_out=dup[:, k:k + 1]))
                    chain.step(dve.tensor_tensor(target_idx[k][:], dup[:, k:k + 1], v.dst_col[:, bass.ds(tile, 1)], ALU.max))

                def weigh(i, k):
                    tile = i * U + k
                    chain = Chain(dve, dve_chain, tile * STEPS)
                    dve.wait_ge(y_in[k], i * 16 + 16)
                    dve.wait_ge(rad_full, tile + 1)
                    w = p_w[k % 2]
                    y1 = y[:, k, S:D].rearrange("p (i c) -> p i c", i=3)
                    e0 = attr[:, k, 0:1]
                    dve.tensor_tensor(prod[:, k, :, :], w[:, 0:128].rearrange("p (g c) -> p g c", g=2),
                                      y[:, k, 0:S].unsqueeze(1).broadcast_to([P, 2, S]), ALU.mult).then_inc(prods, 1)
                    chain.step(dve.tensor_scalar(w2e[:, k, :], w[:, 128:160], e0, None, ALU.mult))
                    chain.link(dve.tensor_scalar(dot[:, k, 0, :], y1[:, 0, :], attr[:, k, 1:2], None, ALU.mult))
                    chain.step(dve.tensor_tensor(msg[:, k, 1:4, S:96], y1, w2e[:, k, :].unsqueeze(1).broadcast_to([P, 3, V]), ALU.mult))
                    chain.link(dve.scalar_tensor_tensor(dot[:, k, 1, :], y1[:, 1, :], attr[:, k, 2:3], dot[:, k, 0, :], ALU.mult, ALU.add))
                    chain.link(dve.scalar_tensor_tensor(dot[:, k, 2, :], y1[:, 2, :], attr[:, k, 3:4], dot[:, k, 1, :], ALU.mult, ALU.add))
                    dve.tensor_tensor(msg[:, k, 0, S:96], dot[:, k, 2, :], w[:, 160:192], ALU.mult).then_inc(parts_dve, 1)
                    assert chain.n == STEPS, chain.n

                skewed(dve, TILES, U, (1, prepare), (0, weigh))

            @block.vector
            def _(dve):
                choose(dve, v.unblocked_order, fast_vector, slow_vector)

            def fast_tensor(pe):
                pe.sem_inc(added, BODY)

                def hide(i, k):
                    q, c, odd = k // TPB, (k % TPB) // 2, k % TPB % 2
                    if odd or c >= HIDES:
                        return
                    if c == 0:
                        pe.wait_ge(edges_in[q], i * 64 + 64)
                    pe.wait_ge(hid_done, i * 2 * HIDES + q * HIDES + c + 1)
                    pe.matmul(p_bhid[0:100, 0:HC], v.fc1[:], b_lengths[q][:, c * HC:(c + 1) * HC], start=True, stop=True).then_inc(hid_full, 1)

                def radial(i, k):
                    q, j, tile = k // TPB, k % TPB, i * BODY + k
                    pe.wait_ge(hid_done, (i * 2 + q) * HIDES + HIDES + 1)
                    pe.wait_ge(parts_dve, tile + 1)
                    pe.matmul(p_rad[k % 2][:, 0:192], b_hidden[q][:, j::TPB], v.fc2[:], start=True, stop=True).then_inc(rad_full, 1)

                def add_up(i, k):
                    q, j, r, tile = k // TPB, k % TPB, k % R, i * BODY + k
                    pe.wait_ge(hots, tile + 1)
                    pe.wait_ge(parts_act, tile + 1)
                    pe.wait_ge(parts_dve, tile + 3)
                    if j == 0:
                        pe.wait_ge(end_act, i * 4 + 2 * q + 1)
                    pe.matmul(p_acc[q][:, 0:UW], f_hot[:, r, :], f_msg[:, r, :, :].rearrange("p g c -> p (g c)"),
                              start=(j == 0), stop=(j == TPB - 1)).then_inc(added, 1)

                def turn(i, q, b):
                    pe.wait_ge(end_act, b * 2 + 5)
                    pe.sem_inc(passed_pe, 1)
                    for g in range(4):
                        last = pe.transpose(p_trans[0:96, P * g:P * g + P], block_sums[:, 96 * g:96 * g + 96], v.ident[:])
                    last.then_inc(end_pe, 1)

                def combine(i, q, b):
                    pe.wait_ge(end_act, b * 2 + 6)
                    pe.wait_ge(end_dve, b * 6 + 2)
                    pe.matmul(p_res[:, 0:S], block_sums_t[:, 0:P], v.w_out0[:], start=True, stop=True)
                    for c in range(3):
                        last = pe.matmul(p_res[:, S + 32 * c:S + 32 * c + 32], block_sums_t[:, P * (c + 1):P * (c + 2)], v.w_out1[:], start=True, stop=True)
                    last.then_inc(end_pe, 1)

                skewed(pe, ALL, BODY, (23, hide), (12, radial), (9, add_up), (6, block_end(turn)), (3, block_end(combine)))

            def slow_tensor(pe):
                pe.sem_inc(sums_ready, U)

                def hide(i, k):
                    pe.wait_ge(edges_in[k], i * 48 + 48)
                    pe.wait_ge(hidden_ready, i * U + k + 1)
                    pe.matmul(p_hid[k % 2][0:100, 0:P], v.fc1[:], lengths[:, k, :], start=True, stop=True).then_inc(hidden_psum, 1)

                def radial(i, k):
                    tile = i * U + k
                    pe.wait_ge(hidden_ready, tile + 3)
                    pe.wait_ge(parts_dve, tile + 1)
                    pe.matmul(p_w[k % 2][:, 0:192], hidden[:, k, :], v.fc2[:], start=True, stop=True).then_inc(rad_full, 1)

                def add_up(i, k):
                    tile = i * U + k
                    pe.wait_ge(prep_chain, tile * 3 + 3)
                    pe.wait_ge(parts_act, tile + 1)
                    pe.wait_ge(parts_dve, tile + 3)
                    pe.matmul(p_sum[k][:, 0:UW], same[:, k, :], msg[:, k, :, :].rearrange("p g c -> p (g c)"), start=True, stop=True).then_inc(sums_ready, 1)

                skewed(pe, TILES, U, (2, hide), (1, radial), (0, add_up))

            @block.tensor
            def _(pe):
                choose(pe, v.unblocked_order, fast_tensor, slow_tensor)

            def fast_scalar(act):
                act.sem_inc(hid_done, 1)
                act.sem_inc(end_act, 4)

                def rectify(i, k):
                    q, c, odd = k // TPB, (k % TPB) // 2, k % TPB % 2
                    if odd or c >= HIDES:
                        return
                    act.wait_ge(hid_full, i * 2 * HIDES + q * HIDES + c + 1)
                    act.activation(b_hidden[q][:, c * HC:(c + 1) * HC], p_bhid[0:100, 0:HC], ACT.Relu).then_inc(hid_done, 1)

                def weigh(i, k):
                    q, j, r, tile = k // TPB, k % TPB, k % R, i * BODY + k
                    e = b_attr[q]
                    act.wait_ge(prods, tile + 1)
                    act.activation(f_msg[:, r, 0, 0:S], f_prod[:, r, 0, :], ACT.Copy, scale=e[:, j, 0:1])
                    for c in range(3):
                        last = act.activation(f_msg[:, r, 1 + c, 0:S], f_prod[:, r, 1, :], ACT.Copy, scale=e[:, j, 1 + c:2 + c])
                    last.then_inc(parts_act, 1)

                def take_sums(i, q, b):
                    act.wait_ge(added, b * TPB + TPB + BODY)
                    act.copy(block_sums[:], p_acc[q][:, 0:UW]).then_inc(end_act, 1)

                def take_turned(i, q, b):
                    act.wait_ge(end_pe, b * 2 + 1)
                    act.copy(block_sums_t[:], p_trans[0:96, :]).then_inc(end_act, 1)

                skewed(act, ALL, BODY, (23, rectify), (11, weigh), (8, block_end(take_sums)), (5, block_end(take_turned)))

            def slow_scalar(act):
                act.sem_inc(hidden_ready, 2)

                def rectify(i, k):
                    tile = i * U + k
                    act.wait_ge(hidden_psum, tile + 1)
                    act.wait_ge(sums_ready, tile + 1)
                    act.activation(hidden[:, k, :], p_hid[k % 2][0:100, 0:P], ACT.Relu).then_inc(hidden_ready, 1)

                def weigh(i, k):
                    tile = i * U + k
                    act.wait_ge(prods, tile + 1)
                    act.activation(msg[:, k, 0, 0:S], prod[:, k, 0, :], ACT.Copy, scale=attr[:, k, 0:1])
                    for c in range(3):
                        last = act.activation(msg[:, k, 1 + c, 0:S], prod[:, k, 1, :], ACT.Copy, scale=attr[:, k, 1 + c:2 + c])
                    last.then_inc(parts_act, 1)

                def copy_totals(i, k):
                    tile = i * U + k
                    act.wait_ge(scatter_done, tile + 1)
                    act.wait_ge(sums_ready, tile + 5)
                    act.copy(total[:, k, :], p_sum[k][:, 0:UW]).then_inc(totals, 1)

                skewed(act, TILES, U, (3, rectify), (1, weigh), (0, copy_totals))

            @block.scalar
            def _(act):
                choose(act, v.unblocked_order, fast_scalar, slow_scalar)


def layer1_nodes(nc, t, v, out):
    with ExitStack() as local:
        sb = lambda name, shape: [v.sb(f"{name}{k}", shape, F32, local) for k in range(2)]
        sums, sums_t = sb("f_sums", [P, COPIES, UW]), sb("f_sums_t", [96, 512])
        raw, stats, res = sb("f_raw", [P, D]), sb("f_stats", [P, 12]), sb("f_res", [P, D])
        p_t = [v.ps(f"f_p_t{k}", [P, 512], local) for k in range(2)]
        p_o = [v.ps(f"f_p_o{k}", [P, D], local) for k in range(2)]
        loads = [v.sem(f"f_loads{k}", local) for k in range(2)]
        stores = [v.sem(f"f_stores{k}", local) for k in range(2)]
        stored = v.sem("f_stored", local)
        pe_steps = v.sem("f_pe_steps", local)
        act_steps = v.sem("f_act_steps", local)
        dve_chain = v.sem("f_dve_chain", local)
        var_ready = v.sem("f_var_ready", local)
        passed = v.sem("f_passed", local)
        res_ready = v.sem("f_res_ready", local)
        STEPS = 6
        LOADS = COPIES
        FULL = NODES // P
        PARTS = [(b, min(b + 12, FULL)) for b in range(0, FULL, 12)]
        variance, deviation, scale = [v.sb(f"f_{name}", [P, FAST_BLOCKS], F32, local) for name in ("variance", "deviation", "scale")]
        spread_ready = v.sem("f_spread_ready", local)
        root_ready = v.sem("f_root_ready", local)
        part_ready = v.sem("f_part_ready", local)
        fast_stores = v.sem("f_fast_stores", local)
        with nc.Block() as block:

            def blocks(eng, body):
                with eng.Fori(0, FULL // 2) as i:
                    body(i, (0, 1))
                body(FULL // 2, (0,))

            def fast_sync(sp):
                for part, (b0, b1) in enumerate(PARTS):
                    sp.wait_ge(part_ready, part + 1)
                    sp.dma_start(out[b0 * P:b1 * P, :].rearrange("(b p) d -> p b d", p=P), v.own[:, b0:b1, :]).then_inc(fast_stores, 16)
                sp.dma_start(out[FULL * P:, :], v.own[0:NODES - FULL * P, FULL, :]).then_inc(fast_stores, 16)
                sp.wait_ge(fast_stores, 16 * len(PARTS) + 16)

            def slow_sync(sp):
                sp.sem_inc(stored, 2)

                def body(i, ks):
                    for k in ks:
                        at = bass.ds((i * 2 + k) * P, P)
                        sp.wait_ge(stored, i * 2 + k + 1)
                        for r in range(COPIES):
                            sp.dma_start(sums[k][:, r, :], v.sums1[r][at, :]).then_inc(loads[k], 16)
                    for k in ks:
                        sp.wait_ge(res_ready, i * 2 + k + 1)
                        rows = P if len(ks) == 2 else NODES - FULL * P
                        sp.dma_start(out[bass.ds((i * 2 + k) * P, rows), :], res[k][0:rows, :]).then_inc(stores[k], 16)
                        sp.wait_ge(stores[k], i * 16 + 16)
                        sp.sem_inc(stored, 1)

                blocks(sp, body)

            @block.sync
            def _(sp):
                choose(sp, v.unblocked_order, fast_sync, slow_sync)

            def fast_tensor(pe):
                pe.wait_ge(root_ready, 1)

            def slow_tensor(pe):
                def body(i, ks):
                    for k in ks:
                        b = i * 2 + k
                        pe.wait_ge(loads[k], i * 16 * LOADS + 16 * LOADS)
                        for g in range(4):
                            for r in range(COPIES):
                                last = pe.matmul(p_t[k][0:96, P * g:P * g + P], sums[k][:, r, 96 * g:96 * g + 96], v.ident[:],
                                                 start=(r == 0), stop=(r == COPIES - 1))
                        last.then_inc(pe_steps, 1)
                        pe.wait_ge(act_steps, b * 2 + 1)
                        pe.matmul(p_o[k][:, 0:S], sums_t[k][:, 0:P], v.w_out0[:], start=True, stop=True)
                        for c in range(3):
                            last = pe.matmul(p_o[k][:, S + 32 * c:S + 32 * c + 32], sums_t[k][:, P * (c + 1):P * (c + 2)], v.w_out1[:],
                                             start=True, stop=True)
                        last.then_inc(pe_steps, 1)

                blocks(pe, body)

            @block.tensor
            def _(pe):
                choose(pe, v.unblocked_order, fast_tensor, slow_tensor)

            def fast_scalar(act):
                act.wait_ge(spread_ready, 1)
                act.activation(deviation[:], variance[:], ACT.Sqrt).then_inc(root_ready, 1)

            def slow_scalar(act):
                def body(i, ks):
                    for k in ks:
                        b = i * 2 + k
                        act.wait_ge(pe_steps, b * 2 + 1)
                        act.copy(sums_t[k][:], p_t[k][0:96, :]).then_inc(act_steps, 1)
                        act.wait_ge(var_ready, b + 1)
                        act.activation(stats[k][:, 9:10], stats[k][:, 8:9], ACT.Sqrt).then_inc(act_steps, 1)

                blocks(act, body)

            @block.scalar
            def _(act):
                choose(act, v.unblocked_order, fast_scalar, slow_scalar)

            def fast_vector(dve):
                dve.tensor_scalar_add(variance[:], v.moments[:, 0:FAST_BLOCKS, 1], EPS).then_inc(spread_ready, 1)
                dve.wait_ge(root_ready, 1)
                dve.reciprocal(scale[:], deviation[:]).then_inc(passed, 1)
                dve.wait_ge(passed, 1)
                for part, (b0, b1) in enumerate(PARTS):
                    for b in range(b0, b1 + (part == len(PARTS) - 1)):
                        last = dve.tensor_scalar(v.own[:, b, :], v.own[:, b, :], v.moments[:, b, 0:1], scale[:, b:b + 1], ALU.subtract, ALU.mult)
                    last.then_inc(part_ready, 1)

            def slow_vector(dve):
                def body(i, ks):
                    for k in ks:
                        b = i * 2 + k
                        a = v.a_col[:, bass.ds(b, 1)]
                        chain = Chain(dve, dve_chain, b * STEPS)
                        dve.wait_ge(pe_steps, b * 2 + 2)
                        own = v.own[:, bass.ds(b, 1), :].rearrange("p a d -> p (a d)")
                        chain.step(dve.scalar_tensor_tensor(raw[k][:, 0:S], p_o[k][:, 0:S], a, own[:, 0:S], ALU.mult, ALU.add))
                        chain.link(dve.scalar_tensor_tensor(raw[k][:, S:D].rearrange("p (c i) -> p i c", i=3),
                                                            p_o[k][:, S:D].rearrange("p (i c) -> p i c", i=3), a,
                                                            own[:, S:D].rearrange("p (c i) -> p i c", i=3), ALU.mult, ALU.add))
                        normalise(dve, lambda: dve.wait_ge(act_steps, b * 2 + 2), chain, raw[k][:], stats[k],
                                  [(res[k][:], raw[k][:])], var_ready, passed)
                        dve.sem_inc(res_ready, 1)
                        assert chain.n == STEPS, chain.n

                blocks(dve, body)

            @block.vector
            def _(dve):
                choose(dve, v.unblocked_order, fast_vector, slow_vector)


def kernel(**inputs):
    import numpy as np
    import concourse.bacc as bacc
    from concourse.bass_utils import run_bass_kernel_spmd

    a = {k: np.ascontiguousarray(w) for k, w in inputs.items()}

    def padded(w, rows, fill=0):
        p = np.full((rows,) + w.shape[1:], fill, w.dtype)
        p[:w.shape[0]] = w
        return p

    def parts_first(w):
        return np.concatenate([w[:S], w[S:].reshape(V, 3, -1).transpose(1, 0, 2).reshape(96, -1)])

    EP = TILES * P
    EB = EP + BLOCK_EDGES
    x = padded(a["x"], NODE_ROWS)
    src, dst = padded(a["src"], EP, PAD_NODE), padded(a["dst"], EP, PAD_NODE)
    e32 = padded(a["edge_attr_32"], EP)
    e32 = np.concatenate([e32[:, :8], e32[:, 8:].reshape(EP, 8, 3).transpose(0, 2, 1).reshape(EP, 24)], axis=1)
    w1, w2, w3, w4 = (a[f"L0_gnn_W{n}"] for n in (1, 2, 3, 4))
    arrays = {
        "x": x,
        "x_t": parts_first(np.ascontiguousarray(x.T)),
        "src_rows": src.reshape(TILES, P), "dst_rows": dst.reshape(TILES, P),
        "src_cols": src.reshape(TILES, P).T, "dst_cols": dst.reshape(TILES, P).T,
        "src_flat": padded(a["src"], EB, PAD_NODE).reshape(EB, 1), "dst_flat": padded(a["dst"], EB, PAD_NODE).reshape(EB, 1),
        "e4_flat": padded(a["edge_attr_4"], EB), "e32_t": e32.T,
        "e32_cols": e32.reshape(TILES, P, NB).transpose(1, 0, 2),
        "e4_cols": padded(a["edge_attr_4"], EP).reshape(TILES, P, 4).transpose(1, 0, 2),
        "e10_t": padded(a["edge_attr_10"], EB).T,
        "a_cols": padded(a["node_vec1"], NODE_ROWS).reshape(BLOCKS, P).T,
        "w1": w1.reshape(S, 512), "w2": w2.reshape(V, 512), "w3": w3.reshape(S, 256), "w4": w4.reshape(V, 256),
        "wm_t": np.concatenate([parts_first(a["L0_gnn_Wm"]), a["L0_gnn_bm"].reshape(1, D)]).T,
        "wu_top": parts_first(a["L0_gnn_Wu"][:D]), "wu_bot": a["L0_gnn_Wu"][D:], "bu": a["L0_gnn_bu"].reshape(1, D),
        "w_node0": np.concatenate([a["L1_gnn_W_l1_0"], a["L1_gnn_W_si0"]], axis=1),
        "w_node1": np.concatenate([a["L1_gnn_W_l1_1"], a["L1_gnn_W_si1"]], axis=1),
        "w_out0": np.concatenate([a["L1_gnn_W_l2_00"], a["L1_gnn_W_l2_10"]]),
        "w_out1": np.concatenate([a["L1_gnn_W_l2_01"], a["L1_gnn_W_l2_11"]]),
        "fc1": a["L1_gnn_W_fc1"], "fc2": a["L1_gnn_W_fc2"],
    }
    arrays = {f"in_{k}": np.ascontiguousarray(w) for k, w in arrays.items()}
    nc = bacc.Bacc("TRN2", target_bir_lowering=False, num_devices=1)
    t = {k[3:]: nc.dram_tensor(k, w.shape, mybir.dt.from_np(w.dtype), kind="ExternalInput").ap() for k, w in arrays.items()}
    out = nc.dram_tensor("out_0", (NODES, D), F32, kind="ExternalOutput").ap()
    build_program(nc, t, out)
    return run_bass_kernel_spmd(nc, [arrays], core_ids=[0]).results[0]["out_0"]
```
